# Optimizing a Trainium2 kernel written in Bass

```python
import numpy as np
import jax
import jax.numpy as jnp

def _softmax(x, axis=-1):
    return jax.nn.softmax(x, axis=axis)

def _gelu(x):
    return jax.nn.gelu(x, approximate=True)

def _silu(x):
    return jax.nn.silu(x)

def _sigmoid(x):
    return jax.nn.sigmoid(x)

def _layernorm(x, axis=-1, eps=1e-05):
    m = jnp.mean(x, axis=axis, keepdims=True)
    v = jnp.var(x, axis=axis, keepdims=True)
    return (x - m) / jnp.sqrt(v + eps)

def _scatter_add(tgt, idx, src, axis=0):
    return tgt.at[idx].add(src)

def _segment_sum(src, seg, n):
    return jax.ops.segment_sum(src, seg, n)
kernel_name = 'mk_lm_tower_d1_tok_ids512_r4_6ac916'

def setup_inputs(seed: int=0):
    np.random.seed(seed)
    _w = jnp.asarray

    def _rec_inputs():
        import jax
        import jax.numpy as jnp
        _rk = jax.random.key(seed)
        x = jax.random.randint(jax.random.fold_in(_rk, 1), (8, 1024), 0, 24991, jnp.int32)
        return x
    x = _rec_inputs()

    def _L0_tok_setup():
        import jax, jax.numpy as jnp
        import numpy as np
        VOCAB = 25000
        HIDDEN = 128
        NUM_CLUSTERS = 64
        B, S = (8, 512)
        key = jax.random.key(seed)
        k1, k2, k3, k4, k5 = jax.random.split(key, 5)
        return {'location_ids': jax.random.randint(k1, (B, S), 0, VOCAB), 'fine_embed_w': jax.random.normal(k2, (VOCAB, HIDDEN // 2), dtype=jnp.float32), 'coarse_embed_w': jax.random.normal(k3, (NUM_CLUSTERS, HIDDEN // 2), dtype=jnp.float32), 'loc_to_cluster_w': jax.random.normal(k4, (NUM_CLUSTERS, VOCAB), dtype=jnp.float32), 'loc_to_cluster_b': jax.random.normal(k5, (NUM_CLUSTERS,), dtype=jnp.float32)}
    _L0_tok_all = _L0_tok_setup()
    _L0_tok_in = {k: v for k, v in _L0_tok_all.items() if k in ('fine_embed_w', 'coarse_embed_w', 'loc_to_cluster_w', 'loc_to_cluster_b')}
    del _L0_tok_all

    def _L0_attn_setup():
        import jax, jax.numpy as jnp
        import numpy as np
        H = 8
        EPS = 1e-05

        def _ln(x, g=None, b=None):
            m = jnp.mean(x, axis=-1, keepdims=True)
            v = jnp.mean((x - m) ** 2, axis=-1, keepdims=True)
            y = (x - m) * jax.lax.rsqrt(v + EPS)
            if g is not None:
                y = y * g + b
            return y
        key = jax.random.key(seed)
        B, N, C = (1, 1024, 128)
        inner = 128
        ks = jax.random.split(key, 8)
        sc = 1.0 / np.sqrt(C).astype(np.float32)
        return {'x': jax.random.normal(ks[0], (B, N, C), jnp.float32), 'w_q': jax.random.normal(ks[1], (C, inner), jnp.float32) * sc, 'b_q': jnp.zeros((inner,), jnp.float32), 'w_k': jax.random.normal(ks[2], (C, inner), jnp.float32) * sc, 'b_k': jnp.zeros((inner,), jnp.float32), 'w_v': jax.random.normal(ks[3], (C, inner), jnp.float32) * sc, 'b_v': jnp.zeros((inner,), jnp.float32), 'g_q': jnp.ones((inner,), jnp.float32), 'be_q': jnp.zeros((inner,), jnp.float32), 'g_k': jnp.ones((inner,), jnp.float32), 'be_k': jnp.zeros((inner,), jnp.float32), 'w_o': jax.random.normal(ks[4], (inner, C), jnp.float32) * sc, 'b_o': jnp.zeros((C,), jnp.float32)}
    _L0_attn_all = _L0_attn_setup()
    _L0_attn_in = {k: v for k, v in _L0_attn_all.items() if k in ('w_q', 'b_q', 'w_k', 'b_k', 'w_v', 'b_v', 'g_q', 'be_q', 'g_k', 'be_k', 'w_o', 'b_o')}
    del _L0_attn_all

    def _L0_ffn_setup():
        import jax, jax.numpy as jnp
        import numpy as np
        E = 64
        K = 2
        CAP = 128
        H = 128
        FFN = 512
        B, S = (8, 1024)
        key = jax.random.key(seed)
        ks = jax.random.split(key, 6)
        hidden_states = jax.random.normal(ks[0], (B, S, H), dtype=jnp.float32)
        router_w = jax.random.normal(ks[1], (E, H), dtype=jnp.float32) * (0.01 / np.sqrt(H))
        w1 = jax.random.normal(ks[2], (FFN, H), dtype=jnp.float32) * (1.0 / np.sqrt(H))
        b1 = jnp.zeros((FFN,), dtype=jnp.float32)
        w2 = jax.random.normal(ks[3], (H, FFN), dtype=jnp.float32) * (1.0 / np.sqrt(FFN))
        b2 = jnp.zeros((H,), dtype=jnp.float32)
        return {'hidden_states': hidden_states, 'router_w': router_w, 'w1': w1, 'b1': b1, 'w2': w2, 'b2': b2}
    _L0_ffn_all = _L0_ffn_setup()
    _L0_ffn_in = {k: v for k, v in _L0_ffn_all.items() if k in ('router_w', 'w1', 'b1', 'w2', 'b2')}
    del _L0_ffn_all
    return {'x': x, 'L0_tok_fine_embed_w': _L0_tok_in['fine_embed_w'], 'L0_tok_coarse_embed_w': _L0_tok_in['coarse_embed_w'], 'L0_tok_loc_to_cluster_w': _L0_tok_in['loc_to_cluster_w'], 'L0_tok_loc_to_cluster_b': _L0_tok_in['loc_to_cluster_b'], 'L0_attn_w_q': _L0_attn_in['w_q'], 'L0_attn_b_q': _L0_attn_in['b_q'], 'L0_attn_w_k': _L0_attn_in['w_k'], 'L0_attn_b_k': _L0_attn_in['b_k'], 'L0_attn_w_v': _L0_attn_in['w_v'], 'L0_attn_b_v': _L0_attn_in['b_v'], 'L0_attn_g_q': _L0_attn_in['g_q'], 'L0_attn_be_q': _L0_attn_in['be_q'], 'L0_attn_g_k': _L0_attn_in['g_k'], 'L0_attn_be_k': _L0_attn_in['be_k'], 'L0_attn_w_o': _L0_attn_in['w_o'], 'L0_attn_b_o': _L0_attn_in['b_o'], 'L0_ffn_router_w': _L0_ffn_in['router_w'], 'L0_ffn_w1': _L0_ffn_in['w1'], 'L0_ffn_b1': _L0_ffn_in['b1'], 'L0_ffn_w2': _L0_ffn_in['w2'], 'L0_ffn_b2': _L0_ffn_in['b2']}

def reference(x, L0_tok_fine_embed_w, L0_tok_coarse_embed_w, L0_tok_loc_to_cluster_w, L0_tok_loc_to_cluster_b, L0_attn_w_q, L0_attn_b_q, L0_attn_w_k, L0_attn_b_k, L0_attn_w_v, L0_attn_b_v, L0_attn_g_q, L0_attn_be_q, L0_attn_g_k, L0_attn_be_k, L0_attn_w_o, L0_attn_b_o, L0_ffn_router_w, L0_ffn_w1, L0_ffn_b1, L0_ffn_w2, L0_ffn_b2):
    import jax
    import jax.numpy as jnp

    def _L0_tok_ref(location_ids, fine_embed_w, coarse_embed_w, loc_to_cluster_w, loc_to_cluster_b):
        import jax, jax.numpy as jnp
        import numpy as np
        VOCAB = 25000
        HIDDEN = 128
        NUM_CLUSTERS = 64
        B, S = (8, 512)
        fine_emb = fine_embed_w[location_ids]
        cluster_logits = loc_to_cluster_w.T[location_ids] + loc_to_cluster_b
        cluster_dist = jax.nn.softmax(cluster_logits, axis=-1)
        coarse_emb = jnp.einsum('bsc,ch->bsh', cluster_dist, coarse_embed_w)
        return jnp.concatenate([fine_emb, coarse_emb], axis=-1)

    def _L0_attn_ref(x, w_q, b_q, w_k, b_k, w_v, b_v, g_q, be_q, g_k, be_k, w_o, b_o):
        import jax, jax.numpy as jnp
        import numpy as np
        H = 8
        EPS = 1e-05

        def _ln(x, g=None, b=None):
            m = jnp.mean(x, axis=-1, keepdims=True)
            v = jnp.mean((x - m) ** 2, axis=-1, keepdims=True)
            y = (x - m) * jax.lax.rsqrt(v + EPS)
            if g is not None:
                y = y * g + b
            return y
        B, N, C = x.shape
        silu = jax.nn.silu
        xn = _ln(x)
        q = silu(xn) @ w_q + b_q
        k = silu(xn) @ w_k + b_k
        v = silu(xn) @ w_v + b_v
        q = _ln(q, g_q, be_q)
        k = _ln(k, g_k, be_k)
        inner = q.shape[-1]
        q = q * inner ** (-0.5)
        d = inner // H
        qh = q.reshape(B, N, H, d).transpose(0, 2, 1, 3)
        kh = k.reshape(B, N, H, d).transpose(0, 2, 1, 3)
        vh = v.reshape(B, N, H, d).transpose(0, 2, 1, 3)
        w = jax.nn.softmax(jnp.einsum('bhid,bhjd->bhij', qh, kh), axis=-1)
        o = jnp.einsum('bhij,bhjd->bhid', w, vh)
        o = o.transpose(0, 2, 1, 3).reshape(B, N, inner)
        return silu(o) @ w_o + b_o

    def _L0_ffn_ref(hidden_states, router_w, w1, b1, w2, b2):
        import jax, jax.numpy as jnp
        import numpy as np
        E = 64
        K = 2
        CAP = 128
        H = 128
        FFN = 512
        B, S = (8, 1024)
        orig_shape = hidden_states.shape
        x = hidden_states.reshape(-1, orig_shape[-1])
        T = x.shape[0]
        N = T * K
        logits = jnp.einsum('th,eh->te', x, router_w)
        probs_full = jax.nn.softmax(logits, axis=-1)
        probs, idx = jax.lax.top_k(probs_full, K)
        flat_e = idx.reshape(-1)
        flat_p = probs.reshape(-1)
        order = jnp.argsort(flat_e, stable=True)
        sorted_e = flat_e[order]
        counts = jnp.zeros((E,), jnp.int32).at[flat_e].add(1)
        offsets = jnp.concatenate([jnp.zeros((1,), jnp.int32), jnp.cumsum(counts)[:-1]])
        pos = jnp.arange(N, dtype=jnp.int32) - offsets[sorted_e]
        keep = pos < CAP
        slot = sorted_e * CAP + jnp.minimum(pos, CAP - 1)
        dest = jnp.where(keep, slot, E * CAP)
        tok = order // K
        buf = jnp.zeros((E * CAP + 1, x.shape[-1]), x.dtype).at[dest].set(x[tok])
        buf = buf[:-1]
        h = jax.nn.gelu(jnp.einsum('nh,fh->nf', buf, w1) + b1, approximate=False)
        y = jnp.einsum('nf,hf->nh', h, w2) + b2
        gate = jnp.where(keep, flat_p[order], 0.0)
        contrib = y[jnp.minimum(slot, E * CAP - 1)] * gate[:, None]
        out = jnp.zeros_like(x).at[tok].add(contrib)
        return out.reshape(orig_shape)
    h = _L0_tok_ref(x, L0_tok_fine_embed_w, L0_tok_coarse_embed_w, L0_tok_loc_to_cluster_w, L0_tok_loc_to_cluster_b)
    h = h + _L0_attn_ref(_layernorm(h, axis=-1), L0_attn_w_q, L0_attn_b_q, L0_attn_w_k, L0_attn_b_k, L0_attn_w_v, L0_attn_b_v, L0_attn_g_q, L0_attn_be_q, L0_attn_g_k, L0_attn_be_k, L0_attn_w_o, L0_attn_b_o)
    h = h + _L0_ffn_ref(_layernorm(h, axis=-1), L0_ffn_router_w, L0_ffn_w1, L0_ffn_b1, L0_ffn_w2, L0_ffn_b2)
    return h

_drawn_inputs = setup_inputs


def setup_inputs(seed=0):
    import zlib

    import numpy as np

    out = dict(_drawn_inputs(seed))
    spreads = {'L0_attn_b_q': (0.0, 2.0),
     'L0_attn_b_k': (0.0, 2.0),
     'L0_attn_b_v': (0.0, 0.1),
     'L0_attn_g_q': (1.0, 0.6),
     'L0_attn_be_q': (0.0, 0.8),
     'L0_attn_g_k': (1.0, 0.6),
     'L0_attn_be_k': (0.0, 2.0),
     'L0_attn_b_o': (0.0, 0.1),
     'L0_ffn_b1': (0.0, 0.8),
     'L0_ffn_b2': (0.0, 2.0)}
    factors = {'L0_attn_w_q': 3.319,
     'L0_attn_w_k': 3.353,
     'L0_ffn_router_w': 7.323,
     'L0_ffn_w1': 3.707,
     'L0_ffn_w2': 3.312}
    for name, (base, spread) in spreads.items():
        noise = np.random.default_rng([zlib.crc32(name.encode()), seed]).standard_normal(out[name].shape)
        drawn = base * np.exp(spread * noise) if base else spread * noise
        out[name] = jnp.asarray(drawn.astype(out[name].dtype))
    for name, factor in factors.items():
        out[name] = (out[name] * factor).astype(out[name].dtype)
    return out
```

```python
import concourse.bass as bass
from concourse import mybir
from contextlib import ExitStack

F32 = mybir.dt.float32
BF16 = mybir.dt.bfloat16
I32 = mybir.dt.int32
U32 = mybir.dt.uint32
ALU = mybir.AluOpType
ACT = mybir.ActivationFunctionType
AX = mybir.AxisListType

P = 128
BATCH, SEQ, DIM = 8, 1024, 128
HEADS = 8
HD = DIM // HEADS
HALF = DIM // 2
CLUSTERS = 64
EXPERTS = 64
CAP = 128
FFN = 512
FK = FFN // P
EPS = 1e-5
QSCALE = float(DIM) ** -0.5

WAYS = 4
SLOTS = 2
TILES = 4
CHUNK = TILES * P
ITERS = BATCH * SEQ // (CHUNK * WAYS)
PER_BATCH = SEQ // CHUNK

BANK = 512
HALVES = SEQ // BANK
TOKT = SEQ // P
PARTS = 3
Q_TERMS = (0, 0, 1, 1, 0, 2)
K_TERMS = (0, 1, 0, 1, 2, 0)
DATA_ROWS = HD * len(Q_TERMS)
ROWS = DATA_ROWS + PARTS
VW = HD + 1
GH = 4
GROUPS = HEADS // GH
HP = 32


def build(nc, x_idx, table, cluster_b, coarse_w, w_q, b_q, w_k, b_k, w_v, b_v, g_q, be_q, g_k, be_k,
          w_o, b_o, router_t, w1_t, b1_c, w2_t, b2, out):
    qk_parts = nc.dram_tensor("qk_parts", (BATCH, 2, PARTS, P, SEQ), BF16).ap()
    v_rows = nc.dram_tensor("v_rows", (BATCH, P, TOKT, HEADS * VW), F32).ap()
    h_rows = nc.dram_tensor("h_rows", (ITERS, WAYS, P, TILES * DIM), F32).ap()
    o_cols = nc.dram_tensor("o_cols", (BATCH, GROUPS, P, SEQ), F32).ap()

    ctx = ExitStack()
    with ctx:
        def keep(name, shape, dt=F32):
            return ctx.enter_context(nc.sbuf_tensor(name, shape, dt))

        c = {}
        c["ident"] = keep("ident", [P, P])
        c["later"] = keep("later", [P, P], BF16)
        c["ones"] = keep("ones", [P, P], BF16)
        c["expert_ids"] = keep("expert_ids", [P, EXPERTS])
        c["neg_half"] = keep("neg_half", [P, 2 * TILES])
        c["w_qkv"] = keep("w_qkv", [P, 3 * DIM])
        c["b_qkv"] = keep("b_qkv", [P, 3 * DIM])
        c["cluster_b"] = keep("cluster_b_sb", [P, CLUSTERS])
        c["coarse_w"] = keep("coarse_w_sb", [CLUSTERS, HALF])
        c["gain"] = keep("gain", [P, 2])
        c["shift"] = keep("shift", [P, 2])
        c["w_o"] = keep("w_o_sb", [P, DIM])
        c["b_o"] = keep("b_o_sb", [P, DIM])
        c["router"] = keep("router_sb", [P, EXPERTS])
        c["w1"] = keep("w1_sb", [P, FFN])
        c["b1"] = keep("b1_sb", [P, FK])
        c["w2"] = keep("w2_sb", [P, FK, DIM])
        c["b2"] = keep("b2_sb", [P, DIM])
        c["carry"] = keep("carry", [P, EXPERTS])
        c["idx_all"] = keep("idx_all", [P, (ITERS + 1) * WAYS * TILES], I32)

        setup(nc, ctx, c, x_idx, cluster_b, coarse_w, w_q, b_q, w_k, b_k, w_v, b_v, g_q, be_q, g_k, be_k,
              w_o, b_o, router_t, w1_t, b1_c, w2_t, b2)
        embed(nc, c, table, qk_parts, v_rows, h_rows)
        attend(nc, qk_parts, v_rows, o_cols)
        finish(nc, c, h_rows, o_cols, out)


def wait_apart(engine, sem, n):
    engine.to_reg(n)
    engine.wait_ge(sem, 1)
    engine.wait_ge(sem, n)


def preset(engine, sem, n):
    engine.sem_inc(sem, n)


def setup(nc, ctx, c, x_idx, cluster_b, coarse_w, w_q, b_q, w_k, b_k, w_v, b_v, g_q, be_q, g_k, be_k,
          w_o, b_o, router_t, w1_t, b1_c, w2_t, b2):
    loaded = ctx.enter_context(nc.semaphore("weights_loaded"))
    made = ctx.enter_context(nc.semaphore("constants_made"))
    scaled = ctx.enter_context(nc.semaphore("q_gain_scaled"))
    idx_int = ctx.enter_context(nc.sbuf_tensor("expert_ids_int", [P, EXPERTS], I32))
    idx_pad = ITERS * WAYS * TILES

    def rows(v):
        return v.rearrange("(a n) -> a n", a=1).to_broadcast([P, v.shape[0]])

    def column(v):
        return v.rearrange("(p a) -> p a", a=1)

    loads = [(c["w_qkv"][:, 0:DIM], w_q), (c["w_qkv"][:, DIM:2 * DIM], w_k), (c["w_qkv"][:, 2 * DIM:], w_v),
             (c["b_qkv"][:, 0:DIM], rows(b_q)), (c["b_qkv"][:, DIM:2 * DIM], rows(b_k)),
             (c["b_qkv"][:, 2 * DIM:], rows(b_v)),
             (c["cluster_b"][:, :], rows(cluster_b)), (c["coarse_w"][:, :], coarse_w),
             (c["gain"][:, 0:1], column(g_q)), (c["gain"][:, 1:2], column(g_k)),
             (c["shift"][:, 0:1], column(be_q)), (c["shift"][:, 1:2], column(be_k)),
             (c["w_o"][:, :], w_o), (c["b_o"][:, :], rows(b_o)), (c["router"][:, :], router_t),
             (c["w1"][:, :], w1_t), (c["b1"][:, :], b1_c),
             (c["w2"][:, :, :], w2_t.rearrange("(k p) n -> p k n", p=P)), (c["b2"][:, :], rows(b2)),
             (c["idx_all"][:, 0:idx_pad].rearrange("p (i t) -> p i t", t=TILES), x_idx.rearrange("i p t -> p i t"))]

    with nc.Block() as block:
        @block.sync
        def _(sp):
            for dst, src in loads:
                sp.dma_start(dst, src).then_inc(loaded, 16)
            sp.wait_ge(loaded, 16 * len(loads))

        @block.gpsimd
        def _(pool):
            nc.gpsimd.memset(c["ident"][:, :], 0.0).then_inc(made, 1)
            nc.gpsimd.memset(c["later"][:, :], 0.0).then_inc(made, 1)
            nc.gpsimd.memset(c["ones"][:, :], 1.0).then_inc(made, 1)
            nc.gpsimd.memset(c["neg_half"][:, :], -0.5).then_inc(made, 1)
            nc.gpsimd.memset(c["carry"][:, :], 0.0).then_inc(made, 1)
            nc.gpsimd.memset(c["idx_all"][:, idx_pad:], 0).then_inc(made, 1)
            nc.gpsimd.iota(idx_int[:, :], pattern=[[1, EXPERTS]], base=0, channel_multiplier=0).then_inc(made, 1)
            pool.wait_ge(made, 7)
            nc.gpsimd.affine_select(out=c["ident"][:, :], in_=c["ident"][:, :], compare_op=ALU.not_equal, fill=1.0,
                                    base=0, pattern=[[-1, P]], channel_multiplier=1).then_inc(made, 1)
            nc.gpsimd.affine_select(out=c["later"][:, :], in_=c["later"][:, :], compare_op=ALU.is_ge, fill=1.0,
                                    base=0, pattern=[[-1, P]], channel_multiplier=1).then_inc(made, 1)
            nc.gpsimd.tensor_copy(c["expert_ids"][:, :], idx_int[:, :]).then_inc(made, 1)

        @block.vector
        def _(dve):
            dve.wait_ge(loaded, 16 * len(loads))
            nc.vector.tensor_scalar(c["gain"][:, 0:1], c["gain"][:, 0:1], QSCALE, None, ALU.mult).then_inc(scaled, 1)
            nc.vector.tensor_scalar(c["shift"][:, 0:1], c["shift"][:, 0:1], QSCALE, None, ALU.mult).then_inc(scaled, 1)


def embed(nc, c, table, qk_parts, v_rows, h_rows):
    ctx = ExitStack()
    with ctx:
        def ways(name, shape, dt=F32):
            return [ctx.enter_context(nc.sbuf_tensor(f"{name}{w}", shape, dt)) for w in range(WAYS)]

        def sem(name):
            return ctx.enter_context(nc.semaphore("a_" + name))

        def way_sems(name):
            return [sem(f"{name}{w}") for w in range(WAYS)]

        idx = ways("idx", [P, TILES], I32)
        emb = ways("emb", [P, TILES, DIM])
        logit = ways("logit", [P, TILES, CLUSTERS])
        expo = ways("expo", [P, TILES, CLUSTERS])
        neg_max = ways("a_neg_max", [P, TILES])
        inv_sum = ways("a_inv_sum", [P, TILES])
        expo_t = ways("expo_t", [CLUSTERS, CHUNK])
        h = ways("h", [P, TILES, DIM])
        stat = ways("a_stat", [P, TILES, 6])
        mv = ways("a_mv", [P, TILES, 2])
        rs = ways("a_rs", [P, TILES])
        xn = ways("xn", [P, TILES, DIM])
        sx = ways("sx", [P, TILES, DIM])
        sx_t = ways("sx_t", [P, CHUNK])
        qk = ways("qk", [P, TILES, 2, DIM])
        vrow = ways("vrow", [P, TILES, HEADS, VW])
        stat2 = ways("a_stat2", [P, TILES * 2, 6])
        mv2 = ways("a_mv2", [P, TILES * 2, 2])
        rs3 = ways("a_rs3", [P, TILES * 2])
        full = ways("qk_full", [P, 2, CHUNK])
        rest = ways("qk_rest", [P, 2, CHUNK])
        part = [ways(f"qk_part{n}_", [P, 2, CHUNK], BF16) for n in range(PARTS)]
        psA = [ctx.enter_context(nc.psum_tensor(f"a_psA{i}", [P, BANK], F32)) for i in range(SLOTS)] * (WAYS // SLOTS)
        psV = [ctx.enter_context(nc.psum_tensor(f"a_psV{i}", [P, BANK], F32)) for i in range(SLOTS)] * (WAYS // SLOTS)
        psQK = [ctx.enter_context(nc.psum_tensor(f"a_psQK{i}", [P, 2, BANK], F32)) for i in range(SLOTS)] * (WAYS // SLOTS)

        ones_set = sem("ones_set")
        idx_copied = sem("idx_copied")
        gathered = way_sems("gathered")
        logit_biased = sem("logit_biased")
        max_found = sem("max_found")
        logit_shifted = sem("logit_shifted")
        exp_done = sem("exp_done")
        sum_done = sem("sum_done")
        inv_done = sem("inv_done")
        exp_t_done = sem("exp_t_done")
        exp_t_copied = sem("exp_t_copied")
        coarse_done = sem("coarse_done")
        coarse_scaled = sem("coarse_scaled")
        fine_copied = sem("fine_copied")
        h_stored = way_sems("h_stored")
        stats_done = sem("stats_done")
        aggr_done = sem("aggr_done")
        both_var_done = sem("both_var_done")
        rstd_done = sem("rstd_done")
        xn_done = sem("xn_done")
        tanh_done = sem("tanh_done")
        silu_done = sem("silu_done")
        silu_t_done = sem("silu_t_done")
        silu_t_copied = sem("silu_t_copied")
        qk_projected = sem("qk_projected")
        v_projected = sem("v_projected")
        qk_biased = sem("qk_biased")
        v_biased = sem("v_biased")
        v_stored = way_sems("v_stored")
        stats2_done = sem("stats2_done")
        aggr2_done = sem("aggr2_done")
        means2_done = sem("means2_done")
        rstd2_done = sem("rstd2_done")
        qk_normed = sem("qk_normed")
        qk_t_done = sem("qk_t_done")
        qk_scaled = sem("qk_scaled")
        part0_done = sem("part0_done")
        rest1_done = sem("rest1_done")
        part1_done = sem("part1_done")
        part2_done = sem("part2_done")
        parts_stored = way_sems("parts_stored")

        with nc.Block() as block:
            @block.sync
            def _(sp):
                for w in range(WAYS):
                    for s in (h_stored, v_stored, parts_stored):
                        preset(sp, s[w], 16 * (PARTS if s is parts_stored else 1))
                preset(sp, qk_scaled, SLOTS)

            @block.vector
            def _(dve):
                for w in range(WAYS):
                    last = nc.vector.memset(vrow[w][:, :, :, HD:VW], 1.0)
                last.then_inc(ones_set, 1)

        with nc.Block() as block:
            @block.gpsimd
            def _(pool):
                def gather(it, w):
                    cols = bass.ds((it * WAYS + w) * TILES, TILES)
                    nc.gpsimd.tensor_copy(idx[w][:, :], c["idx_all"][:, cols]).then_inc(idx_copied, 1)
                    wait_apart(pool, idx_copied, it * WAYS + w + 1)
                    for t in range(TILES):
                        nc.gpsimd.indirect_dma_start(
                            out=emb[w][:, t, :], out_offset=None, in_=table,
                            in_offset=bass.IndirectOffsetOnAxis(ap=idx[w][:, t:t + 1], axis=0)).then_inc(gathered[w], 16)

                for w in range(WAYS):
                    gather(0, w)
                with pool.Fori(0, ITERS) as it:
                    for w in range(WAYS):
                        pool.wait_ge(both_var_done, it * WAYS + w + 1)
                        nc.gpsimd.tensor_tensor(rs[w][:, :], rs[w][:, :], c["neg_half"][:, 0:TILES],
                                                ALU.pow).then_inc(rstd_done, 1)
                    for w in range(WAYS):
                        pool.wait_ge(fine_copied, it * WAYS + w + 1)
                        wait_apart(pool, logit_biased, it * WAYS + w + 1)
                        gather(it + 1, w)
                    for w in range(WAYS):
                        n = it * WAYS + w + 1
                        pool.wait_ge(aggr2_done, n)
                        nc.gpsimd.tensor_tensor(rs3[w][:, :], rs3[w][:, :], c["neg_half"][:, :], ALU.pow).then_inc(rstd2_done, 1)
                    for w in range(WAYS):
                        n = it * WAYS + w + 1
                        pool.wait_ge(qk_scaled, n + SLOTS)
                        pool.wait_ge(part0_done, n)
                        nc.gpsimd.tensor_tensor(rest[w][:, :, :], full[w][:, :, :], part[0][w][:, :, :],
                                                ALU.subtract).then_inc(rest1_done, 1)
                for w in range(WAYS):
                    pool.wait_ge(gathered[w], (ITERS + 1) * 16 * TILES)

            @block.vector
            def _(dve):
                with dve.Fori(0, ITERS) as it:
                    for w in range(WAYS):
                        n = it * WAYS + w + 1
                        dve.wait_ge(gathered[w], (it + 1) * 16 * TILES)
                        nc.vector.tensor_tensor(logit[w][:, :, :], emb[w][:, :, HALF:DIM],
                                                c["cluster_b"][:, :].unsqueeze(1).to_broadcast([P, TILES, CLUSTERS]),
                                                ALU.add).then_inc(logit_biased, 1)
                    for w in range(WAYS):
                        n = it * WAYS + w + 1
                        dve.wait_ge(logit_biased, n)
                        nc.vector.tensor_reduce(neg_max[w][:, :], logit[w][:, :, :], AX.X, ALU.max,
                                                negate=True).then_inc(max_found, 1)
                    for w in range(WAYS):
                        n = it * WAYS + w + 1
                        dve.wait_ge(max_found, n)
                        nc.vector.tensor_tensor(logit[w][:, :, :], logit[w][:, :, :],
                                                neg_max[w][:, :].unsqueeze(2).to_broadcast([P, TILES, CLUSTERS]),
                                                ALU.add).then_inc(logit_shifted, 1)
                    for w in range(WAYS):
                        n = it * WAYS + w + 1
                        dve.wait_ge(exp_done, n)
                        nc.vector.tensor_reduce(inv_sum[w][:, :], expo[w][:, :, :], AX.X, ALU.add).then_inc(sum_done, 1)
                    for w in range(WAYS):
                        n = it * WAYS + w + 1
                        dve.wait_ge(sum_done, n)
                        nc.vector.reciprocal(inv_sum[w][:, :], inv_sum[w][:, :]).then_inc(inv_done, 1)
                    for w in range(WAYS):
                        n = it * WAYS + w + 1
                        dve.wait_ge(inv_done, n)
                        dve.wait_ge(coarse_done, n)
                        dve.wait_ge(h_stored[w], (it + 1) * 16)
                        nc.vector.tensor_tensor(h[w][:, :, HALF:DIM],
                                                psV[w][:, 0:TILES * HALF].rearrange("p (t n) -> p t n", t=TILES),
                                                inv_sum[w][:, :].unsqueeze(2).to_broadcast([P, TILES, HALF]),
                                                ALU.mult).then_inc(coarse_scaled, 1)
                    for w in range(WAYS):
                        n = it * WAYS + w + 1
                        dve.wait_ge(coarse_scaled, n)
                        dve.wait_ge(fine_copied, n)
                        for t in range(TILES):
                            last = nc.vector.bn_stats(stat[w][:, t, :], h[w][:, t, :])
                        last.then_inc(stats_done, 1)
                    for w in range(WAYS):
                        n = it * WAYS + w + 1
                        wait_apart(dve, stats_done, n)
                        for t in range(TILES):
                            last = nc.vector.bn_aggr(mv[w][:, t, :], stat[w][:, t, :])
                        last.then_inc(aggr_done, 1)
                        dve.wait_ge(aggr_done, n)
                        nc.vector.tensor_scalar(rs[w][:, :], mv[w][:, :, 1], 1.0 + EPS, EPS * EPS, ALU.mult,
                                                ALU.add).then_inc(both_var_done, 1)
                    for w in range(WAYS):
                        n = it * WAYS + w + 1
                        dve.wait_ge(rstd_done, n)
                        for t in range(TILES):
                            last = nc.vector.tensor_scalar(xn[w][:, t, :], h[w][:, t, :], mv[w][:, t, 0:1],
                                                           rs[w][:, t:t + 1], ALU.subtract, ALU.mult)
                        last.then_inc(xn_done, 1)
                    for w in range(WAYS):
                        n = it * WAYS + w + 1
                        dve.wait_ge(tanh_done, n)
                        nc.vector.scalar_tensor_tensor(out=sx[w][:, :, :], in0=sx[w][:, :, :], scalar=1.0,
                                                       in1=xn[w][:, :, :], op0=ALU.add, op1=ALU.mult).then_inc(silu_done, 1)
                    for w in range(WAYS):
                        n = it * WAYS + w + 1
                        dve.wait_ge(qk_projected, n)
                        nc.vector.tensor_tensor(qk[w][:, :, :, :].rearrange("p t a n -> p t (a n)"),
                                                psQK[w][:, :, :].rearrange("p b (t n) -> p (b t) n", t=2),
                                                c["b_qkv"][:, 0:2 * DIM].unsqueeze(1).to_broadcast([P, TILES, 2 * DIM]),
                                                ALU.add).then_inc(qk_biased, 1)
                        dve.wait_ge(v_projected, n)
                        dve.wait_ge(v_stored[w], (it + 1) * 16)
                        nc.vector.tensor_tensor(vrow[w][:, :, :, 0:HD],
                                                psV[w][:, :].rearrange("p (t h d) -> p t h d", t=TILES, h=HEADS),
                                                c["b_qkv"][:, 2 * DIM:].rearrange("p (a h d) -> p a h d", a=1, h=HEADS)
                                                .to_broadcast([P, TILES, HEADS, HD]),
                                                ALU.add).then_inc(v_biased, 1)
                    for w in range(WAYS):
                        n = it * WAYS + w + 1
                        dve.wait_ge(qk_biased, n)
                        for t in range(TILES):
                            for a in range(2):
                                last = nc.vector.bn_stats(stat2[w][:, 2 * t + a, :], qk[w][:, t, a, :])
                        last.then_inc(stats2_done, 1)
                    for w in range(WAYS):
                        n = it * WAYS + w + 1
                        wait_apart(dve, stats2_done, n)
                        for j in range(2 * TILES):
                            last = nc.vector.bn_aggr(mv2[w][:, j, :], stat2[w][:, j, :])
                        last.then_inc(means2_done, 1)
                        dve.wait_ge(means2_done, n)
                        nc.vector.tensor_scalar(rs3[w][:, :], mv2[w][:, :, 1], EPS, None, ALU.add).then_inc(aggr2_done, 1)
                    for w in range(WAYS):
                        n = it * WAYS + w + 1
                        dve.wait_ge(rstd2_done, n)
                        for t in range(TILES):
                            for a in range(2):
                                j = 2 * t + a
                                last = nc.vector.tensor_scalar(qk[w][:, t, a, :], qk[w][:, t, a, :], mv2[w][:, j, 0:1],
                                                               rs3[w][:, j:j + 1], ALU.subtract, ALU.mult)
                        last.then_inc(qk_normed, 1)
                    for w in range(WAYS):
                        n = it * WAYS + w + 1
                        dve.wait_ge(rest1_done, n)
                        nc.vector.tensor_copy(part[1][w][:, :, :], rest[w][:, :, :]).then_inc(part1_done, 1)
                    for w in range(WAYS):
                        n = it * WAYS + w + 1
                        dve.wait_ge(part1_done, n)
                        nc.vector.tensor_tensor(part[2][w][:, :, :], rest[w][:, :, :], part[1][w][:, :, :],
                                                ALU.subtract).then_inc(part2_done, 1)

            @block.scalar
            def _(act):
                with act.Fori(0, ITERS) as it:
                    for w in range(WAYS):
                        act.wait_ge(gathered[w], (it + 1) * 16 * TILES)
                        act.wait_ge(h_stored[w], (it + 1) * 16)
                        nc.scalar.activation(h[w][:, :, 0:HALF], emb[w][:, :, 0:HALF], ACT.Copy).then_inc(fine_copied, 1)
                    for w in range(WAYS):
                        act.wait_ge(logit_shifted, it * WAYS + w + 1)
                        nc.scalar.activation(expo[w][:, :, :], logit[w][:, :, :], ACT.Exp).then_inc(exp_done, 1)
                    for w in range(WAYS):
                        act.wait_ge(exp_t_done, it * WAYS + w + 1)
                        nc.scalar.activation(expo_t[w][:, :], psA[w][0:CLUSTERS, :], ACT.Copy).then_inc(exp_t_copied, 1)
                    for w in range(WAYS):
                        act.wait_ge(xn_done, it * WAYS + w + 1)
                        nc.scalar.activation(sx[w][:, :, :], xn[w][:, :, :], ACT.Tanh, scale=0.5).then_inc(tanh_done, 1)
                    for w in range(WAYS):
                        act.wait_ge(silu_t_done, it * WAYS + w + 1)
                        nc.scalar.activation(sx_t[w][:, :], psA[w][:, :], ACT.Copy, scale=0.5).then_inc(silu_t_copied, 1)
                    for w in range(WAYS):
                        act.wait_ge(qk_t_done, it * WAYS + w + 1)
                        for a in range(2):
                            last = nc.scalar.activation(full[w][:, a, :], psQK[w][:, a, :], ACT.Identity,
                                                        bias=c["shift"][:, a:a + 1], scale=c["gain"][:, a:a + 1])
                        last.then_inc(qk_scaled, 1)
                        act.wait_ge(parts_stored[w], (it + 1) * 16 * PARTS)
                        act.wait_ge(qk_scaled, it * WAYS + w + 1 + SLOTS)
                        nc.scalar.activation(part[0][w][:, :, :], full[w][:, :, :], ACT.Copy).then_inc(part0_done, 1)

            @block.tensor
            def _(pe):
                with pe.Fori(0, ITERS) as it:
                    for w in range(WAYS):
                        if w >= SLOTS:
                            pe.wait_ge(exp_t_copied, it * WAYS + w + 1 - SLOTS)
                        wait_apart(pe, exp_done, it * WAYS + w + 1)
                        for t in range(TILES):
                            last = nc.tensor.transpose(psA[w][0:CLUSTERS, t * P:(t + 1) * P], expo[w][:, t, :], c["ident"][:, :])
                        last.then_inc(exp_t_done, 1)
                    for w in range(WAYS):
                        pe.wait_ge(exp_t_copied, it * WAYS + w + 1)
                        if w >= SLOTS:
                            pe.wait_ge(coarse_scaled, it * WAYS + w + 1 - SLOTS)
                        for t in range(TILES):
                            last = nc.tensor.matmul(psV[w][:, t * HALF:(t + 1) * HALF], expo_t[w][:, t * P:(t + 1) * P],
                                                    c["coarse_w"][:, :], start=True, stop=True)
                        last.then_inc(coarse_done, 1)
                    for w in range(WAYS):
                        pe.wait_ge(silu_done, it * WAYS + w + 1)
                        if w >= SLOTS:
                            pe.wait_ge(silu_t_copied, it * WAYS + w + 1 - SLOTS)
                        for t in range(TILES):
                            last = nc.tensor.transpose(psA[w][:, t * P:(t + 1) * P], sx[w][:, t, :], c["ident"][:, :])
                        last.then_inc(silu_t_done, 1)
                    for w in range(WAYS):
                        pe.wait_ge(silu_t_copied, it * WAYS + w + 1)
                        if w >= SLOTS:
                            pe.wait_ge(qk_biased, it * WAYS + w + 1 - SLOTS)
                            pe.wait_ge(v_biased, it * WAYS + w + 1 - SLOTS)
                        else:
                            pe.wait_ge(qk_scaled, it * WAYS + w + 1)
                        for t in range(TILES):
                            last = nc.tensor.matmul(psQK[w][:, t // 2, (t % 2) * 2 * DIM:(t % 2 + 1) * 2 * DIM],
                                                    sx_t[w][:, t * P:(t + 1) * P], c["w_qkv"][:, 0:2 * DIM],
                                                    start=True, stop=True)
                        last.then_inc(qk_projected, 1)
                        for t in range(TILES):
                            last = nc.tensor.matmul(psV[w][:, t * DIM:(t + 1) * DIM], sx_t[w][:, t * P:(t + 1) * P],
                                                    c["w_qkv"][:, 2 * DIM:], start=True, stop=True)
                        last.then_inc(v_projected, 1)
                    for w in range(WAYS):
                        pe.wait_ge(qk_normed, it * WAYS + w + 1)
                        if w >= SLOTS:
                            pe.wait_ge(qk_scaled, it * WAYS + w + 1)
                        for a in range(2):
                            for t in range(TILES):
                                last = nc.tensor.transpose(psQK[w][:, a, t * P:(t + 1) * P], qk[w][:, t, a, :], c["ident"][:, :])
                        last.then_inc(qk_t_done, 1)

            @block.sync
            def _(sp):
                with sp.Fori(0, ITERS) as it:
                    for w in range(WAYS):
                        sp.wait_ge(coarse_scaled, it * WAYS + w + 1)
                        sp.wait_ge(fine_copied, it * WAYS + w + 1)
                        sp.dma_start(h_rows[it, w], h[w][:, :, :].rearrange("p t n -> p (t n)")).then_inc(h_stored[w], 16)
                    for w in range(WAYS):
                        sp.wait_ge(v_biased, it * WAYS + w + 1)
                        at = w % PER_BATCH
                        sp.dma_start(v_rows[it * (WAYS // PER_BATCH) + w // PER_BATCH, :, at * TILES:(at + 1) * TILES, :],
                                     vrow[w][:, :, :, :].rearrange("p t h d -> p t (h d)")).then_inc(v_stored[w], 16)
                    for w in range(WAYS):
                        sp.wait_ge(part2_done, it * WAYS + w + 1)
                        for n in range(PARTS):
                            at = w % PER_BATCH
                            sp.dma_start(qk_parts[it * (WAYS // PER_BATCH) + w // PER_BATCH, :, n, :,
                                                  at * CHUNK:(at + 1) * CHUNK].rearrange("a p n -> p a n"),
                                         part[n][w][:, :, :]).then_inc(parts_stored[w], 16)
                for w in range(WAYS):
                    sp.wait_ge(h_stored[w], (ITERS + 1) * 16)
                    sp.wait_ge(v_stored[w], (ITERS + 1) * 16)
                    sp.wait_ge(parts_stored[w], (ITERS + 1) * 16 * PARTS)


def attend(nc, qk_parts, v_rows, o_cols):
    STEPS = HALVES * TOKT
    PAIR = 2 * GROUPS * STEPS
    PAIRS = BATCH // 2
    LEAD = STEPS + 3
    SRING, MRING, PRING = 3, 2, 4
    MAXES = GH * TOKT
    M_STEP = MAXES // STEPS
    LOADS = 2 * len(Q_TERMS) + 1

    ctx = ExitStack()
    with ctx:
        def sb(name, shape, dt=F32):
            return ctx.enter_context(nc.sbuf_tensor(name, shape, dt))

        def ps(name, shape):
            return ctx.enter_context(nc.psum_tensor(name, shape, F32))

        def sem(name):
            return ctx.enter_context(nc.semaphore("b_" + name))

        qs = [sb(f"qs{i}", [ROWS, HEADS, SEQ], BF16) for i in range(2)]
        ks = [sb(f"ks{i}", [ROWS, HEADS, SEQ], BF16) for i in range(2)]
        vs = [sb(f"vs{i}", [P, TOKT, HEADS, VW]) for i in range(2)]
        prob = [sb(f"prob{i}", [P, GH, BANK]) for i in range(PRING)]
        neg_max = [sb(f"b_neg_max{i}", [P, MAXES]) for i in range(2)]
        mrest = [sb(f"mrest{i}", [P, MAXES]) for i in range(2)]
        mpart = [sb(f"mpart{i}", [P, PARTS, MAXES], BF16) for i in range(2)]
        mpart_t = [sb(f"mpart_t{i}", [P, PARTS, MAXES], BF16) for i in range(2)]
        ot = [sb(f"ot{i}", [P, BANK]) for i in range(2)]
        psS = [ps(f"psS{i}", [P, BANK]) for i in range(SRING)]
        psM = [ps(f"psM{i}", [P, HALVES, BANK]) for i in range(MRING)]
        psO = ps("psO", [P, BANK])

        loaded = [sem(f"loaded{i}") for i in range(2)]
        cleared = sem("cleared")
        scored = sem("scored")
        score_free = sem("score_free")
        prob_free = sem("prob_free")
        max_scored = sem("max_scored")
        max_free = sem("max_free")
        split = sem("split")
        max_t_done = sem("max_t_done")
        max_loaded = [sem(f"max_loaded{i}") for i in range(2)]
        out_free = sem("out_free")
        o_stored = [sem(f"o_stored{i}") for i in range(2)]
        SPLITS = 4

        with nc.Block() as block:
            @block.sync
            def _(sp):
                preset(sp, score_free, 1)
                preset(sp, prob_free, PRING)
                preset(sp, max_free, MRING)
                preset(sp, out_free, 1)
                for i in range(2):
                    preset(sp, o_stored[i], 16)

            @block.gpsimd
            def _(pool):
                for i in range(2):
                    nc.gpsimd.memset(ks[i][DATA_ROWS:ROWS, :, :], 1.0).then_inc(cleared, 1)

            @block.vector
            def _(dve):
                nc.vector.memset(psO[:, :], 0.0).then_inc(cleared, 1)

        def load(sp, batch, buf):
            for i, (qp, kp) in enumerate(zip(Q_TERMS, K_TERMS)):
                r = slice(i * HD, (i + 1) * HD)
                sp.dma_start(qs[buf][r, :, :], qk_parts[batch, 0, qp].rearrange("(h d) n -> d h n", d=HD)).then_inc(loaded[buf], 16)
                sp.dma_start(ks[buf][r, :, :], qk_parts[batch, 1, kp].rearrange("(h d) n -> d h n", d=HD)).then_inc(loaded[buf], 16)
            sp.dma_start(vs[buf][:, :, :, :].rearrange("p t h d -> p t (h d)"), v_rows[batch]).then_inc(loaded[buf], 16)

        def place(step):
            g = step // STEPS
            return g, (g // GROUPS) % 2, g % GROUPS, step % STEPS // TOKT, step % TOKT

        with nc.Block() as block:
            @block.sync
            def _(sp):
                def place_maxima(p, g):
                    buf, gb = (g // GROUPS) % 2, g % GROUPS
                    sp.wait_ge(max_t_done, p * 2 * GROUPS + g + 1)
                    for n in range(PARTS):
                        dst = qs[buf][DATA_ROWS + n:DATA_ROWS + n + 1, GH * gb:GH * (gb + 1), :]
                        dst = dst.rearrange("o h (t a r) -> o a (h t) r", t=TOKT, a=P // MAXES)
                        for a in range(P // MAXES):
                            sp.dma_start(dst[:, a, :, :], mpart_t[g % 2][a * MAXES:(a + 1) * MAXES, n, :]).then_inc(
                                max_loaded[g % 2], 16)

                def store(p, half):
                    sp.wait_ge(out_free, p * (PAIR // TOKT) + half + 2)
                    sp.dma_start(o_cols[2 * p + half // 4, half // 2 % 2, :, half % 2 * BANK:(half % 2 + 1) * BANK],
                                 ot[half % 2][:, :]).then_inc(o_stored[half % 2], 16)

                def pair(p, last):
                    sp.wait_ge(prob_free, p * PAIR + PRING)
                    load(sp, 2 * p + 1, 1)
                    store(p, 0)
                    place_maxima(p, 1)
                    store(p, 1)
                    store(p, 2)
                    place_maxima(p, 2)
                    store(p, 3)
                    if not last:
                        sp.wait_ge(prob_free, p * PAIR + PAIR // 2 + PRING)
                        load(sp, 2 * p + 2, 0)
                    store(p, 4)
                    place_maxima(p, 3)
                    store(p, 5)
                    store(p, 6)
                    if not last:
                        place_maxima(p, 4)
                    store(p, 7)

                load(sp, 0, 0)
                place_maxima(0, 0)
                with sp.Fori(0, PAIRS - 1) as p:
                    pair(p, False)
                pair(PAIRS - 1, True)
                for i in range(2):
                    sp.wait_ge(o_stored[i], 16 + 16 * BATCH * GROUPS)

            @block.tensor
            def _(pe):
                def find_max(p, step):
                    g, buf, gb, _, _ = place(step)
                    if step % (GROUPS * STEPS) == 0:
                        pe.wait_ge(loaded[buf], (p + 1 + step // PAIR) * 16 * LOADS)
                    for m in range(M_STEP):
                        unit = step % STEPS * M_STEP + m
                        hh, tile = GH * gb + unit // TOKT, unit % TOKT
                        count = step * M_STEP + m
                        pe.wait_ge(max_free, p * PAIR * M_STEP + count + 1)
                        for half in range(HALVES):
                            last_mm = nc.tensor.matmul(psM[count % MRING][:, half, :],
                                                       qs[buf][0:DATA_ROWS, hh, tile * P:(tile + 1) * P],
                                                       ks[buf][0:DATA_ROWS, hh, half * BANK:(half + 1) * BANK],
                                                       start=True, stop=True)
                        last_mm.then_inc(max_scored, 1)
                        yield

                def score(p, step, heads):
                    g, buf, gb, half, tile = place(step)
                    if step % STEPS == 0 and heads[0] == 0:
                        pe.wait_ge(max_loaded[g % 2], (p * GROUPS + g // 2 + 1) * 16 * PARTS * (P // MAXES))
                    for hh in heads:
                        unit = step * GH + hh
                        pe.wait_ge(score_free, p * PAIR * GH + 1 + max(unit - SRING + 1, 0))
                        nc.tensor.matmul(psS[unit % SRING][:, :],
                                         ks[buf][0:ROWS, GH * gb + hh, tile * P:(tile + 1) * P],
                                         qs[buf][0:ROWS, GH * gb + hh, half * BANK:(half + 1) * BANK],
                                         start=True, stop=True).then_inc(scored, 1)

                def add_values(p, step):
                    g, buf, gb, _, tile = place(step)
                    pe.wait_ge(score_free, p * PAIR * GH + (step + 1) * GH + 1)
                    if tile == 0:
                        pe.wait_ge(out_free, p * (PAIR // TOKT) + step // TOKT + 1)
                    for hh in range(GH):
                        last_mm = nc.tensor.matmul(psO[HP * hh:HP * hh + VW, :], vs[buf][:, tile, GH * gb + hh, :],
                                                   prob[step % PRING][:, hh, :], start=tile == 0, stop=tile == TOKT - 1)
                    last_mm.then_inc(prob_free, 1)

                def pair(p, last):
                    for step in range(PAIR):
                        ahead = step + LEAD
                        units = find_max(p, ahead) if not (last and ahead >= PAIR) else iter(())
                        score(p, step, (0, 1))
                        next(units, None)
                        score(p, step, (2, 3))
                        next(units, None)
                        if step:
                            add_values(p, step - 1)
                    add_values(p, PAIR - 1)

                pe.wait_ge(cleared, 3)
                for step in range(LEAD):
                    for _ in find_max(0, step):
                        pass
                with pe.Fori(0, PAIRS - 1) as p:
                    pair(p, False)
                pair(PAIRS - 1, True)

            @block.scalar
            def _(act):
                def pair(p):
                    for step in range(PAIR):
                        act.wait_ge(prob_free, p * PAIR + step + 1)
                        for hh in range(GH):
                            unit = step * GH + hh
                            act.wait_ge(scored, p * PAIR * GH + unit + 1)
                            nc.scalar.activation(prob[step % PRING][:, hh, :], psS[unit % SRING][:, :],
                                                 ACT.Exp).then_inc(score_free, 1)

                with act.Fori(0, PAIRS) as p:
                    pair(p)

            @block.vector
            def _(dve):
                def find_max(p, step):
                    g = step // STEPS
                    for m in range(M_STEP):
                        unit = step % STEPS * M_STEP + m
                        count = step * M_STEP + m
                        dve.wait_ge(max_scored, p * PAIR * M_STEP + count + 1)
                        nc.vector.tensor_reduce(neg_max[g % 2][:, unit:unit + 1], psM[count % MRING][:, :, :],
                                                AX.XY, ALU.max, negate=True).then_inc(max_free, 1)
                    if step % STEPS == STEPS - 1:
                        i, k = g % 2, (p * 2 * GROUPS + g) * SPLITS
                        dve.wait_ge(max_free, p * PAIR * M_STEP + (step + 1) * M_STEP + MRING)
                        nc.vector.tensor_copy(mpart[i][:, 0, :], neg_max[i][:, :]).then_inc(split, 1)
                        dve.wait_ge(split, k + 1)
                        nc.vector.tensor_tensor(mrest[i][:, :], neg_max[i][:, :], mpart[i][:, 0, :], ALU.subtract).then_inc(split, 1)
                        dve.wait_ge(split, k + 2)
                        nc.vector.tensor_copy(mpart[i][:, 1, :], mrest[i][:, :]).then_inc(split, 1)
                        dve.wait_ge(split, k + 3)
                        nc.vector.tensor_tensor(mpart[i][:, 2, :], mrest[i][:, :], mpart[i][:, 1, :], ALU.subtract).then_inc(split, 1)
                        dve.wait_ge(split, k + 4)
                        nc.vector.transpose(mpart_t[i][:, :, :].rearrange("p n m -> p (n m)"),
                                            mpart[i][:, :, :].rearrange("p n m -> p (n m)")).then_inc(max_t_done, 1)

                def copy_out(p, half):
                    dve.wait_ge(prob_free, p * PAIR + (half + 1) * TOKT + PRING)
                    dve.wait_ge(o_stored[half % 2], (p * (PAIR // TOKT // 2) + half // 2 + 1) * 16)
                    nc.vector.tensor_copy(ot[half % 2][:, :], psO[:, :]).then_inc(out_free, 1)

                def pair(p, last):
                    for step in range(PAIR):
                        ahead = step + LEAD
                        if not (last and ahead >= PAIR):
                            find_max(p, ahead)
                        if step and step % TOKT == 0:
                            copy_out(p, step // TOKT - 1)
                    copy_out(p, PAIR // TOKT - 1)

                for step in range(LEAD):
                    find_max(0, step)
                with dve.Fori(0, PAIRS - 1) as p:
                    pair(p, False)
                pair(PAIRS - 1, True)


def finish(nc, c, h_rows, o_cols, out):
    ctx = ExitStack()
    with ctx:
        def ways(name, shape, dt=F32):
            return [ctx.enter_context(nc.sbuf_tensor(f"{name}{w}", shape, dt)) for w in range(WAYS)]

        def sem(name):
            return ctx.enter_context(nc.semaphore("c_" + name))

        def way_sems(name):
            return [sem(f"{name}{w}") for w in range(WAYS)]

        GHH = TILES * HEADS
        o_in = ways("o_in", [P, GROUPS, CHUNK])
        h_in = ways("h_in", [P, TILES, DIM])
        h_bias = ways("h_bias", [P, TILES, DIM])
        inv_l = ways("inv_l", [P, GHH])
        o = ways("o", [P, TILES, DIM])
        so = ways("so", [P, TILES, DIM])
        so_t = ways("so_t", [P, CHUNK])
        h2 = ways("h2_", [P, TILES, DIM])
        stat = ways("c_stat", [P, TILES, 6])
        mv = ways("c_mv", [P, TILES, 2])
        var_eps = ways("c_var_eps", [P, TILES])
        rstd = ways("c_rstd", [P, TILES])
        y = ways("y", [P, TILES, DIM])
        y_t = ways("y_t", [P, CHUNK])
        neg_max = ways("c_neg_max", [P, TILES])
        logit = ways("c_logit", [P, TILES, EXPERTS])
        prob = ways("c_prob", [P, TILES, EXPERTS])
        inv_sum = ways("c_inv_sum", [P, TILES])
        top = ways("top", [P, TILES, 8])
        top_i = ways("top_i", [P, TILES, 8], U32)
        top_f = ways("top_f", [P, TILES, 2])
        first = ways("first", [P, TILES, EXPERTS])
        second = ways("second", [P, TILES, EXPERTS])
        chosen = ways("chosen", [P, TILES, EXPERTS], BF16)
        before = ways("before", [P, TILES, EXPERTS])
        gate = ways("gate", [P, TILES])
        hid = ways("hid", [P, FK, CHUNK])
        y2 = ways("y2_", [P, TILES, DIM])
        res = ways("res", [P, TILES, DIM])
        psT = [ctx.enter_context(nc.psum_tensor(f"c_psT{i}", [P, 2, BANK], F32)) for i in range(SLOTS)] * (WAYS // SLOTS)
        psR = [ctx.enter_context(nc.psum_tensor(f"c_psR{i}", [P, 2, TILES * EXPERTS], F32)) for i in range(SLOTS)] * (WAYS // SLOTS)
        psF = [ctx.enter_context(nc.psum_tensor(f"c_psF{i}", [P, BANK], F32)) for i in range(SLOTS)] * (WAYS // SLOTS)

        o_loaded = way_sems("o_loaded")
        h_loaded = way_sems("h_loaded")
        o_free = sem("o_free")
        h_biased = sem("h_biased")
        inv_l_done = sem("inv_l_done")
        o_done = sem("o_done")
        tanh_done = sem("tanh_done")
        silu_done = sem("silu_done")
        silu_t_done = sem("silu_t_done")
        silu_t_copied = sem("silu_t_copied")
        projected = sem("projected")
        h2_done = sem("h2_done")
        stats_done = sem("stats_done")
        aggr_done = sem("aggr_done")
        eps_done = sem("eps_done")
        rstd_done = sem("rstd_done")
        y_done = sem("y_done")
        y_t_done = sem("y_t_done")
        y_t_copied = sem("y_t_copied")
        routed = sem("routed")
        max_found = sem("max_found")
        logit_shifted = sem("logit_shifted")
        exp_done = sem("exp_done")
        sum_done = sem("sum_done")
        inv_sum_done = sem("inv_sum_done")
        prob_done = sem("prob_done")
        top_done = sem("top_done")
        index_done = sem("index_done")
        index_cast = sem("index_cast")
        hot_done = sem("hot_done")
        chosen_done = sem("chosen_done")
        counted = sem("counted")
        before_done = sem("before_done")
        carried = sem("carried")
        kept_done = sem("kept_done")
        kept_prob_done = sem("kept_prob_done")
        gate_done = sem("gate_done")
        up_done = sem("up_done")
        gelu_done = sem("gelu_done")
        down_done = sem("down_done")
        y2_done = sem("y2_done")
        res_done = sem("res_done")
        res_stored = way_sems("res_stored")

        with nc.Block() as block:
            @block.sync
            def _(sp):
                preset(sp, o_free, WAYS)
                preset(sp, h_biased, WAYS)
                preset(sp, h2_done, WAYS)
                preset(sp, y2_done, SLOTS)
                preset(sp, carried, 1)
                for w in range(WAYS):
                    preset(sp, res_stored[w], 16)

        def count_chosen(pe, it, w):
            pe.wait_ge(chosen_done, it * WAYS + w + 1)
            if w >= SLOTS:
                pe.wait_ge(carried, it * WAYS + w + 2 - SLOTS)
            for t in range(TILES):
                dst = psR[w][:, 1, t * EXPERTS:(t + 1) * EXPERTS]
                for u in range(t):
                    nc.tensor.matmul(dst, c["ones"][:, :], chosen[w][:, u, :], start=u == 0, stop=False)
                nc.tensor.matmul(dst, c["later"][:, :], chosen[w][:, t, :], start=t == 0, stop=True)
            for u in range(TILES):
                last = nc.tensor.matmul(psR[w][:, 0, 0:EXPERTS], c["ones"][:, :], chosen[w][:, u, :],
                                        start=u == 0, stop=u == TILES - 1)
            last.then_inc(counted, 1)

        with nc.Block() as block:
            @block.sync
            def _(sp):
                with sp.Fori(0, ITERS) as it:
                    for w in range(WAYS):
                        n = it * WAYS + w + 1
                        sp.wait_ge(o_free, n)
                        at = w % PER_BATCH
                        sp.dma_start(o_in[w][:, :, :], o_cols[it * (WAYS // PER_BATCH) + w // PER_BATCH, :, :,
                                                              at * CHUNK:(at + 1) * CHUNK]
                                     .rearrange("g p n -> p g n")).then_inc(o_loaded[w], 16)
                        sp.wait_ge(h_biased, n)
                        sp.dma_start(h_in[w][:, :, :].rearrange("p t n -> p (t n)"), h_rows[it, w]).then_inc(h_loaded[w], 16)

            @block.gpsimd
            def _(pool):
                with pool.Fori(0, ITERS) as it:
                    for w in range(WAYS):
                        n = it * WAYS + w + 1
                        pool.wait_ge(h_loaded[w], (it + 1) * 16)
                        pool.wait_ge(h2_done, n)
                        nc.gpsimd.tensor_tensor(h_bias[w][:, :, :], h_in[w][:, :, :],
                                                c["b_o"][:, :].unsqueeze(1).to_broadcast([P, TILES, DIM]),
                                                ALU.add).then_inc(h_biased, 1)
                    for w in range(WAYS):
                        pool.wait_ge(eps_done, it * WAYS + w + 1)
                        nc.gpsimd.tensor_tensor(rstd[w][:, :], var_eps[w][:, :], c["neg_half"][:, 0:TILES], ALU.pow).then_inc(rstd_done, 1)

            @block.scalar
            def _(act):
                with act.Fori(0, ITERS) as it:
                    for w in range(WAYS):
                        act.wait_ge(o_done, it * WAYS + w + 1)
                        nc.scalar.activation(so[w][:, :, :], o[w][:, :, :], ACT.Tanh, scale=0.5).then_inc(tanh_done, 1)
                    for w in range(WAYS):
                        act.wait_ge(silu_t_done, it * WAYS + w + 1)
                        nc.scalar.activation(so_t[w][:, :], psT[w][:, 0, :], ACT.Copy, scale=0.5).then_inc(silu_t_copied, 1)
                    for w in range(WAYS):
                        act.wait_ge(y_t_done, it * WAYS + w + 1)
                        nc.scalar.activation(y_t[w][:, :], psT[w][:, 0, :], ACT.Copy).then_inc(y_t_copied, 1)
                    for w in range(WAYS):
                        act.wait_ge(logit_shifted, it * WAYS + w + 1)
                        nc.scalar.activation(prob[w][:, :, :], logit[w][:, :, :], ACT.Exp).then_inc(exp_done, 1)
                    for w in range(WAYS):
                        for k in range(FK):
                            act.wait_ge(up_done, (it * WAYS + w) * FK + k + 1)
                            src = psF[w][:, :] if k % 2 == 0 else psT[w][:, 0, :]
                            nc.scalar.activation(hid[w][:, k, :], src, ACT.Gelu, bias=c["b1"][:, k:k + 1]).then_inc(gelu_done, 1)
                    for w in range(WAYS):
                        n = it * WAYS + w + 1
                        act.wait_ge(res_done, n)
                        at = w % PER_BATCH
                        act.dma_start(out[it * (WAYS // PER_BATCH) + w // PER_BATCH, :, at * TILES:(at + 1) * TILES, :],
                                      res[w][:, :, :]).then_inc(res_stored[w], 16)
                for w in range(WAYS):
                    act.wait_ge(res_stored[w], (ITERS + 1) * 16)

            @block.tensor
            def _(pe):
                with pe.Fori(0, ITERS) as it:
                    for w in range(WAYS):
                        pe.wait_ge(o_loaded[w], (it + 1) * 16)
                        if w >= SLOTS:
                            pe.wait_ge(o_done, it * WAYS + w + 1 - SLOTS)
                        else:
                            pe.wait_ge(y2_done, it * WAYS + w + 1)
                        for t in range(TILES):
                            for g in range(GROUPS):
                                at = (t % 2 * GROUPS + g) * P
                                last = nc.tensor.transpose(psT[w][:, t // 2, at:at + P], o_in[w][:, g, t * P:(t + 1) * P], c["ident"][:, :])
                        last.then_inc(o_free, 1)
                    for w in range(WAYS):
                        pe.wait_ge(silu_done, it * WAYS + w + 1)
                        if w >= SLOTS:
                            pe.wait_ge(silu_t_copied, it * WAYS + w + 1 - SLOTS)
                        for t in range(TILES):
                            last = nc.tensor.transpose(psT[w][:, 0, t * P:(t + 1) * P], so[w][:, t, :], c["ident"][:, :])
                        last.then_inc(silu_t_done, 1)
                    for w in range(WAYS):
                        pe.wait_ge(silu_t_copied, it * WAYS + w + 1)
                        if w >= SLOTS:
                            pe.wait_ge(h2_done, it * WAYS + w + 1 + WAYS - SLOTS)
                        for t in range(TILES):
                            last = nc.tensor.matmul(psT[w][:, 1, t * DIM:(t + 1) * DIM], so_t[w][:, t * P:(t + 1) * P],
                                                    c["w_o"][:, :], start=True, stop=True)
                        last.then_inc(projected, 1)
                    for w in range(WAYS):
                        pe.wait_ge(y_done, it * WAYS + w + 1)
                        if w >= SLOTS:
                            pe.wait_ge(y_t_copied, it * WAYS + w + 1 - SLOTS)
                        for t in range(TILES):
                            last = nc.tensor.transpose(psT[w][:, 0, t * P:(t + 1) * P], y[w][:, t, :], c["ident"][:, :])
                        last.then_inc(y_t_done, 1)
                    for w in range(WAYS):
                        pe.wait_ge(y_t_copied, it * WAYS + w + 1)
                        if w >= SLOTS:
                            pe.wait_ge(logit_shifted, it * WAYS + w + 1 - SLOTS)
                        for t in range(TILES):
                            last = nc.tensor.matmul(psR[w][:, 0, t * EXPERTS:(t + 1) * EXPERTS], y_t[w][:, t * P:(t + 1) * P],
                                                    c["router"][:, :], start=True, stop=True)
                        last.then_inc(routed, 1)
                    for w in range(WAYS):
                        for k in range(FK):
                            if k >= 2:
                                pe.wait_ge(gelu_done, (it * WAYS + w) * FK + k - 1)
                            elif w >= SLOTS:
                                pe.wait_ge(gelu_done, (it * WAYS + w - SLOTS) * FK + k + 3)
                            dst = psF[w][:, :] if k % 2 == 0 else psT[w][:, 0, :]
                            nc.tensor.matmul(dst, c["w1"][:, k * P:(k + 1) * P], y_t[w][:, :], start=True, stop=True).then_inc(up_done, 1)
                    for w in range(WAYS):
                        count_chosen(pe, it, w)
                    for w in range(WAYS):
                        pe.wait_ge(gelu_done, (it * WAYS + w + 1) * FK)
                        if w >= SLOTS:
                            pe.wait_ge(y2_done, it * WAYS + w + 1)
                        for t in range(TILES):
                            for k in range(FK):
                                last = nc.tensor.matmul(psT[w][:, 1, t * DIM:(t + 1) * DIM], hid[w][:, k, t * P:(t + 1) * P],
                                                        c["w2"][:, k, :], start=k == 0, stop=k == FK - 1)
                        last.then_inc(down_done, 1)

            @block.vector
            def _(dve):
                with dve.Fori(0, ITERS) as it:
                    for w in range(WAYS):
                        n = it * WAYS + w + 1
                        dve.wait_ge(o_free, n + WAYS)
                        blocks = psT[w][:, :, :].rearrange("p b (x d) -> p (b x) d", d=HP)
                        nc.vector.reciprocal(inv_l[w][:, :].unsqueeze(2), blocks[:, :, HD:VW]).then_inc(inv_l_done, 1)
                        dve.wait_ge(inv_l_done, n)
                        nc.vector.tensor_tensor(o[w][:, :, :].rearrange("p t (x d) -> p (t x) d", d=HD), blocks[:, :, 0:HD],
                                                inv_l[w][:, :].unsqueeze(2).to_broadcast([P, GHH, HD]), ALU.mult).then_inc(o_done, 1)
                    for w in range(WAYS):
                        n = it * WAYS + w + 1
                        dve.wait_ge(tanh_done, n)
                        nc.vector.scalar_tensor_tensor(out=so[w][:, :, :], in0=so[w][:, :, :], scalar=1.0,
                                                       in1=o[w][:, :, :], op0=ALU.add, op1=ALU.mult).then_inc(silu_done, 1)
                    for w in range(WAYS):
                        n = it * WAYS + w + 1
                        dve.wait_ge(projected, n)
                        dve.wait_ge(h_biased, n + WAYS)
                        nc.vector.tensor_tensor(h2[w][:, :, :], psT[w][:, 1, :].rearrange("p (t n) -> p t n", t=TILES),
                                                h_bias[w][:, :, :], ALU.add).then_inc(h2_done, 1)
                    for w in range(WAYS):
                        dve.wait_ge(h2_done, it * WAYS + w + 1 + WAYS)
                        for t in range(TILES):
                            last = nc.vector.bn_stats(stat[w][:, t, :], h2[w][:, t, :])
                        last.then_inc(stats_done, 1)
                    for w in range(WAYS):
                        n = it * WAYS + w + 1
                        wait_apart(dve, stats_done, n)
                        for t in range(TILES):
                            last = nc.vector.bn_aggr(mv[w][:, t, :], stat[w][:, t, :])
                        last.then_inc(aggr_done, 1)
                        dve.wait_ge(aggr_done, n)
                        nc.vector.tensor_scalar(var_eps[w][:, :], mv[w][:, :, 1], EPS, None, ALU.add).then_inc(eps_done, 1)
                    for w in range(WAYS):
                        dve.wait_ge(rstd_done, it * WAYS + w + 1)
                        for t in range(TILES):
                            last = nc.vector.tensor_scalar(y[w][:, t, :], h2[w][:, t, :], mv[w][:, t, 0:1],
                                                           rstd[w][:, t:t + 1], ALU.subtract, ALU.mult)
                        last.then_inc(y_done, 1)
                    for w in range(WAYS):
                        n = it * WAYS + w + 1
                        scores = psR[w][:, 0, :].rearrange("p (t e) -> p t e", t=TILES)
                        dve.wait_ge(routed, n)
                        nc.vector.tensor_reduce(neg_max[w][:, :], scores, AX.X, ALU.max, negate=True).then_inc(max_found, 1)
                        dve.wait_ge(max_found, n)
                        nc.vector.tensor_tensor(logit[w][:, :, :], scores,
                                                neg_max[w][:, :].unsqueeze(2).to_broadcast([P, TILES, EXPERTS]),
                                                ALU.add).then_inc(logit_shifted, 1)
                    for w in range(WAYS):
                        n = it * WAYS + w + 1
                        dve.wait_ge(exp_done, n)
                        nc.vector.tensor_reduce(inv_sum[w][:, :], prob[w][:, :, :], AX.X, ALU.add).then_inc(sum_done, 1)
                        dve.wait_ge(sum_done, n)
                        nc.vector.reciprocal(inv_sum[w][:, :], inv_sum[w][:, :]).then_inc(inv_sum_done, 1)
                        dve.wait_ge(inv_sum_done, n)
                        nc.vector.tensor_tensor(prob[w][:, :, :], prob[w][:, :, :],
                                                inv_sum[w][:, :].unsqueeze(2).to_broadcast([P, TILES, EXPERTS]),
                                                ALU.mult).then_inc(prob_done, 1)
                    for w in range(WAYS):
                        n = it * WAYS + w + 1
                        wait_apart(dve, prob_done, n)
                        for t in range(TILES):
                            last = nc.vector.max(top[w][:, t, :], prob[w][:, t, :])
                        last.then_inc(top_done, 1)
                    for w in range(WAYS):
                        n = it * WAYS + w + 1
                        wait_apart(dve, top_done, n)
                        for t in range(TILES):
                            last = nc.vector.max_index(top_i[w][:, t, :], top[w][:, t, :], prob[w][:, t, :])
                        last.then_inc(index_done, 1)
                    for w in range(WAYS):
                        n = it * WAYS + w + 1
                        dve.wait_ge(index_done, n)
                        nc.vector.tensor_copy(top_f[w][:, :, :], top_i[w][:, :, 0:2]).then_inc(index_cast, 1)
                    for w in range(WAYS):
                        n = it * WAYS + w + 1
                        dve.wait_ge(index_cast, n)
                        ids = c["expert_ids"][:, :].unsqueeze(1).to_broadcast([P, TILES, EXPERTS])
                        for j, hot in enumerate((first, second)):
                            last = nc.vector.tensor_tensor(hot[w][:, :, :], ids,
                                                           top_f[w][:, :, j:j + 1].to_broadcast([P, TILES, EXPERTS]),
                                                           ALU.is_equal)
                        last.then_inc(hot_done, 1)
                    for w in range(WAYS):
                        dve.wait_ge(hot_done, it * WAYS + w + 1)
                        nc.vector.tensor_tensor(chosen[w][:, :, :], first[w][:, :, :], second[w][:, :, :],
                                                ALU.add).then_inc(chosen_done, 1)
                    for w in range(WAYS):
                        n = it * WAYS + w + 1
                        dve.wait_ge(counted, n)
                        dve.wait_ge(carried, n)
                        nc.vector.tensor_tensor(before[w][:, :, :],
                                                psR[w][:, 1, :].rearrange("p (t e) -> p t e", t=TILES),
                                                c["carry"][:, :].unsqueeze(1).to_broadcast([P, TILES, EXPERTS]),
                                                ALU.add).then_inc(before_done, 1)
                        dve.wait_ge(before_done, n)
                        nc.vector.tensor_tensor(c["carry"][:, :], psR[w][:, 0, 0:EXPERTS], c["carry"][:, :],
                                                ALU.add).then_inc(carried, 1)
                        nc.vector.scalar_tensor_tensor(out=before[w][:, :, :], in0=before[w][:, :, :], scalar=float(CAP),
                                                       in1=chosen[w][:, :, :], op0=ALU.is_lt, op1=ALU.mult).then_inc(kept_done, 1)
                        dve.wait_ge(kept_done, n)
                        nc.vector.tensor_tensor(before[w][:, :, :], before[w][:, :, :], prob[w][:, :, :],
                                                ALU.mult).then_inc(kept_prob_done, 1)
                        dve.wait_ge(kept_prob_done, n)
                        nc.vector.tensor_reduce(gate[w][:, :], before[w][:, :, :], AX.X, ALU.add).then_inc(gate_done, 1)
                    for w in range(WAYS):
                        n = it * WAYS + w + 1
                        dve.wait_ge(down_done, n)
                        nc.vector.tensor_tensor(y2[w][:, :, :], psT[w][:, 1, :].rearrange("p (t n) -> p t n", t=TILES),
                                                c["b2"][:, :].unsqueeze(1).to_broadcast([P, TILES, DIM]),
                                                ALU.add).then_inc(y2_done, 1)
                    for w in range(WAYS):
                        n = it * WAYS + w + 1
                        dve.wait_ge(gate_done, n)
                        dve.wait_ge(y2_done, n + SLOTS)
                        dve.wait_ge(res_stored[w], (it + 1) * 16)
                        for t in range(TILES):
                            last = nc.vector.scalar_tensor_tensor(out=res[w][:, t, :], in0=y2[w][:, t, :],
                                                                  scalar=gate[w][:, t:t + 1], in1=h2[w][:, t, :],
                                                                  op0=ALU.mult, op1=ALU.add)
                        last.then_inc(res_done, 1)


def kernel(**inputs):
    import numpy as _np
    import concourse.bacc as _bacc
    from concourse.bass_utils import run_bass_kernel_spmd as _run

    a = {k: _np.asarray(v) for k, v in inputs.items()}
    t, at, f = "L0_tok_", "L0_attn_", "L0_ffn_"
    chunks = BATCH * SEQ // CHUNK
    arrays = {
        "x_idx": a["x"].reshape(chunks, TILES, P).transpose(0, 2, 1),
        "table": _np.concatenate([a[t + "fine_embed_w"], a[t + "loc_to_cluster_w"].T], axis=1),
        "cluster_b": a[t + "loc_to_cluster_b"], "coarse_w": a[t + "coarse_embed_w"],
        "w_q": a[at + "w_q"], "b_q": a[at + "b_q"], "w_k": a[at + "w_k"], "b_k": a[at + "b_k"],
        "w_v": a[at + "w_v"], "b_v": a[at + "b_v"], "g_q": a[at + "g_q"], "be_q": a[at + "be_q"],
        "g_k": a[at + "g_k"], "be_k": a[at + "be_k"], "w_o": a[at + "w_o"], "b_o": a[at + "b_o"],
        "router_t": a[f + "router_w"].T, "w1_t": a[f + "w1"].T, "b1_c": a[f + "b1"].reshape(FK, P).T,
        "w2_t": a[f + "w2"].T, "b2": a[f + "b2"],
    }
    arrays = {k: _np.ascontiguousarray(v) for k, v in arrays.items()}
    nc = _bacc.Bacc("TRN2", target_bir_lowering=False, num_devices=1)
    args = {k: nc.dram_tensor("in_" + k, v.shape, mybir.dt.from_np(v.dtype), kind="ExternalInput").ap()
            for k, v in arrays.items()}
    out = nc.dram_tensor("out", (BATCH, SEQ, DIM), F32, kind="ExternalOutput").ap()
    build(nc, out=out.rearrange("b (t p) n -> b p t n", p=P), **args)
    r = _run(nc, [{"in_" + k: v for k, v in arrays.items()}], core_ids=[0])
    return r.results[0]["out"]
```

```python
import concourse.bass as bass
from concourse import mybir
from contextlib import ExitStack

F32 = mybir.dt.float32
BF16 = mybir.dt.bfloat16
I32 = mybir.dt.int32
U32 = mybir.dt.uint32
ALU = mybir.AluOpType
ACT = mybir.ActivationFunctionType
AX = mybir.AxisListType

P = 128
BATCH, SEQ, DIM = 8, 1024, 128
HEADS = 8
HD = DIM // HEADS
HALF = DIM // 2
CLUSTERS = 64
EXPERTS = 64
CAP = 128
FFN = 512
FK = FFN // P
EPS = 1e-5
QSCALE = float(DIM) ** -0.5

WAYS = 4
SLOTS = 2
TILES = 4
CHUNK = TILES * P
ITERS = BATCH * SEQ // (CHUNK * WAYS)
PER_BATCH = SEQ // CHUNK

BANK = 512
HALVES = SEQ // BANK
TOKT = SEQ // P
PARTS = 3
Q_TERMS = (0, 0, 1, 1, 0, 2)
K_TERMS = (0, 1, 0, 1, 2, 0)
DATA_ROWS = HD * len(Q_TERMS)
ROWS = DATA_ROWS + PARTS
VW = HD + 1
GH = 4
GROUPS = HEADS // GH
HP = 32
BIAS_ROWS = (PARTS - 1) * HP + 1


def build(nc, x_idx, table, cluster_b, coarse_w, w_q, b_q, w_k, b_k, w_v, b_v, g_q, be_q, g_k, be_k,
          w_o, b_o, router_t, w1_t, b1_c, w2_t, b2, out):
    qk_parts = nc.dram_tensor("qk_parts", (BATCH, 2, PARTS, P, SEQ), BF16).ap()
    v_rows = nc.dram_tensor("v_rows", (BATCH, P, TOKT, HEADS * VW), F32).ap()
    h_rows = nc.dram_tensor("h_rows", (ITERS, WAYS, P, TILES * DIM), F32).ap()
    o_cols = nc.dram_tensor("o_cols", (BATCH, GROUPS, P, SEQ), F32).ap()
    inv_l = nc.dram_tensor("inv_l", (BATCH * HEADS, SEQ), F32).ap()

    ctx = ExitStack()
    with ctx:
        def keep(name, shape, dt=F32):
            return ctx.enter_context(nc.sbuf_tensor(name, shape, dt))

        c = {}
        c["ident"] = keep("ident", [P, P])
        c["later"] = keep("later", [P, P], BF16)
        c["ones"] = keep("ones", [P, P], BF16)
        c["expert_ids"] = keep("expert_ids", [P, EXPERTS])
        c["neg_half"] = keep("neg_half", [P, 2 * TILES])
        c["w_qkv"] = keep("w_qkv", [P, 3 * DIM])
        c["bias"] = keep("bias", [BIAS_ROWS, 5 * DIM])
        c["bias_parts"] = keep("bias_parts", [BIAS_ROWS, 5 * DIM], BF16)
        c["cluster_b"] = keep("cluster_b_sb", [P, CLUSTERS])
        c["coarse_w"] = keep("coarse_w_sb", [CLUSTERS, HALF])
        c["gain"] = keep("gain", [P, 2])
        c["shift"] = keep("shift", [P, 2])
        c["w_o"] = keep("w_o_sb", [P, DIM])
        c["router"] = keep("router_sb", [P, EXPERTS])
        c["w1"] = keep("w1_sb", [P, FFN])
        c["b1"] = keep("b1_sb", [P, FK])
        c["w2"] = keep("w2_sb", [P, FK, DIM])
        c["carry"] = keep("carry", [P, EXPERTS])
        c["idx_all"] = keep("idx_all", [P, (ITERS + 1) * WAYS * TILES], I32)

        setup(nc, ctx, c, x_idx, cluster_b, coarse_w, w_q, b_q, w_k, b_k, w_v, b_v, g_q, be_q, g_k, be_k,
              w_o, b_o, router_t, w1_t, b1_c, w2_t, b2)
        with ExitStack() as own:
            stacks = {name: own.enter_context(nc.semaphore("b_" + name + "0")) for name in ("loaded", "cleared")}
            stacks["qs"] = own.enter_context(nc.sbuf_tensor("qs0", [ROWS, HALVES, HEADS, BANK], BF16))
            stacks["ks"] = own.enter_context(nc.sbuf_tensor("ks0", [ROWS, HEADS, SEQ], BF16))
            stacks["vs"] = own.enter_context(nc.sbuf_tensor("vs0", [P, TOKT, HEADS, VW], F32))
            embed(nc, c, table, qk_parts, v_rows, h_rows, stacks)
            attend(nc, qk_parts, v_rows, o_cols, inv_l, stacks)
        finish(nc, c, h_rows, o_cols, inv_l, out)


def wait_apart(engine, sem, n):
    engine.to_reg(n)
    engine.wait_ge(sem, 1)
    engine.wait_ge(sem, n)


def add_bias(nc, c, dst, first, width):
    src = c["bias_parts"][:, first:first + width].unsqueeze(1).to_broadcast([BIAS_ROWS, BANK // width, width])
    nc.tensor.matmul(dst.rearrange("p (t n) -> p t n", n=width), c["ones"][0:BIAS_ROWS, :], src, start=True, stop=False)


def by_head(o_cols):
    return o_cols.rearrange("b g (h x) n -> (b g h) x n", x=HP)


def in_pieces(rows, piece):
    return rows.rearrange("r (s n) -> r s n", n=piece)


def preset(engine, sem, n):
    engine.sem_inc(sem, n)


def setup(nc, ctx, c, x_idx, cluster_b, coarse_w, w_q, b_q, w_k, b_k, w_v, b_v, g_q, be_q, g_k, be_k,
          w_o, b_o, router_t, w1_t, b1_c, w2_t, b2):
    loaded = ctx.enter_context(nc.semaphore("weights_loaded"))
    made = ctx.enter_context(nc.semaphore("constants_made"))
    scaled = ctx.enter_context(nc.semaphore("q_gain_scaled"))
    idx_int = ctx.enter_context(nc.sbuf_tensor("expert_ids_int", [P, EXPERTS], I32))
    idx_pad = ITERS * WAYS * TILES

    def rows(v, n=P):
        return v.rearrange("(a n) -> a n", a=1).to_broadcast([n, v.shape[0]])

    def column(v):
        return v.rearrange("(p a) -> p a", a=1)

    loads = [(c["w_qkv"][:, 0:DIM], w_q), (c["w_qkv"][:, DIM:2 * DIM], w_k), (c["w_qkv"][:, 2 * DIM:], w_v),
             (c["bias"][:, 0:DIM], rows(b_q, BIAS_ROWS)), (c["bias"][:, DIM:2 * DIM], rows(b_k, BIAS_ROWS)),
             (c["bias"][:, 2 * DIM:3 * DIM], rows(b_v, BIAS_ROWS)), (c["bias"][:, 3 * DIM:4 * DIM], rows(b_o, BIAS_ROWS)),
             (c["bias"][:, 4 * DIM:], rows(b2, BIAS_ROWS)),
             (c["cluster_b"][:, :], rows(cluster_b)), (c["coarse_w"][:, :], coarse_w),
             (c["gain"][:, 0:1], column(g_q)), (c["gain"][:, 1:2], column(g_k)),
             (c["shift"][:, 0:1], column(be_q)), (c["shift"][:, 1:2], column(be_k)),
             (c["w_o"][:, :], w_o), (c["router"][:, :], router_t),
             (c["w1"][:, :], w1_t), (c["b1"][:, :], b1_c),
             (c["w2"][:, :, :], w2_t.rearrange("(k p) n -> p k n", p=P)),
             (c["idx_all"][:, 0:idx_pad].rearrange("p (i t) -> p i t", t=TILES), x_idx.rearrange("i p t -> p i t"))]

    with nc.Block() as block:
        @block.sync
        def _(sp):
            for dst, src in loads:
                sp.dma_start(dst, src).then_inc(loaded, 16)
            sp.wait_ge(loaded, 16 * len(loads))

        @block.gpsimd
        def _(pool):
            nc.gpsimd.memset(c["ident"][:, :], 0.0).then_inc(made, 1)
            nc.gpsimd.memset(c["later"][:, :], 0.0).then_inc(made, 1)
            nc.gpsimd.memset(c["ones"][:, :], 1.0).then_inc(made, 1)
            nc.gpsimd.memset(c["neg_half"][:, :], -0.5).then_inc(made, 1)
            nc.gpsimd.memset(c["carry"][:, :], 0.0).then_inc(made, 1)
            nc.gpsimd.memset(c["idx_all"][:, idx_pad:], 0).then_inc(made, 1)
            nc.gpsimd.iota(idx_int[:, :], pattern=[[1, EXPERTS]], base=0, channel_multiplier=0).then_inc(made, 1)
            pool.wait_ge(made, 7)
            nc.gpsimd.affine_select(out=c["ident"][:, :], in_=c["ident"][:, :], compare_op=ALU.not_equal, fill=1.0,
                                    base=0, pattern=[[-1, P]], channel_multiplier=1).then_inc(made, 1)
            nc.gpsimd.affine_select(out=c["later"][:, :], in_=c["later"][:, :], compare_op=ALU.is_ge, fill=1.0,
                                    base=0, pattern=[[-1, P]], channel_multiplier=1).then_inc(made, 1)
            nc.gpsimd.tensor_copy(c["expert_ids"][:, :], idx_int[:, :]).then_inc(made, 1)

        @block.vector
        def _(dve):
            dve.wait_ge(loaded, 16 * len(loads))
            nc.vector.tensor_scalar(c["gain"][:, 0:1], c["gain"][:, 0:1], QSCALE, None, ALU.mult).then_inc(scaled, 1)
            nc.vector.tensor_scalar(c["shift"][:, 0:1], c["shift"][:, 0:1], QSCALE, None, ALU.mult).then_inc(scaled, 1)


def embed(nc, c, table, qk_parts, v_rows, h_rows, stacks):
    ctx = ExitStack()
    with ctx:
        def ways(name, shape, dt=F32):
            return [ctx.enter_context(nc.sbuf_tensor(f"{name}{w}", shape, dt)) for w in range(WAYS)]

        def sem(name):
            return ctx.enter_context(nc.semaphore("a_" + name))

        def way_sems(name):
            return [sem(f"{name}{w}") for w in range(WAYS)]

        idx = ways("idx", [P, TILES], I32)
        emb = ways("emb", [P, TILES, DIM])
        logit = ways("logit", [P, TILES, CLUSTERS])
        expo = ways("expo", [P, TILES, CLUSTERS])
        neg_max = ways("a_neg_max", [P, TILES])
        inv_sum = ways("a_inv_sum", [P, TILES])
        expo_t = ways("expo_t", [CLUSTERS, CHUNK])
        h = ways("h", [P, TILES, DIM])
        stat = ways("a_stat", [P, TILES, 6])
        mv = ways("a_mv", [P, TILES, 2])
        rs = ways("a_rs", [P, TILES])
        xn = ways("xn", [P, TILES, DIM])
        sx = ways("sx", [P, TILES, DIM])
        sx_t = ways("sx_t", [P, CHUNK])
        qk = ways("qk", [P, TILES, 2, DIM])
        vrow = ways("vrow", [P, TILES, HEADS, VW])
        stat2 = ways("a_stat2", [P, TILES * 2, 6])
        mv2 = ways("a_mv2", [P, TILES * 2, 2])
        rs3 = ways("a_rs3", [P, TILES * 2])
        k_offset = ways("k_offset", [P, TILES])
        full = ways("qk_full", [P, 2, CHUNK])
        rest = ways("qk_rest", [P, 2, CHUNK])
        part = [ways(f"qk_part{n}_", [P, 2, CHUNK], BF16) for n in range(PARTS)]
        psA = [ctx.enter_context(nc.psum_tensor(f"a_psA{i}", [P, BANK], F32)) for i in range(SLOTS)] * (WAYS // SLOTS)
        psV = [ctx.enter_context(nc.psum_tensor(f"a_psV{i}", [P, BANK], F32)) for i in range(SLOTS)] * (WAYS // SLOTS)
        psQK = [ctx.enter_context(nc.psum_tensor(f"a_psQK{i}", [P, 2, BANK], F32)) for i in range(SLOTS)] * (WAYS // SLOTS)

        ones_set = sem("ones_set")
        bias_split = sem("bias_split")
        bias_ready = sem("bias_ready")
        bias_rest = ctx.enter_context(nc.sbuf_tensor("bias_rest", [BIAS_ROWS, 5 * DIM], F32))
        bias_part = [ctx.enter_context(nc.sbuf_tensor(f"bias_part{n}", [BIAS_ROWS, 5 * DIM], BF16)) for n in range(PARTS)]
        idx_copied = sem("idx_copied")
        gathered = way_sems("gathered")
        logit_biased = sem("logit_biased")
        max_found = sem("max_found")
        logit_shifted = sem("logit_shifted")
        exp_done = sem("exp_done")
        sum_done = sem("sum_done")
        inv_done = sem("inv_done")
        exp_t_done = sem("exp_t_done")
        exp_t_copied = sem("exp_t_copied")
        coarse_done = sem("coarse_done")
        coarse_scaled = sem("coarse_scaled")
        fine_copied = sem("fine_copied")
        h_stored = way_sems("h_stored")
        stats_done = sem("stats_done")
        aggr_done = sem("aggr_done")
        both_var_done = sem("both_var_done")
        rstd_done = sem("rstd_done")
        xn_done = sem("xn_done")
        tanh_done = sem("tanh_done")
        silu_done = sem("silu_done")
        silu_t_done = sem("silu_t_done")
        silu_t_copied = sem("silu_t_copied")
        qk_projected = sem("qk_projected")
        v_projected = sem("v_projected")
        qk_copied = sem("qk_copied")
        v_copied = sem("v_copied")
        v_stored = way_sems("v_stored")
        stats2_done = sem("stats2_done")
        aggr2_done = sem("aggr2_done")
        means2_done = sem("means2_done")
        rstd2_done = sem("rstd2_done")
        k_offset_done = sem("k_offset_done")
        q_normed = sem("q_normed")
        k_normed = sem("k_normed")
        qk_t_done = sem("qk_t_done")
        qk_scaled = sem("qk_scaled")
        part0_done = sem("part0_done")
        rest1_done = sem("rest1_done")
        part1_done = sem("part1_done")
        part2_done = sem("part2_done")
        parts_stored = way_sems("parts_stored")

        with nc.Block() as block:
            @block.sync
            def _(sp):
                for w in range(WAYS):
                    for s in (h_stored, v_stored, parts_stored):
                        preset(sp, s[w], 16 * (PARTS if s is parts_stored else 1))
                preset(sp, qk_scaled, SLOTS)

            @block.vector
            def _(dve):
                for w in range(WAYS):
                    last = nc.vector.memset(vrow[w][:, :, :, HD:VW], 1.0)
                last.then_inc(ones_set, 1)

        with nc.Block() as block:
            @block.gpsimd
            def _(pool):
                def gather(r):
                    for w in range(WAYS):
                        cols = bass.ds((r * WAYS + w) * TILES, TILES)
                        nc.gpsimd.tensor_copy(idx[w][:, :], c["idx_all"][:, cols]).then_inc(idx_copied, 1)
                        wait_apart(pool, idx_copied, r * WAYS + w + 1)
                        for t in range(TILES):
                            nc.gpsimd.indirect_dma_start(
                                out=emb[w][:, t, :], out_offset=None, in_=table,
                                in_offset=bass.IndirectOffsetOnAxis(ap=idx[w][:, t:t + 1], axis=0)).then_inc(gathered[w], 16)

                def regather(r):
                    pool.wait_ge(fine_copied, r * WAYS)
                    wait_apart(pool, logit_biased, r * WAYS)
                    for w in range(WAYS):
                        pool.wait_ge(gathered[w], r * 16 * TILES)
                    gather(r)

                def root_front(r):
                    for w in range(WAYS):
                        pool.wait_ge(both_var_done, r * WAYS + w + 1)
                        nc.gpsimd.tensor_tensor(rs[w][:, :], rs[w][:, :], c["neg_half"][:, 0:TILES],
                                                ALU.pow).then_inc(rstd_done, 1)

                def root_back(r):
                    for w in range(WAYS):
                        pool.wait_ge(aggr2_done, r * WAYS + w + 1)
                        nc.gpsimd.tensor_tensor(rs3[w][:, :], rs3[w][:, :], c["neg_half"][:, :], ALU.pow).then_inc(rstd2_done, 1)

                def subtract_part0(r):
                    for w in range(WAYS):
                        n = r * WAYS + w + 1
                        pool.wait_ge(qk_scaled, n + SLOTS)
                        pool.wait_ge(part0_done, n)
                        nc.gpsimd.tensor_tensor(rest[w][:, :, :], full[w][:, :, :], part[0][w][:, :, :],
                                                ALU.subtract).then_inc(rest1_done, 1)

                gather(0)
                regather(1)
                root_front(0)
                with pool.Fori(0, ITERS - 1) as it:
                    regather(it + 2)
                    root_back(it)
                    root_front(it + 1)
                    subtract_part0(it)
                root_back(ITERS - 1)
                subtract_part0(ITERS - 1)
                for w in range(WAYS):
                    pool.wait_ge(gathered[w], (ITERS + 1) * 16 * TILES)

            @block.vector
            def _(dve):
                def logits(r):
                    for w in range(WAYS):
                        dve.wait_ge(gathered[w], (r + 1) * 16 * TILES)
                        nc.vector.tensor_tensor(logit[w][:, :, :], emb[w][:, :, HALF:DIM],
                                                c["cluster_b"][:, :].unsqueeze(1).to_broadcast([P, TILES, CLUSTERS]),
                                                ALU.add).then_inc(logit_biased, 1)
                    for w in range(WAYS):
                        dve.wait_ge(logit_biased, r * WAYS + w + 1)
                        nc.vector.tensor_reduce(neg_max[w][:, :], logit[w][:, :, :], AX.X, ALU.max,
                                                negate=True).then_inc(max_found, 1)
                    for w in range(WAYS):
                        dve.wait_ge(max_found, r * WAYS + w + 1)
                        nc.vector.tensor_tensor(logit[w][:, :, :], logit[w][:, :, :],
                                                neg_max[w][:, :].unsqueeze(2).to_broadcast([P, TILES, CLUSTERS]),
                                                ALU.add).then_inc(logit_shifted, 1)

                def exp_sums(r):
                    for w in range(WAYS):
                        dve.wait_ge(exp_done, r * WAYS + w + 1)
                        nc.vector.tensor_reduce(inv_sum[w][:, :], expo[w][:, :, :], AX.X, ALU.add).then_inc(sum_done, 1)
                    for w in range(WAYS):
                        dve.wait_ge(sum_done, r * WAYS + w + 1)
                        nc.vector.reciprocal(inv_sum[w][:, :], inv_sum[w][:, :]).then_inc(inv_done, 1)

                def coarse_half(r):
                    for w in range(WAYS):
                        n = r * WAYS + w + 1
                        dve.wait_ge(inv_done, n)
                        dve.wait_ge(coarse_done, n)
                        dve.wait_ge(h_stored[w], (r + 1) * 16)
                        nc.vector.tensor_tensor(h[w][:, :, HALF:DIM],
                                                psV[w][:, 0:TILES * HALF].rearrange("p (t n) -> p t n", t=TILES),
                                                inv_sum[w][:, :].unsqueeze(2).to_broadcast([P, TILES, HALF]),
                                                ALU.mult).then_inc(coarse_scaled, 1)

                def stats_front(r):
                    for w in range(WAYS):
                        dve.wait_ge(coarse_scaled, r * WAYS + w + 1)
                        dve.wait_ge(fine_copied, r * WAYS + w + 1)
                        for t in range(TILES):
                            last = nc.vector.bn_stats(stat[w][:, t, :], h[w][:, t, :])
                        last.then_inc(stats_done, 1)
                    for w in range(WAYS):
                        n = r * WAYS + w + 1
                        wait_apart(dve, stats_done, n)
                        for t in range(TILES):
                            last = nc.vector.bn_aggr(mv[w][:, t, :], stat[w][:, t, :])
                        last.then_inc(aggr_done, 1)
                        dve.wait_ge(aggr_done, n)
                        nc.vector.tensor_scalar(rs[w][:, :], mv[w][:, :, 1], 1.0 + EPS, EPS * EPS, ALU.mult,
                                                ALU.add).then_inc(both_var_done, 1)

                def norm_front(r):
                    for w in range(WAYS):
                        dve.wait_ge(rstd_done, r * WAYS + w + 1)
                        for t in range(TILES):
                            last = nc.vector.tensor_scalar(xn[w][:, t, :], h[w][:, t, :], mv[w][:, t, 0:1],
                                                           rs[w][:, t:t + 1], ALU.subtract, ALU.mult)
                        last.then_inc(xn_done, 1)

                def silu(r):
                    for w in range(WAYS):
                        dve.wait_ge(tanh_done, r * WAYS + w + 1)
                        nc.vector.scalar_tensor_tensor(out=sx[w][:, :, :], in0=sx[w][:, :, :], scalar=1.0,
                                                       in1=xn[w][:, :, :], op0=ALU.add, op1=ALU.mult).then_inc(silu_done, 1)

                def stats_back(r):
                    for w in range(WAYS):
                        dve.wait_ge(qk_copied, r * WAYS + w + 1)
                        for t in range(TILES):
                            for a in range(2):
                                last = nc.vector.bn_stats(stat2[w][:, 2 * t + a, :], qk[w][:, t, a, :])
                        last.then_inc(stats2_done, 1)

                def aggregate_back(r):
                    for w in range(WAYS):
                        n = r * WAYS + w + 1
                        wait_apart(dve, stats2_done, n)
                        for j in range(2 * TILES):
                            last = nc.vector.bn_aggr(mv2[w][:, j, :], stat2[w][:, j, :])
                        last.then_inc(means2_done, 1)
                        dve.wait_ge(means2_done, n)
                        nc.vector.tensor_scalar(rs3[w][:, :], mv2[w][:, :, 1], EPS, None, ALU.add).then_inc(aggr2_done, 1)

                def norm_back(r):
                    for w in range(WAYS):
                        dve.wait_ge(rstd2_done, r * WAYS + w + 1)
                        nc.vector.scalar_tensor_tensor(
                            out=k_offset[w][:, :], in0=mv2[w][:, :, 0].rearrange("p (t a) -> p t a", a=2)[:, :, 1], scalar=-1.0,
                            in1=rs3[w][:, :].rearrange("p (t a) -> p t a", a=2)[:, :, 1],
                            op0=ALU.mult, op1=ALU.mult).then_inc(k_offset_done, 1)
                        for t in range(TILES):
                            last = nc.vector.tensor_scalar(qk[w][:, t, 0, :], qk[w][:, t, 0, :], mv2[w][:, 2 * t, 0:1],
                                                           rs3[w][:, 2 * t:2 * t + 1], ALU.subtract, ALU.mult)
                        last.then_inc(q_normed, 1)

                def subtract_part1(r):
                    for w in range(WAYS):
                        dve.wait_ge(part1_done, r * WAYS + w + 1)
                        nc.vector.tensor_tensor(part[2][w][:, :, :], rest[w][:, :, :], part[1][w][:, :, :],
                                                ALU.subtract).then_inc(part2_done, 1)

                nc.vector.memset(stacks["ks"][DATA_ROWS:ROWS, :, :], 1.0).then_inc(stacks["cleared"], 1)
                nc.vector.memset(c["bias_parts"][:, :], 0.0).then_inc(bias_split, 1)
                nc.vector.tensor_copy(bias_part[0][:, :], c["bias"][:, :]).then_inc(bias_split, 1)
                dve.wait_ge(bias_split, 2)
                nc.vector.tensor_tensor(bias_rest[:, :], c["bias"][:, :], bias_part[0][:, :], ALU.subtract).then_inc(bias_split, 1)
                dve.wait_ge(bias_split, 3)
                nc.vector.tensor_copy(bias_part[1][:, :], bias_rest[:, :]).then_inc(bias_split, 1)
                dve.wait_ge(bias_split, 4)
                nc.vector.tensor_tensor(bias_part[2][:, :], bias_rest[:, :], bias_part[1][:, :], ALU.subtract).then_inc(bias_split, 1)
                dve.wait_ge(bias_split, 5)
                for n in range(PARTS):
                    row = slice(n * HP, n * HP + 1)
                    nc.vector.tensor_copy(c["bias_parts"][row, :], bias_part[n][row, :]).then_inc(bias_ready, 1)

                logits(0)
                exp_sums(0)
                coarse_half(0)
                stats_front(0)
                norm_front(0)
                silu(0)
                with dve.Fori(0, ITERS - 1) as it:
                    logits(it + 1)
                    stats_back(it)
                    exp_sums(it + 1)
                    aggregate_back(it)
                    coarse_half(it + 1)
                    norm_back(it)
                    stats_front(it + 1)
                    norm_front(it + 1)
                    silu(it + 1)
                    subtract_part1(it)
                stats_back(ITERS - 1)
                aggregate_back(ITERS - 1)
                norm_back(ITERS - 1)
                subtract_part1(ITERS - 1)

            @block.scalar
            def _(act):
                def copy_fine(r):
                    for w in range(WAYS):
                        act.wait_ge(gathered[w], (r + 1) * 16 * TILES)
                        act.wait_ge(h_stored[w], (r + 1) * 16)
                        nc.scalar.activation(h[w][:, :, 0:HALF], emb[w][:, :, 0:HALF], ACT.Copy).then_inc(fine_copied, 1)

                def exponentials(r):
                    for w in range(WAYS):
                        act.wait_ge(logit_shifted, r * WAYS + w + 1)
                        nc.scalar.activation(expo[w][:, :, :], logit[w][:, :, :], ACT.Exp).then_inc(exp_done, 1)

                def copy_exp_t(r):
                    for w in range(WAYS):
                        act.wait_ge(exp_t_done, r * WAYS + w + 1)
                        nc.scalar.activation(expo_t[w][:, :], psA[w][0:CLUSTERS, :], ACT.Copy).then_inc(exp_t_copied, 1)

                def tanh(r):
                    for w in range(WAYS):
                        act.wait_ge(xn_done, r * WAYS + w + 1)
                        nc.scalar.activation(sx[w][:, :, :], xn[w][:, :, :], ACT.Tanh, scale=0.5).then_inc(tanh_done, 1)

                def copy_silu_t(r):
                    for w in range(WAYS):
                        act.wait_ge(silu_t_done, r * WAYS + w + 1)
                        nc.scalar.activation(sx_t[w][:, :], psA[w][:, :], ACT.Copy, scale=0.5).then_inc(silu_t_copied, 1)

                def copy_projected(r, ways_now):
                    for w in ways_now:
                        n = r * WAYS + w + 1
                        act.wait_ge(qk_projected, n)
                        nc.scalar.activation(qk[w][:, :, :, :].rearrange("p t a n -> p (t a n)"),
                                             psQK[w][:, :, :].rearrange("p b n -> p (b n)"), ACT.Copy).then_inc(qk_copied, 1)
                        act.wait_ge(v_stored[w], (r + 1) * 16)
                        act.wait_ge(v_projected, n)
                        nc.scalar.activation(vrow[w][:, :, :, 0:HD],
                                             psV[w][:, :].rearrange("p (t h d) -> p t h d", t=TILES, h=HEADS),
                                             ACT.Copy).then_inc(v_copied, 1)

                def norm_k(r):
                    for w in range(WAYS):
                        act.wait_ge(k_offset_done, r * WAYS + w + 1)
                        for t in range(TILES):
                            last = nc.scalar.activation(qk[w][:, t, 1, :], qk[w][:, t, 1, :], ACT.Identity,
                                                        bias=k_offset[w][:, t:t + 1], scale=rs3[w][:, 2 * t + 1:2 * t + 2])
                        last.then_inc(k_normed, 1)

                def scale_qk(r):
                    for w in range(WAYS):
                        act.wait_ge(qk_t_done, r * WAYS + w + 1)
                        for a in range(2):
                            last = nc.scalar.activation(full[w][:, a, :], psQK[w][:, a, :], ACT.Identity,
                                                        bias=c["shift"][:, a:a + 1], scale=c["gain"][:, a:a + 1])
                        last.then_inc(qk_scaled, 1)
                        act.wait_ge(parts_stored[w], (r + 1) * 16 * PARTS)
                        act.wait_ge(qk_scaled, r * WAYS + w + 1 + SLOTS)
                        nc.scalar.activation(part[0][w][:, :, :], full[w][:, :, :], ACT.Copy).then_inc(part0_done, 1)

                def round_rest(r):
                    for w in range(WAYS):
                        act.wait_ge(rest1_done, r * WAYS + w + 1)
                        nc.scalar.activation(part[1][w][:, :, :], rest[w][:, :, :], ACT.Copy).then_inc(part1_done, 1)

                copy_fine(0)
                exponentials(0)
                copy_exp_t(0)
                tanh(0)
                with act.Fori(0, ITERS - 1) as it:
                    copy_silu_t(it)
                    copy_fine(it + 1)
                    exponentials(it + 1)
                    copy_projected(it, range(SLOTS))
                    copy_exp_t(it + 1)
                    copy_projected(it, range(SLOTS, WAYS))
                    norm_k(it)
                    scale_qk(it)
                    tanh(it + 1)
                    round_rest(it)
                copy_silu_t(ITERS - 1)
                copy_projected(ITERS - 1, range(WAYS))
                norm_k(ITERS - 1)
                scale_qk(ITERS - 1)
                round_rest(ITERS - 1)

            @block.tensor
            def _(pe):
                def transpose_exp(r, alone=False):
                    for w in range(WAYS):
                        if w >= SLOTS:
                            pe.wait_ge(exp_t_copied, r * WAYS + w + 1 - SLOTS)
                        elif not alone:
                            pe.wait_ge(silu_t_copied, (r - 1) * WAYS + w + 1 + SLOTS)
                        wait_apart(pe, exp_done, r * WAYS + w + 1)
                        for t in range(TILES):
                            last = nc.tensor.transpose(psA[w][0:CLUSTERS, t * P:(t + 1) * P], expo[w][:, t, :], c["ident"][:, :])
                        last.then_inc(exp_t_done, 1)

                def coarse(r, alone=False):
                    for w in range(WAYS):
                        pe.wait_ge(exp_t_copied, r * WAYS + w + 1)
                        if w >= SLOTS:
                            pe.wait_ge(coarse_scaled, r * WAYS + w + 1 - SLOTS)
                        elif not alone:
                            pe.wait_ge(v_copied, (r - 1) * WAYS + w + 1 + SLOTS)
                        for t in range(TILES):
                            last = nc.tensor.matmul(psV[w][:, t * HALF:(t + 1) * HALF], expo_t[w][:, t * P:(t + 1) * P],
                                                    c["coarse_w"][:, :], start=True, stop=True)
                        last.then_inc(coarse_done, 1)

                def transpose_silu(r):
                    for w in range(WAYS):
                        pe.wait_ge(silu_done, r * WAYS + w + 1)
                        if w >= SLOTS:
                            pe.wait_ge(silu_t_copied, r * WAYS + w + 1 - SLOTS)
                        for t in range(TILES):
                            last = nc.tensor.transpose(psA[w][:, t * P:(t + 1) * P], sx[w][:, t, :], c["ident"][:, :])
                        last.then_inc(silu_t_done, 1)

                def project(r, ways_now):
                    for w in ways_now:
                        if w >= SLOTS:
                            pe.wait_ge(qk_copied, r * WAYS + w + 1 - SLOTS)
                            pe.wait_ge(v_copied, r * WAYS + w + 1 - SLOTS)
                        else:
                            pe.wait_ge(qk_scaled, r * WAYS + w + 1)
                        for half in range(2):
                            add_bias(nc, c, psQK[w][:, half, :], 0, 2 * DIM)
                        add_bias(nc, c, psV[w][:, :], 2 * DIM, DIM)
                        pe.wait_ge(silu_t_copied, r * WAYS + w + 1)
                        for t in range(TILES):
                            last = nc.tensor.matmul(psQK[w][:, t // 2, (t % 2) * 2 * DIM:(t % 2 + 1) * 2 * DIM],
                                                    sx_t[w][:, t * P:(t + 1) * P], c["w_qkv"][:, 0:2 * DIM],
                                                    start=False, stop=t % 2 == 1)
                        last.then_inc(qk_projected, 1)
                        for t in range(TILES):
                            last = nc.tensor.matmul(psV[w][:, t * DIM:(t + 1) * DIM], sx_t[w][:, t * P:(t + 1) * P],
                                                    c["w_qkv"][:, 2 * DIM:], start=False, stop=t == TILES - 1)
                        last.then_inc(v_projected, 1)

                def transpose_qk(r):
                    for w in range(WAYS):
                        pe.wait_ge(q_normed, r * WAYS + w + 1)
                        pe.wait_ge(k_normed, r * WAYS + w + 1)
                        if w >= SLOTS:
                            pe.wait_ge(qk_scaled, r * WAYS + w + 1)
                        for a in range(2):
                            for t in range(TILES):
                                last = nc.tensor.transpose(psQK[w][:, a, t * P:(t + 1) * P], qk[w][:, t, a, :], c["ident"][:, :])
                        last.then_inc(qk_t_done, 1)

                pe.wait_ge(bias_ready, PARTS)
                transpose_exp(0, alone=True)
                coarse(0, alone=True)
                with pe.Fori(0, ITERS - 1) as it:
                    transpose_silu(it)
                    project(it, range(SLOTS))
                    transpose_exp(it + 1)
                    project(it, range(SLOTS, WAYS))
                    coarse(it + 1)
                    transpose_qk(it)
                transpose_silu(ITERS - 1)
                project(ITERS - 1, range(WAYS))
                transpose_qk(ITERS - 1)

            @block.sync
            def _(sp):
                def store_h(r):
                    for w in range(WAYS):
                        sp.wait_ge(coarse_scaled, r * WAYS + w + 1)
                        sp.wait_ge(fine_copied, r * WAYS + w + 1)
                        sp.dma_start(h_rows[r, w], h[w][:, :, :].rearrange("p t n -> p (t n)")).then_inc(h_stored[w], 16)

                def store_v(r):
                    for w in range(WAYS):
                        sp.wait_ge(v_copied, r * WAYS + w + 1)
                        at = w % PER_BATCH
                        sp.dma_start(v_rows[r * (WAYS // PER_BATCH) + w // PER_BATCH, :, at * TILES:(at + 1) * TILES, :],
                                     vrow[w][:, :, :, :].rearrange("p t h d -> p t (h d)")).then_inc(v_stored[w], 16)

                def store_parts(r):
                    for w in range(WAYS):
                        sp.wait_ge(part2_done, r * WAYS + w + 1)
                        for n in range(PARTS):
                            at = w % PER_BATCH
                            sp.dma_start(qk_parts[r * (WAYS // PER_BATCH) + w // PER_BATCH, :, n, :,
                                                  at * CHUNK:(at + 1) * CHUNK].rearrange("a p n -> p a n"),
                                         part[n][w][:, :, :]).then_inc(parts_stored[w], 16)

                store_h(0)
                with sp.Fori(0, ITERS - 1) as it:
                    store_v(it)
                    store_h(it + 1)
                    store_parts(it)
                for w in range(PER_BATCH):
                    sp.wait_ge(parts_stored[w], ITERS * 16 * PARTS)
                    sp.wait_ge(v_stored[w], ITERS * 16)
                load_stacks(sp, 0, qk_parts, v_rows, stacks["qs"], stacks["ks"], stacks["vs"], stacks["loaded"])
                store_v(ITERS - 1)
                store_parts(ITERS - 1)
                for w in range(WAYS):
                    sp.wait_ge(h_stored[w], (ITERS + 1) * 16)
                    sp.wait_ge(v_stored[w], (ITERS + 1) * 16)
                    sp.wait_ge(parts_stored[w], (ITERS + 1) * 16 * PARTS)


def load_stacks(sp, batch, qk_parts, v_rows, qs, ks, vs, loaded):
    for i, (qp, kp) in enumerate(zip(Q_TERMS, K_TERMS)):
        r = slice(i * HD, (i + 1) * HD)
        for half in range(HALVES):
            sp.dma_start(qs[r, half, :, :], qk_parts[batch, 0, qp].rearrange("(h d) (s n) -> d s h n", d=HD, s=HALVES)[:, half]).then_inc(
                loaded, 16)
        sp.dma_start(ks[r, :, :], qk_parts[batch, 1, kp].rearrange("(h d) n -> d h n", d=HD)).then_inc(loaded, 16)
    sp.dma_start(vs[:, :, :, :].rearrange("p t h d -> p t (h d)"), v_rows[batch]).then_inc(loaded, 16)


def attend(nc, qk_parts, v_rows, o_cols, inv_l, stacks):
    STEPS = HALVES * TOKT
    PAIR = 2 * GROUPS * STEPS
    PAIRS = BATCH // 2
    LEAD = TOKT + 5
    SRING, MRING, PRING = 3, 2, 4
    HTILES = TOKT // HALVES
    MAXES = GH * HTILES
    M_STEP = MAXES // TOKT
    SETS = 2 * GROUPS * HALVES
    PLACES = PARTS * (P // HP)
    LOADS = (HALVES + 1) * len(Q_TERMS) + 1

    ctx = ExitStack()
    with ctx:
        def sb(name, shape, dt=F32):
            return ctx.enter_context(nc.sbuf_tensor(name, shape, dt))

        def ps(name, shape):
            return ctx.enter_context(nc.psum_tensor(name, shape, F32))

        def sem(name):
            return ctx.enter_context(nc.semaphore("b_" + name))

        qs = [stacks["qs"], sb("qs1", [ROWS, HALVES, HEADS, BANK], BF16)]
        ks = [stacks["ks"], sb("ks1", [ROWS, HEADS, SEQ], BF16)]
        vs = [stacks["vs"], sb("vs1", [P, TOKT, HEADS, VW])]
        prob = [sb(f"prob{i}", [P, GH, BANK]) for i in range(PRING)]
        neg_max = [sb(f"b_neg_max{i}", [P, MAXES]) for i in range(2)]
        mrest = [sb(f"mrest{i}", [P, MAXES]) for i in range(2)]
        mpart = [sb(f"mpart{i}", [P, PARTS + 1, MAXES], BF16) for i in range(2)]
        mpart_t = [sb(f"mpart_t{i}", [P, (PARTS + 1) * MAXES // HP, HP], BF16) for i in range(2)]
        ot = [sb(f"ot{i}", [P, BANK]) for i in range(2)]
        early_rows = (BATCH - 2) * HEADS
        sums = sb("early_sums", [early_rows * HALVES, BANK])
        psS = [ps(f"psS{i}", [P, BANK]) for i in range(SRING)]
        psM = [ps(f"psM{i}", [P, HALVES, BANK]) for i in range(MRING)]
        psO = ps("psO", [P, BANK])

        loaded = [stacks["loaded"], sem("loaded1")]
        cleared = [stacks["cleared"], sem("cleared1")]
        out_cleared = sem("out_cleared")
        scored = sem("scored")
        score_free = sem("score_free")
        prob_free = sem("prob_free")
        max_scored = sem("max_scored")
        max_free = sem("max_free")
        split = sem("split")
        max_t_done = sem("max_t_done")
        max_loaded = [sem(f"max_loaded{i}") for i in range(2)]
        out_free = sem("out_free")
        o_stored = [sem(f"o_stored{i}") for i in range(2)]
        SPLITS = 4
        sums_loaded = sem("sums_loaded")
        sums_inverted = sem("sums_inverted")
        inv_stored = sem("inv_stored")

        with nc.Block() as block:
            @block.sync
            def _(sp):
                preset(sp, score_free, 1)
                preset(sp, prob_free, PRING)
                preset(sp, max_free, MRING)
                preset(sp, out_free, 1)
                for i in range(2):
                    preset(sp, o_stored[i], 16)

            @block.vector
            def _(dve):
                nc.vector.memset(psO[:, :], 0.0).then_inc(out_cleared, 1)
                for i in range(2):
                    nc.vector.memset(mpart[i][:, PARTS, :], 0.0)

        def load(sp, batch, buf):
            load_stacks(sp, batch, qk_parts, v_rows, qs[buf], ks[buf], vs[buf], loaded[buf])

        def place(step):
            g = step // STEPS
            return g, (g // GROUPS) % 2, g % GROUPS, step % STEPS // TOKT, step % TOKT

        with nc.Block() as block:
            @block.gpsimd
            def _(pool):
                nc.gpsimd.memset(ks[1][DATA_ROWS:ROWS, :, :], 1.0).then_inc(cleared[1], 1)

            @block.sync
            def _(sp):
                def place_maxima(p, e):
                    buf, gb, half = e // (GROUPS * HALVES) % 2, e // HALVES % GROUPS, e % HALVES
                    sp.wait_ge(max_t_done, p * SETS + e + 1)
                    for a in range(P // HP):
                        for n in range(PARTS):
                            dst = qs[buf][DATA_ROWS + n:DATA_ROWS + n + 1, half, GH * gb:GH * (gb + 1), :]
                            dst = dst.rearrange("o h (t a r) -> o a (h t) r", a=P // HP, r=HP)[:, a, :, :]
                            row = a * HP + n * MAXES % HP
                            sp.dma_start(dst, mpart_t[e % 2][row:row + MAXES, n * MAXES // HP, :]).then_inc(max_loaded[e % 2], 16)

                def store(p, half):
                    sp.wait_ge(out_free, p * (PAIR // TOKT) + half + 2)
                    sp.dma_start(o_cols[2 * p + half // 4, half // 2 % 2, :, half % 2 * BANK:(half % 2 + 1) * BANK],
                                 ot[half % 2][:, :]).then_inc(o_stored[half % 2], 16)

                def load_next(p, buf, last):
                    if buf == 1 or not last:
                        sp.wait_ge(prob_free, p * PAIR + (PAIR // 2 if buf == 0 else 0) + PRING)
                        load(sp, 2 * p + 2 - buf, buf)
                    if buf == 1 and last:
                        for i in range(2):
                            sp.wait_ge(o_stored[i], 16 + 16 * (BATCH - 2) * GROUPS)
                        sp.dma_start(sums[:, :], in_pieces(by_head(o_cols)[0:early_rows, HD, :], BANK)).then_inc(sums_loaded, 16)
                    if buf == 0 and last:
                        sp.wait_ge(sums_inverted, 1)
                        sp.dma_start(in_pieces(inv_l[0:early_rows, :], BANK), sums[:, :]).then_inc(inv_stored, 16)

                def pair(p, last):
                    for e in range(SETS):
                        if not (last and e == SETS - 1):
                            place_maxima(p, e + 1)
                        if e % (SETS // 2) == 0:
                            load_next(p, 0 if e else 1, last)
                        store(p, e)

                place_maxima(0, 0)
                with sp.Fori(0, PAIRS - 1) as p:
                    pair(p, False)
                pair(PAIRS - 1, True)
                for i in range(2):
                    sp.wait_ge(o_stored[i], 16 + 16 * BATCH * GROUPS)
                sp.wait_ge(inv_stored, 16)

            @block.tensor
            def _(pe):
                def find_max(p, step):
                    g, buf, gb, half, _ = place(step)
                    if step % (GROUPS * STEPS) == 0:
                        pe.wait_ge(loaded[buf], (p + 1 + step // PAIR) * 16 * LOADS)
                    for m in range(M_STEP):
                        unit = step % TOKT * M_STEP + m
                        hh = GH * gb + unit // HTILES
                        count = step * M_STEP + m
                        pe.wait_ge(max_free, p * PAIR * M_STEP + count + 1)
                        for kh in range(HALVES):
                            last_mm = nc.tensor.matmul(psM[count % MRING][:, kh, :],
                                                       qs[buf][0:DATA_ROWS, half, hh, unit % HTILES * P:(unit % HTILES + 1) * P],
                                                       ks[buf][0:DATA_ROWS, hh, kh * BANK:(kh + 1) * BANK],
                                                       start=True, stop=True)
                        last_mm.then_inc(max_scored, 1)
                        yield

                def score(p, step, heads):
                    g, buf, gb, half, tile = place(step)
                    if step % TOKT == 0 and heads[0] == 0:
                        e = step // TOKT
                        if e % (SETS // 2) == 0:
                            pe.wait_ge(cleared[buf], 1)
                        pe.wait_ge(max_loaded[e % 2], (p * (SETS // 2) + e // 2 + 1) * 16 * PLACES)
                    for hh in heads:
                        unit = step * GH + hh
                        pe.wait_ge(score_free, p * PAIR * GH + 1 + max(unit - SRING + 1, 0))
                        nc.tensor.matmul(psS[unit % SRING][:, :],
                                         ks[buf][0:ROWS, GH * gb + hh, tile * P:(tile + 1) * P],
                                         qs[buf][0:ROWS, half, GH * gb + hh, :],
                                         start=True, stop=True).then_inc(scored, 1)

                def add_values(p, step):
                    g, buf, gb, _, tile = place(step)
                    pe.wait_ge(score_free, p * PAIR * GH + (step + 1) * GH + 1)
                    if tile == 0:
                        pe.wait_ge(out_free, p * (PAIR // TOKT) + step // TOKT + 1)
                    for hh in range(GH):
                        last_mm = nc.tensor.matmul(psO[HP * hh:HP * hh + VW, :], vs[buf][:, tile, GH * gb + hh, :],
                                                   prob[step % PRING][:, hh, :], start=tile == 0, stop=tile == TOKT - 1)
                    last_mm.then_inc(prob_free, 1)

                def pair(p, last):
                    for step in range(PAIR):
                        ahead = step + LEAD
                        units = find_max(p, ahead) if not (last and ahead >= PAIR) else iter(())
                        score(p, step, (0, 1))
                        next(units, None)
                        score(p, step, (2, 3))
                        next(units, None)
                        if step:
                            add_values(p, step - 1)
                    add_values(p, PAIR - 1)

                pe.wait_ge(out_cleared, 1)
                for step in range(LEAD):
                    for _ in find_max(0, step):
                        pass
                with pe.Fori(0, PAIRS - 1) as p:
                    pair(p, False)
                pair(PAIRS - 1, True)

            @block.scalar
            def _(act):
                def pair(p):
                    for step in range(PAIR):
                        act.wait_ge(prob_free, p * PAIR + step + 1)
                        for hh in range(GH):
                            unit = step * GH + hh
                            act.wait_ge(scored, p * PAIR * GH + unit + 1)
                            nc.scalar.activation(prob[step % PRING][:, hh, :], psS[unit % SRING][:, :],
                                                 ACT.Exp).then_inc(score_free, 1)

                with act.Fori(0, PAIRS) as p:
                    pair(p)

            @block.vector
            def _(dve):
                def find_max(p, step):
                    e = step // TOKT
                    for m in range(M_STEP):
                        unit = step % TOKT * M_STEP + m
                        count = step * M_STEP + m
                        dve.wait_ge(max_scored, p * PAIR * M_STEP + count + 1)
                        nc.vector.tensor_reduce(neg_max[e % 2][:, unit:unit + 1], psM[count % MRING][:, :, :],
                                                AX.XY, ALU.max, negate=True).then_inc(max_free, 1)
                    if step % TOKT == TOKT - 1:
                        i, k = e % 2, (p * SETS + e) * SPLITS
                        dve.wait_ge(max_free, p * PAIR * M_STEP + (step + 1) * M_STEP + MRING)
                        nc.vector.tensor_copy(mpart[i][:, 0, :], neg_max[i][:, :]).then_inc(split, 1)
                        dve.wait_ge(split, k + 1)
                        nc.vector.tensor_tensor(mrest[i][:, :], neg_max[i][:, :], mpart[i][:, 0, :], ALU.subtract).then_inc(split, 1)
                        dve.wait_ge(split, k + 2)
                        nc.vector.tensor_copy(mpart[i][:, 1, :], mrest[i][:, :]).then_inc(split, 1)
                        dve.wait_ge(split, k + 3)
                        nc.vector.tensor_tensor(mpart[i][:, 2, :], mrest[i][:, :], mpart[i][:, 1, :], ALU.subtract).then_inc(split, 1)
                        dve.wait_ge(split, k + 4)
                        nc.vector.transpose(mpart_t[i][:, :, :].rearrange("p b r -> p (b r)"),
                                            mpart[i][:, :, :].rearrange("p n m -> p (n m)")).then_inc(max_t_done, 1)

                def copy_out(p, half):
                    dve.wait_ge(prob_free, p * PAIR + (half + 1) * TOKT + PRING)
                    dve.wait_ge(o_stored[half % 2], (p * (PAIR // TOKT // 2) + half // 2 + 1) * 16)
                    nc.vector.tensor_copy(ot[half % 2][:, :], psO[:, :]).then_inc(out_free, 1)

                def pair(p, last):
                    for step in range(PAIR):
                        ahead = step + LEAD
                        if not (last and ahead >= PAIR):
                            find_max(p, ahead)
                        if last and step == 2 * TOKT:
                            dve.wait_ge(sums_loaded, 16)
                            nc.vector.reciprocal(sums[:, :], sums[:, :]).then_inc(sums_inverted, 1)
                        if step and step % TOKT == 0:
                            copy_out(p, step // TOKT - 1)
                    copy_out(p, PAIR // TOKT - 1)

                for step in range(LEAD):
                    find_max(0, step)
                with dve.Fori(0, PAIRS - 1) as p:
                    pair(p, False)
                pair(PAIRS - 1, True)


def finish(nc, c, h_rows, o_cols, inv_l, out):
    ctx = ExitStack()
    with ctx:
        def ways(name, shape, dt=F32):
            return [ctx.enter_context(nc.sbuf_tensor(f"{name}{w}", shape, dt)) for w in range(WAYS)]

        def sem(name):
            return ctx.enter_context(nc.semaphore("c_" + name))

        def way_sems(name):
            return [sem(f"{name}{w}") for w in range(WAYS)]

        late_rows = 2 * HEADS
        piece = late_rows * SEQ // P
        sums = ctx.enter_context(nc.sbuf_tensor("late_sums", [P, piece], F32))
        o_in = ways("o_in", [P, CHUNK])
        inv_in = ways("inv_in", [P, CHUNK])
        h_in = ways("h_in", [P, TILES, DIM])
        half_o = ways("half_o", [P, CHUNK])
        so = ways("so", [P, CHUNK])
        h2 = ways("h2_", [P, TILES, DIM])
        h2_kept = ways("h2_kept", [P, TILES, DIM])
        stat = ways("c_stat", [P, TILES, 6])
        mv = ways("c_mv", [P, TILES, 2])
        var_eps = ways("c_var_eps", [P, TILES])
        rstd = ways("c_rstd", [P, TILES])
        y = ways("y", [P, TILES, DIM])
        y_t = ways("y_t", [P, CHUNK])
        neg_max = ways("c_neg_max", [P, TILES])
        logit = ways("c_logit", [P, TILES, EXPERTS])
        prob = ways("c_prob", [P, TILES, EXPERTS])
        inv_sum = ways("c_inv_sum", [P, TILES])
        top = ways("top", [P, TILES, 8])
        top_i = ways("top_i", [P, TILES, 8], U32)
        top_f = ways("top_f", [P, TILES, 2])
        first = ways("first", [P, TILES, EXPERTS])
        second = ways("second", [P, TILES, EXPERTS])
        chosen = ways("chosen", [P, TILES, EXPERTS], BF16)
        before = ways("before", [P, TILES, EXPERTS])
        gate = ways("gate", [P, TILES])
        hid = ways("hid", [P, FK, CHUNK])
        res = ways("res", [P, TILES, DIM])
        psT = [ctx.enter_context(nc.psum_tensor(f"c_psT{i}", [P, 2, BANK], F32)) for i in range(SLOTS)] * (WAYS // SLOTS)
        psR = [ctx.enter_context(nc.psum_tensor(f"c_psR{i}", [P, 2, TILES * EXPERTS], F32)) for i in range(SLOTS)] * (WAYS // SLOTS)
        psF = [ctx.enter_context(nc.psum_tensor(f"c_psF{i}", [P, BANK], F32)) for i in range(SLOTS)] * (WAYS // SLOTS)

        o_loaded = way_sems("o_loaded")
        h_loaded = way_sems("h_loaded")
        sums_loaded = sem("sums_loaded")
        sums_inverted = sem("sums_inverted")
        inv_stored = sem("inv_stored")
        o_done = sem("o_done")
        tanh_done = sem("tanh_done")
        silu_done = sem("silu_done")
        projected = sem("projected")
        h2_done = sem("h2_done")
        h2_copied = sem("h2_copied")
        stats_done = sem("stats_done")
        aggr_done = sem("aggr_done")
        eps_done = sem("eps_done")
        rstd_done = sem("rstd_done")
        y_done = sem("y_done")
        y_t_done = sem("y_t_done")
        y_t_copied = sem("y_t_copied")
        routed = sem("routed")
        max_found = sem("max_found")
        logit_shifted = sem("logit_shifted")
        exp_done = sem("exp_done")
        sum_done = sem("sum_done")
        inv_sum_done = sem("inv_sum_done")
        prob_done = sem("prob_done")
        top_done = sem("top_done")
        index_done = sem("index_done")
        index_cast = sem("index_cast")
        hot_done = sem("hot_done")
        chosen_done = sem("chosen_done")
        counted = sem("counted")
        before_done = sem("before_done")
        carried = sem("carried")
        kept_done = sem("kept_done")
        kept_prob_done = sem("kept_prob_done")
        gate_done = sem("gate_done")
        up_done = sem("up_done")
        gelu_done = sem("gelu_done")
        down_done = sem("down_done")
        res_done = sem("res_done")
        res_stored = way_sems("res_stored")
        RES_PRESET = 2 * WAYS

        with nc.Block() as block:
            @block.sync
            def _(sp):
                preset(sp, o_done, WAYS)
                preset(sp, h2_done, WAYS)
                preset(sp, h2_copied, WAYS)
                preset(sp, res_done, RES_PRESET)
                preset(sp, carried, 1)
                for w in range(WAYS):
                    preset(sp, res_stored[w], 16)

        def count_chosen(pe, it, w):
            pe.wait_ge(chosen_done, it * WAYS + w + 1)
            if w >= SLOTS:
                pe.wait_ge(carried, it * WAYS + w + 2 - SLOTS)
            for t in range(TILES):
                dst = psR[w][:, 1, t * EXPERTS:(t + 1) * EXPERTS]
                for u in range(t):
                    nc.tensor.matmul(dst, c["ones"][:, :], chosen[w][:, u, :], start=u == 0, stop=False)
                nc.tensor.matmul(dst, c["later"][:, :], chosen[w][:, t, :], start=t == 0, stop=True)
            for u in range(TILES):
                last = nc.tensor.matmul(psR[w][:, 0, 0:EXPERTS], c["ones"][:, :], chosen[w][:, u, :],
                                        start=u == 0, stop=u == TILES - 1)
            last.then_inc(counted, 1)

        with nc.Block() as block:
            @block.sync
            def _(sp):
                with sp.Fori(0, ITERS) as it:
                    for w in range(WAYS):
                        n = it * WAYS + w + 1
                        sp.wait_ge(o_done, n)
                        heads = bass.ds((it * (WAYS // PER_BATCH) + w // PER_BATCH) * HEADS, HEADS)
                        tokens = slice(w % PER_BATCH * CHUNK, (w % PER_BATCH + 1) * CHUNK)
                        sp.dma_start(o_in[w][:, :], by_head(o_cols)[heads, 0:HD, tokens]).then_inc(o_loaded[w], 16)
                        sp.dma_start(inv_in[w][:, :], inv_l[heads, tokens].unsqueeze(1).to_broadcast([HEADS, HD, CHUNK])).then_inc(
                            o_loaded[w], 16)
                        sp.wait_ge(h2_done, n)
                        sp.dma_start(h_in[w][:, :, :].rearrange("p t n -> p (t n)"), h_rows[it, w]).then_inc(h_loaded[w], 16)
                    sp.wait_ge(inv_stored, 16)

            @block.gpsimd
            def _(pool):
                def root(r):
                    for w in range(WAYS):
                        pool.wait_ge(eps_done, r * WAYS + w + 1)
                        nc.gpsimd.tensor_tensor(rstd[w][:, :], var_eps[w][:, :], c["neg_half"][:, 0:TILES], ALU.pow).then_inc(rstd_done, 1)

                def keep_h2(r):
                    for w in range(WAYS):
                        pool.wait_ge(res_done, (r - 1) * WAYS + w + 1 + RES_PRESET)
                        wait_apart(pool, h2_done, r * WAYS + w + 1 + WAYS)
                        nc.gpsimd.tensor_copy(h2_kept[w][:, :, :], h2[w][:, :, :]).then_inc(h2_copied, 1)

                root(0)
                keep_h2(0)
                with pool.Fori(0, ITERS - 1) as it:
                    root(it + 1)
                    keep_h2(it + 1)

            @block.scalar
            def _(act):
                def tanh(r):
                    for w in range(WAYS):
                        act.wait_ge(o_done, r * WAYS + w + 1 + WAYS)
                        nc.scalar.activation(so[w][:, :], half_o[w][:, :], ACT.Tanh).then_inc(tanh_done, 1)

                def copy_y_t(r):
                    for w in range(WAYS):
                        act.wait_ge(y_t_done, r * WAYS + w + 1)
                        nc.scalar.activation(y_t[w][:, :], psT[w][:, 0, :], ACT.Copy).then_inc(y_t_copied, 1)

                def exponentials(r):
                    for w in range(WAYS):
                        act.wait_ge(logit_shifted, r * WAYS + w + 1)
                        nc.scalar.activation(prob[w][:, :, :], logit[w][:, :, :], ACT.Exp).then_inc(exp_done, 1)

                def gelu(r):
                    for w in range(WAYS):
                        for k in range(FK):
                            act.wait_ge(up_done, (r * WAYS + w) * FK + k + 1)
                            src = psF[w][:, :] if k % 2 == 0 else psT[w][:, 0, :]
                            nc.scalar.activation(hid[w][:, k, :], src, ACT.Gelu, bias=c["b1"][:, k:k + 1]).then_inc(gelu_done, 1)

                def store(r):
                    for w in range(WAYS):
                        act.wait_ge(res_done, r * WAYS + w + 1 + RES_PRESET)
                        at = w % PER_BATCH
                        act.dma_start(out[r * (WAYS // PER_BATCH) + w // PER_BATCH, :, at * TILES:(at + 1) * TILES, :],
                                      res[w][:, :, :]).then_inc(res_stored[w], 16)

                act.dma_start(sums[:, :], in_pieces(by_head(o_cols)[BATCH * HEADS - late_rows:, HD, :], piece)).then_inc(sums_loaded, 16)
                act.wait_ge(sums_inverted, 1)
                act.dma_start(in_pieces(inv_l[BATCH * HEADS - late_rows:, :], piece), sums[:, :]).then_inc(inv_stored, 16)
                tanh(0)
                copy_y_t(0)
                exponentials(0)
                with act.Fori(0, ITERS - 1) as it:
                    tanh(it + 1)
                    gelu(it)
                    copy_y_t(it + 1)
                    exponentials(it + 1)
                    store(it)
                gelu(ITERS - 1)
                store(ITERS - 1)
                for w in range(WAYS):
                    act.wait_ge(res_stored[w], (ITERS + 1) * 16)

            @block.tensor
            def _(pe):
                def project(r):
                    for w in range(WAYS):
                        if w >= SLOTS:
                            pe.wait_ge(h2_done, r * WAYS + w + 1 + WAYS - SLOTS)
                        else:
                            pe.wait_ge(res_done, (r - 2) * WAYS + w + 1 + SLOTS + RES_PRESET)
                        add_bias(nc, c, psT[w][:, 1, :], 3 * DIM, DIM)
                        pe.wait_ge(silu_done, r * WAYS + w + 1)
                        for t in range(TILES):
                            last = nc.tensor.matmul(psT[w][:, 1, t * DIM:(t + 1) * DIM], so[w][:, t * P:(t + 1) * P],
                                                    c["w_o"][:, :], start=False, stop=t == TILES - 1)
                        last.then_inc(projected, 1)

                def transpose_y(r, alone=False):
                    for w in range(WAYS):
                        if w >= SLOTS:
                            pe.wait_ge(y_t_copied, r * WAYS + w + 1 - SLOTS)
                        elif not alone:
                            pe.wait_ge(gelu_done, ((r - 1) * WAYS + w + 1 + SLOTS) * FK)
                        pe.wait_ge(y_done, r * WAYS + w + 1)
                        for t in range(TILES):
                            last = nc.tensor.transpose(psT[w][:, 0, t * P:(t + 1) * P], y[w][:, t, :], c["ident"][:, :])
                        last.then_inc(y_t_done, 1)

                def route(r):
                    for w in range(WAYS):
                        pe.wait_ge(y_t_copied, r * WAYS + w + 1)
                        if w >= SLOTS:
                            pe.wait_ge(logit_shifted, r * WAYS + w + 1 - SLOTS)
                        for t in range(TILES):
                            last = nc.tensor.matmul(psR[w][:, 0, t * EXPERTS:(t + 1) * EXPERTS], y_t[w][:, t * P:(t + 1) * P],
                                                    c["router"][:, :], start=True, stop=True)
                        last.then_inc(routed, 1)

                def up(r, ways_now):
                    for w in ways_now:
                        for k in range(FK):
                            if k >= 2:
                                pe.wait_ge(gelu_done, (r * WAYS + w) * FK + k - 1)
                            elif w >= SLOTS:
                                pe.wait_ge(gelu_done, (r * WAYS + w - SLOTS) * FK + k + 3)
                            dst = psF[w][:, :] if k % 2 == 0 else psT[w][:, 0, :]
                            nc.tensor.matmul(dst, c["w1"][:, k * P:(k + 1) * P], y_t[w][:, :], start=True, stop=True).then_inc(up_done, 1)

                def down(r):
                    for w in range(WAYS):
                        if w >= SLOTS:
                            pe.wait_ge(res_done, r * WAYS + w + 1 - SLOTS + RES_PRESET)
                        add_bias(nc, c, psT[w][:, 1, :], 4 * DIM, DIM)
                        pe.wait_ge(gelu_done, (r * WAYS + w + 1) * FK)
                        for t in range(TILES):
                            for k in range(FK):
                                last = nc.tensor.matmul(psT[w][:, 1, t * DIM:(t + 1) * DIM], hid[w][:, k, t * P:(t + 1) * P],
                                                        c["w2"][:, k, :], start=False,
                                                        stop=t == TILES - 1 and k == FK - 1)
                        last.then_inc(down_done, 1)

                def count(r, ways_now):
                    for w in ways_now:
                        count_chosen(pe, r, w)

                project(0)
                transpose_y(0, alone=True)
                route(0)
                with pe.Fori(0, ITERS - 1) as it:
                    count(it, range(SLOTS))
                    up(it, range(1))
                    project(it + 1)
                    count(it, range(SLOTS, WAYS))
                    up(it, range(1, WAYS))
                    transpose_y(it + 1)
                    route(it + 1)
                    down(it)
                count(ITERS - 1, range(WAYS))
                up(ITERS - 1, range(WAYS))
                down(ITERS - 1)

            @block.vector
            def _(dve):
                def divide(r):
                    for w in range(WAYS):
                        dve.wait_ge(o_loaded[w], (r + 1) * 32)
                        nc.vector.scalar_tensor_tensor(out=half_o[w][:, :], in0=o_in[w][:, :], scalar=0.5, in1=inv_in[w][:, :],
                                                       op0=ALU.mult, op1=ALU.mult).then_inc(o_done, 1)

                def silu(r):
                    for w in range(WAYS):
                        dve.wait_ge(tanh_done, r * WAYS + w + 1)
                        nc.vector.scalar_tensor_tensor(out=so[w][:, :], in0=so[w][:, :], scalar=1.0, in1=half_o[w][:, :],
                                                       op0=ALU.add, op1=ALU.mult).then_inc(silu_done, 1)

                def residual(r):
                    for w in range(WAYS):
                        n = r * WAYS + w + 1
                        dve.wait_ge(projected, n)
                        dve.wait_ge(h_loaded[w], (r + 1) * 16)
                        dve.wait_ge(h2_copied, n)
                        nc.vector.tensor_tensor(h2[w][:, :, :], psT[w][:, 1, :].rearrange("p (t n) -> p t n", t=TILES),
                                                h_in[w][:, :, :], ALU.add).then_inc(h2_done, 1)

                def statistics(r):
                    for w in range(WAYS):
                        dve.wait_ge(h2_done, r * WAYS + w + 1 + WAYS)
                        for t in range(TILES):
                            last = nc.vector.bn_stats(stat[w][:, t, :], h2[w][:, t, :])
                        last.then_inc(stats_done, 1)
                    for w in range(WAYS):
                        n = r * WAYS + w + 1
                        wait_apart(dve, stats_done, n)
                        for t in range(TILES):
                            last = nc.vector.bn_aggr(mv[w][:, t, :], stat[w][:, t, :])
                        last.then_inc(aggr_done, 1)
                        dve.wait_ge(aggr_done, n)
                        nc.vector.tensor_scalar(var_eps[w][:, :], mv[w][:, :, 1], EPS, None, ALU.add).then_inc(eps_done, 1)

                def norm(r):
                    for w in range(WAYS):
                        dve.wait_ge(rstd_done, r * WAYS + w + 1)
                        for t in range(TILES):
                            last = nc.vector.tensor_scalar(y[w][:, t, :], h2[w][:, t, :], mv[w][:, t, 0:1],
                                                           rstd[w][:, t:t + 1], ALU.subtract, ALU.mult)
                        last.then_inc(y_done, 1)

                def softmax(r):
                    for w in range(WAYS):
                        n = r * WAYS + w + 1
                        scores = psR[w][:, 0, :].rearrange("p (t e) -> p t e", t=TILES)
                        dve.wait_ge(routed, n)
                        nc.vector.tensor_reduce(neg_max[w][:, :], scores, AX.X, ALU.max, negate=True).then_inc(max_found, 1)
                        dve.wait_ge(max_found, n)
                        nc.vector.tensor_tensor(logit[w][:, :, :], scores,
                                                neg_max[w][:, :].unsqueeze(2).to_broadcast([P, TILES, EXPERTS]),
                                                ALU.add).then_inc(logit_shifted, 1)
                    for w in range(WAYS):
                        n = r * WAYS + w + 1
                        dve.wait_ge(exp_done, n)
                        nc.vector.tensor_reduce(inv_sum[w][:, :], prob[w][:, :, :], AX.X, ALU.add).then_inc(sum_done, 1)
                        dve.wait_ge(sum_done, n)
                        nc.vector.reciprocal(inv_sum[w][:, :], inv_sum[w][:, :]).then_inc(inv_sum_done, 1)
                        dve.wait_ge(inv_sum_done, n)
                        nc.vector.tensor_tensor(prob[w][:, :, :], prob[w][:, :, :],
                                                inv_sum[w][:, :].unsqueeze(2).to_broadcast([P, TILES, EXPERTS]),
                                                ALU.mult).then_inc(prob_done, 1)

                def choose(r):
                    for w in range(WAYS):
                        n = r * WAYS + w + 1
                        wait_apart(dve, prob_done, n)
                        for t in range(TILES):
                            last = nc.vector.max(top[w][:, t, :], prob[w][:, t, :])
                        last.then_inc(top_done, 1)
                    for w in range(WAYS):
                        n = r * WAYS + w + 1
                        wait_apart(dve, top_done, n)
                        for t in range(TILES):
                            last = nc.vector.max_index(top_i[w][:, t, :], top[w][:, t, :], prob[w][:, t, :])
                        last.then_inc(index_done, 1)
                    for w in range(WAYS):
                        n = r * WAYS + w + 1
                        dve.wait_ge(index_done, n)
                        nc.vector.tensor_copy(top_f[w][:, :, :], top_i[w][:, :, 0:2]).then_inc(index_cast, 1)
                    for w in range(WAYS):
                        n = r * WAYS + w + 1
                        dve.wait_ge(index_cast, n)
                        ids = c["expert_ids"][:, :].unsqueeze(1).to_broadcast([P, TILES, EXPERTS])
                        for j, hot in enumerate((first, second)):
                            last = nc.vector.tensor_tensor(hot[w][:, :, :], ids,
                                                           top_f[w][:, :, j:j + 1].to_broadcast([P, TILES, EXPERTS]),
                                                           ALU.is_equal)
                        last.then_inc(hot_done, 1)
                    for w in range(WAYS):
                        dve.wait_ge(hot_done, r * WAYS + w + 1)
                        nc.vector.tensor_tensor(chosen[w][:, :, :], first[w][:, :, :], second[w][:, :, :],
                                                ALU.add).then_inc(chosen_done, 1)

                def weigh(r, ways_now):
                    for w in ways_now:
                        n = r * WAYS + w + 1
                        dve.wait_ge(counted, n)
                        dve.wait_ge(carried, n)
                        nc.vector.tensor_tensor(before[w][:, :, :],
                                                psR[w][:, 1, :].rearrange("p (t e) -> p t e", t=TILES),
                                                c["carry"][:, :].unsqueeze(1).to_broadcast([P, TILES, EXPERTS]),
                                                ALU.add).then_inc(before_done, 1)
                        dve.wait_ge(before_done, n)
                        nc.vector.tensor_tensor(c["carry"][:, :], psR[w][:, 0, 0:EXPERTS], c["carry"][:, :],
                                                ALU.add).then_inc(carried, 1)
                        nc.vector.scalar_tensor_tensor(out=before[w][:, :, :], in0=before[w][:, :, :], scalar=float(CAP),
                                                       in1=chosen[w][:, :, :], op0=ALU.is_lt, op1=ALU.mult).then_inc(kept_done, 1)
                        dve.wait_ge(kept_done, n)
                        nc.vector.tensor_tensor(before[w][:, :, :], before[w][:, :, :], prob[w][:, :, :],
                                                ALU.mult).then_inc(kept_prob_done, 1)
                        dve.wait_ge(kept_prob_done, n)
                        nc.vector.tensor_reduce(gate[w][:, :], before[w][:, :, :], AX.X, ALU.add).then_inc(gate_done, 1)

                def result(r, ways_now):
                    for w in ways_now:
                        n = r * WAYS + w + 1
                        dve.wait_ge(gate_done, n)
                        dve.wait_ge(down_done, n)
                        dve.wait_ge(h2_copied, n + WAYS)
                        dve.wait_ge(res_stored[w], (r + 1) * 16)
                        for t in range(TILES):
                            last = nc.vector.scalar_tensor_tensor(out=res[w][:, t, :], in0=psT[w][:, 1, t * DIM:(t + 1) * DIM],
                                                                  scalar=gate[w][:, t:t + 1], in1=h2_kept[w][:, t, :],
                                                                  op0=ALU.mult, op1=ALU.add)
                        last.then_inc(res_done, 1)

                dve.wait_ge(sums_loaded, 16)
                nc.vector.reciprocal(sums[:, :], sums[:, :]).then_inc(sums_inverted, 1)
                divide(0)
                silu(0)
                residual(0)
                statistics(0)
                norm(0)
                softmax(0)
                choose(0)
                with dve.Fori(0, ITERS - 1) as it:
                    divide(it + 1)
                    silu(it + 1)
                    weigh(it, range(SLOTS))
                    residual(it + 1)
                    weigh(it, range(SLOTS, WAYS))
                    statistics(it + 1)
                    norm(it + 1)
                    softmax(it + 1)
                    result(it, range(SLOTS))
                    choose(it + 1)
                    result(it, range(SLOTS, WAYS))
                weigh(ITERS - 1, range(WAYS))
                result(ITERS - 1, range(WAYS))


def kernel(**inputs):
    import numpy as _np
    import concourse.bacc as _bacc
    from concourse.bass_utils import run_bass_kernel_spmd as _run

    a = {k: _np.asarray(v) for k, v in inputs.items()}
    t, at, f = "L0_tok_", "L0_attn_", "L0_ffn_"
    chunks = BATCH * SEQ // CHUNK
    arrays = {
        "x_idx": a["x"].reshape(chunks, TILES, P).transpose(0, 2, 1),
        "table": _np.concatenate([a[t + "fine_embed_w"], a[t + "loc_to_cluster_w"].T], axis=1),
        "cluster_b": a[t + "loc_to_cluster_b"], "coarse_w": a[t + "coarse_embed_w"],
        "w_q": a[at + "w_q"], "b_q": a[at + "b_q"], "w_k": a[at + "w_k"], "b_k": a[at + "b_k"],
        "w_v": a[at + "w_v"], "b_v": a[at + "b_v"], "g_q": a[at + "g_q"], "be_q": a[at + "be_q"],
        "g_k": a[at + "g_k"], "be_k": a[at + "be_k"], "w_o": a[at + "w_o"], "b_o": a[at + "b_o"],
        "router_t": a[f + "router_w"].T, "w1_t": a[f + "w1"].T, "b1_c": a[f + "b1"].reshape(FK, P).T,
        "w2_t": a[f + "w2"].T, "b2": a[f + "b2"],
    }
    arrays = {k: _np.ascontiguousarray(v) for k, v in arrays.items()}
    nc = _bacc.Bacc("TRN2", target_bir_lowering=False, num_devices=1)
    args = {k: nc.dram_tensor("in_" + k, v.shape, mybir.dt.from_np(v.dtype), kind="ExternalInput").ap()
            for k, v in arrays.items()}
    out = nc.dram_tensor("out", (BATCH, SEQ, DIM), F32, kind="ExternalOutput").ap()
    build(nc, out=out.rearrange("b (t p) n -> b p t n", p=P), **args)
    r = _run(nc, [{"in_" + k: v for k, v in arrays.items()}], core_ids=[0])
    return r.results[0]["out"]
```

```python
import concourse.bass as bass
from concourse import mybir
from contextlib import ExitStack

F32 = mybir.dt.float32
BF16 = mybir.dt.bfloat16
I32 = mybir.dt.int32
U32 = mybir.dt.uint32
ALU = mybir.AluOpType
ACT = mybir.ActivationFunctionType
AX = mybir.AxisListType

P = 128
BATCH, SEQ, DIM = 8, 1024, 128
HEADS = 8
HD = DIM // HEADS
HALF = DIM // 2
CLUSTERS = 64
EXPERTS = 64
CAP = 128
FFN = 512
FK = FFN // P
EPS = 1e-5
QSCALE = float(DIM) ** -0.5

WAYS = 4
SLOTS = 2
TILES = 4
CHUNK = TILES * P
ITERS = BATCH * SEQ // (CHUNK * WAYS)
PER_BATCH = SEQ // CHUNK

BANK = 512
HALVES = SEQ // BANK
TOKT = SEQ // P
PARTS = 3
Q_TERMS = (0, 0, 1, 1, 0, 2)
K_TERMS = (0, 1, 0, 1, 2, 0)
DATA_ROWS = HD * len(Q_TERMS)
ROWS = DATA_ROWS + PARTS
VW = HD + 1
GH = 4
GROUPS = HEADS // GH
HP = 32
BIAS_ROWS = (PARTS - 1) * HP + 1


def build(nc, x_idx, table, cluster_b, coarse_w, w_q, b_q, w_k, b_k, w_v, b_v, g_q, be_q, g_k, be_k,
          w_o, b_o, router_t, w1_t, b1_c, w2_t, b2, out):
    qk_parts = nc.dram_tensor("qk_parts", (BATCH, 2, PARTS, P, SEQ), BF16).ap()
    v_rows = nc.dram_tensor("v_rows", (BATCH, P, TOKT, HEADS * VW), F32).ap()
    h_rows = nc.dram_tensor("h_rows", (ITERS, WAYS, P, TILES * DIM), F32).ap()
    o_cols = nc.dram_tensor("o_cols", (BATCH, GROUPS, P, SEQ), F32).ap()
    inv_l = nc.dram_tensor("inv_l", (BATCH * HEADS, SEQ), F32).ap()

    ctx = ExitStack()
    with ctx:
        def keep(name, shape, dt=F32):
            return ctx.enter_context(nc.sbuf_tensor(name, shape, dt))

        c = {name: ctx.enter_context(nc.semaphore(name)) for name in ("idx_loaded", "weights_loaded")}
        c["ident"] = keep("ident", [P, P])
        c["later"] = keep("later", [P, P], BF16)
        c["ones"] = keep("ones", [P, P], BF16)
        c["expert_ids"] = keep("expert_ids", [P, EXPERTS])
        c["neg_half"] = keep("neg_half", [P, 2 * TILES])
        c["w_qkv"] = keep("w_qkv", [P, 3 * DIM])
        c["bias"] = keep("bias", [BIAS_ROWS, 5 * DIM])
        c["bias_parts"] = keep("bias_parts", [BIAS_ROWS, 5 * DIM], BF16)
        c["cluster_b"] = keep("cluster_b_sb", [P, CLUSTERS])
        c["coarse_w"] = keep("coarse_w_sb", [CLUSTERS, HALF])
        c["gain"] = keep("gain", [P, 2])
        c["shift"] = keep("shift", [P, 2])
        c["w_o"] = keep("w_o_sb", [P, DIM])
        c["router"] = keep("router_sb", [P, EXPERTS])
        c["w1"] = keep("w1_sb", [P, FFN])
        c["b1"] = keep("b1_sb", [P, FK])
        c["w2"] = keep("w2_sb", [P, FK, DIM])
        c["carry"] = keep("carry", [P, EXPERTS])
        c["idx_all"] = keep("idx_all", [P, (ITERS + 1) * WAYS * TILES], I32)

        loads = setup(nc, ctx, c, x_idx, cluster_b, coarse_w, w_q, b_q, w_k, b_k, w_v, b_v, g_q, be_q, g_k, be_k,
                      w_o, b_o, router_t, w1_t, b1_c, w2_t, b2)
        stacks = {name: ctx.enter_context(nc.semaphore("b_" + name + "0")) for name in ("loaded", "cleared")}
        stacks["qs"] = keep("qs0", [ROWS, HALVES, HEADS, BANK], BF16)
        stacks["ks"] = keep("ks0", [ROWS, HEADS, SEQ], BF16)
        stacks["vs"] = keep("vs0", [P, TOKT, HEADS, VW])
        embed(nc, c, loads, table, qk_parts, v_rows, h_rows, stacks)

        inputs = {name: [keep(f"{name}{w}", [P, CHUNK]) for w in range(WAYS)] for name in ("o_in", "inv_in", "h_in")}
        for name in ("o_loaded", "h_loaded"):
            inputs[name] = [ctx.enter_context(nc.semaphore(f"c_{name}{w}")) for w in range(WAYS)]
        attend(nc, qk_parts, v_rows, o_cols, inv_l, h_rows, stacks, inputs)
        finish(nc, c, h_rows, o_cols, inv_l, inputs, out)


def wait_apart(engine, sem, n):
    engine.to_reg(n)
    engine.wait_ge(sem, 1)
    engine.wait_ge(sem, n)


def add_bias(nc, c, dst, first, width):
    src = c["bias_parts"][:, first:first + width].unsqueeze(1).to_broadcast([BIAS_ROWS, BANK // width, width])
    nc.tensor.matmul(dst.rearrange("p (t n) -> p t n", n=width), c["ones"][0:BIAS_ROWS, :], src, start=True, stop=False)


def by_head(o_cols):
    return o_cols.rearrange("b g (h x) n -> (b g h) x n", x=HP)


def in_pieces(rows, piece):
    return rows.rearrange("r (s n) -> r s n", n=piece)


def preset(engine, sem, n):
    engine.sem_inc(sem, n)


def setup(nc, ctx, c, x_idx, cluster_b, coarse_w, w_q, b_q, w_k, b_k, w_v, b_v, g_q, be_q, g_k, be_k,
          w_o, b_o, router_t, w1_t, b1_c, w2_t, b2):
    made = ctx.enter_context(nc.semaphore("constants_made"))
    idx_int = ctx.enter_context(nc.sbuf_tensor("expert_ids_int", [P, EXPERTS], I32))
    idx_pad = ITERS * WAYS * TILES

    def rows(v, n=P):
        return v.rearrange("(a n) -> a n", a=1).to_broadcast([n, v.shape[0]])

    def column(v):
        return v.rearrange("(p a) -> p a", a=1)

    loads = [(c["w_qkv"][:, 0:DIM], w_q), (c["w_qkv"][:, DIM:2 * DIM], w_k), (c["w_qkv"][:, 2 * DIM:], w_v),
             (c["bias"][:, 0:DIM], rows(b_q, BIAS_ROWS)), (c["bias"][:, DIM:2 * DIM], rows(b_k, BIAS_ROWS)),
             (c["bias"][:, 2 * DIM:3 * DIM], rows(b_v, BIAS_ROWS)), (c["bias"][:, 3 * DIM:4 * DIM], rows(b_o, BIAS_ROWS)),
             (c["bias"][:, 4 * DIM:], rows(b2, BIAS_ROWS)),
             (c["cluster_b"][:, :], rows(cluster_b)), (c["coarse_w"][:, :], coarse_w),
             (c["gain"][:, 0:1], column(g_q)), (c["gain"][:, 1:2], column(g_k)),
             (c["shift"][:, 0:1], column(be_q)), (c["shift"][:, 1:2], column(be_k)),
             (c["w_o"][:, :], w_o), (c["router"][:, :], router_t),
             (c["w1"][:, :], w1_t), (c["b1"][:, :], b1_c),
             (c["w2"][:, :, :], w2_t.rearrange("(k p) n -> p k n", p=P))]

    with nc.Block() as block:
        @block.sync
        def _(sp):
            sp.dma_start(c["idx_all"][:, 0:idx_pad].rearrange("p (i t) -> p i t", t=TILES),
                         x_idx.rearrange("i p t -> p i t")).then_inc(c["idx_loaded"], 16)

        @block.gpsimd
        def _(pool):
            nc.gpsimd.memset(c["ident"][:, :], 0.0).then_inc(made, 1)
            nc.gpsimd.memset(c["later"][:, :], 0.0).then_inc(made, 1)
            nc.gpsimd.memset(c["ones"][:, :], 1.0).then_inc(made, 1)
            nc.gpsimd.memset(c["neg_half"][:, :], -0.5).then_inc(made, 1)
            nc.gpsimd.memset(c["carry"][:, :], 0.0).then_inc(made, 1)
            nc.gpsimd.memset(c["idx_all"][:, idx_pad:], 0).then_inc(made, 1)
            nc.gpsimd.iota(idx_int[:, :], pattern=[[1, EXPERTS]], base=0, channel_multiplier=0).then_inc(made, 1)
            pool.wait_ge(made, 7)
            nc.gpsimd.affine_select(out=c["ident"][:, :], in_=c["ident"][:, :], compare_op=ALU.not_equal, fill=1.0,
                                    base=0, pattern=[[-1, P]], channel_multiplier=1).then_inc(made, 1)
            nc.gpsimd.affine_select(out=c["later"][:, :], in_=c["later"][:, :], compare_op=ALU.is_ge, fill=1.0,
                                    base=0, pattern=[[-1, P]], channel_multiplier=1).then_inc(made, 1)
            nc.gpsimd.tensor_copy(c["expert_ids"][:, :], idx_int[:, :]).then_inc(made, 1)
    return loads


def embed(nc, c, loads, table, qk_parts, v_rows, h_rows, stacks):
    ctx = ExitStack()
    with ctx:
        def ways(name, shape, dt=F32):
            return [ctx.enter_context(nc.sbuf_tensor(f"{name}{w}", shape, dt)) for w in range(WAYS)]

        def sem(name):
            return ctx.enter_context(nc.semaphore("a_" + name))

        def way_sems(name):
            return [sem(f"{name}{w}") for w in range(WAYS)]

        idx = ways("idx", [P, TILES], I32)
        emb = ways("emb", [P, TILES, DIM])
        logit = ways("logit", [P, TILES, CLUSTERS])
        expo = ways("expo", [P, TILES, CLUSTERS])
        neg_max = ways("a_neg_max", [P, TILES])
        inv_sum = ways("a_inv_sum", [P, TILES])
        expo_t = ways("expo_t", [CLUSTERS, CHUNK])
        h = ways("h", [P, TILES, DIM])
        stat = ways("a_stat", [P, TILES, 6])
        mv = ways("a_mv", [P, TILES, 2])
        rs = ways("a_rs", [P, TILES])
        xn = ways("xn", [P, TILES, DIM])
        sx = ways("sx", [P, TILES, DIM])
        sx_t = ways("sx_t", [P, CHUNK])
        qk = ways("qk", [P, TILES, 2, DIM])
        vrow = ways("vrow", [P, TILES, HEADS, VW])
        stat2 = ways("a_stat2", [P, TILES * 2, 6])
        mv2 = ways("a_mv2", [P, TILES * 2, 2])
        rs3 = ways("a_rs3", [P, TILES * 2])
        k_offset = ways("k_offset", [P, TILES])
        full = ways("qk_full", [P, 2, CHUNK])
        rest = ways("qk_rest", [P, 2, CHUNK])
        part = [ways(f"qk_part{n}_", [P, 2, CHUNK], BF16) for n in range(PARTS)]
        psA = [ctx.enter_context(nc.psum_tensor(f"a_psA{i}", [P, BANK], F32)) for i in range(SLOTS)] * (WAYS // SLOTS)
        psV = [ctx.enter_context(nc.psum_tensor(f"a_psV{i}", [P, BANK], F32)) for i in range(SLOTS)] * (WAYS // SLOTS)
        psQK = [ctx.enter_context(nc.psum_tensor(f"a_psQK{i}", [P, 2, BANK], F32)) for i in range(SLOTS)] * (WAYS // SLOTS)

        ones_set = sem("ones_set")
        gain_scaled = sem("gain_scaled")
        bias_split = sem("bias_split")
        bias_ready = sem("bias_ready")
        bias_rest = ctx.enter_context(nc.sbuf_tensor("bias_rest", [BIAS_ROWS, 5 * DIM], F32))
        bias_part = [ctx.enter_context(nc.sbuf_tensor(f"bias_part{n}", [BIAS_ROWS, 5 * DIM], BF16)) for n in range(PARTS)]
        idx_copied = sem("idx_copied")
        gathered = way_sems("gathered")
        logit_biased = sem("logit_biased")
        max_found = sem("max_found")
        logit_shifted = sem("logit_shifted")
        exp_done = sem("exp_done")
        sum_done = sem("sum_done")
        inv_done = sem("inv_done")
        exp_t_done = sem("exp_t_done")
        exp_t_copied = sem("exp_t_copied")
        coarse_done = sem("coarse_done")
        coarse_scaled = sem("coarse_scaled")
        fine_copied = sem("fine_copied")
        h_stored = way_sems("h_stored")
        stats_done = sem("stats_done")
        aggr_done = sem("aggr_done")
        both_var_done = sem("both_var_done")
        rstd_done = sem("rstd_done")
        xn_done = sem("xn_done")
        tanh_done = sem("tanh_done")
        silu_done = sem("silu_done")
        silu_t_done = sem("silu_t_done")
        silu_t_copied = sem("silu_t_copied")
        qk_projected = sem("qk_projected")
        v_projected = sem("v_projected")
        qk_copied = sem("qk_copied")
        v_copied = sem("v_copied")
        v_stored = way_sems("v_stored")
        stats2_done = sem("stats2_done")
        aggr2_done = sem("aggr2_done")
        means2_done = sem("means2_done")
        rstd2_done = sem("rstd2_done")
        k_offset_done = sem("k_offset_done")
        q_normed = sem("q_normed")
        k_normed = sem("k_normed")
        qk_t_done = sem("qk_t_done")
        qk_scaled = sem("qk_scaled")
        part0_done = sem("part0_done")
        rest1_done = sem("rest1_done")
        rest_by_dve = sem("rest_by_dve")
        part1_done = sem("part1_done")
        part2_done = sem("part2_done")
        parts_stored = way_sems("parts_stored")

        with nc.Block() as block:
            @block.sync
            def _(sp):
                for w in range(WAYS):
                    for s in (h_stored, v_stored, parts_stored):
                        preset(sp, s[w], 16 * (PARTS if s is parts_stored else 1))
                preset(sp, qk_scaled, SLOTS)

            @block.vector
            def _(dve):
                for w in range(WAYS):
                    last = nc.vector.memset(vrow[w][:, :, :, HD:VW], 1.0)
                last.then_inc(ones_set, 1)

        with nc.Block() as block:
            @block.gpsimd
            def _(pool):
                def gather(r, ways_now):
                    for w in ways_now:
                        cols = bass.ds((r * WAYS + w) * TILES, TILES)
                        nc.gpsimd.tensor_copy(idx[w][:, :], c["idx_all"][:, cols]).then_inc(idx_copied, 1)
                        wait_apart(pool, idx_copied, r * WAYS + w + 1)
                        for t in range(TILES):
                            nc.gpsimd.indirect_dma_start(
                                out=emb[w][:, t, :], out_offset=None, in_=table,
                                in_offset=bass.IndirectOffsetOnAxis(ap=idx[w][:, t:t + 1], axis=0)).then_inc(gathered[w], 16)

                def regather(r, ways_now=range(WAYS)):
                    pool.wait_ge(fine_copied, r * WAYS)
                    wait_apart(pool, logit_biased, r * WAYS)
                    for w in ways_now:
                        pool.wait_ge(gathered[w], r * 16 * TILES)
                    gather(r, ways_now)

                def root_front(r):
                    for w in range(WAYS):
                        pool.wait_ge(both_var_done, r * WAYS + w + 1)
                        nc.gpsimd.tensor_tensor(rs[w][:, :], rs[w][:, :], c["neg_half"][:, 0:TILES],
                                                ALU.pow).then_inc(rstd_done, 1)

                def root_back(r, ways_now=range(WAYS)):
                    for w in ways_now:
                        pool.wait_ge(aggr2_done, r * WAYS + w + 1)
                        nc.gpsimd.tensor_tensor(rs3[w][:, :], rs3[w][:, :], c["neg_half"][:, :], ALU.pow).then_inc(rstd2_done, 1)

                def subtract_part0(r, ways_now=range(WAYS)):
                    for w in ways_now:
                        n = r * WAYS + w + 1
                        pool.wait_ge(qk_scaled, n + SLOTS)
                        pool.wait_ge(part0_done, n)
                        nc.gpsimd.tensor_tensor(rest[w][:, :, :], full[w][:, :, :], part[0][w][:, :, :],
                                                ALU.subtract).then_inc(rest1_done, 1)

                pool.wait_ge(c["idx_loaded"], 16)
                gather(0, range(WAYS))
                regather(1, range(WAYS - 1))
                root_front(0)
                regather(1, range(WAYS - 1, WAYS))
                with pool.Fori(0, ITERS - 1) as it:
                    regather(it + 2, (0, 1, 2))
                    root_back(it)
                    regather(it + 2, (3,))
                    root_front(it + 1)
                    subtract_part0(it)
                root_back(ITERS - 1)
                subtract_part0(ITERS - 1, range(SLOTS, WAYS))
                for w in range(WAYS):
                    pool.wait_ge(gathered[w], (ITERS + 1) * 16 * TILES)

            @block.vector
            def _(dve):
                def logits(r):
                    for w in range(WAYS):
                        dve.wait_ge(gathered[w], (r + 1) * 16 * TILES)
                        nc.vector.tensor_tensor(logit[w][:, :, :], emb[w][:, :, HALF:DIM],
                                                c["cluster_b"][:, :].unsqueeze(1).to_broadcast([P, TILES, CLUSTERS]),
                                                ALU.add).then_inc(logit_biased, 1)
                    for w in range(WAYS):
                        dve.wait_ge(logit_biased, r * WAYS + w + 1)
                        nc.vector.tensor_reduce(neg_max[w][:, :], logit[w][:, :, :], AX.X, ALU.max,
                                                negate=True).then_inc(max_found, 1)
                    for w in range(WAYS):
                        dve.wait_ge(max_found, r * WAYS + w + 1)
                        nc.vector.tensor_tensor(logit[w][:, :, :], logit[w][:, :, :],
                                                neg_max[w][:, :].unsqueeze(2).to_broadcast([P, TILES, CLUSTERS]),
                                                ALU.add).then_inc(logit_shifted, 1)

                def exp_sums(r):
                    for w in range(WAYS):
                        dve.wait_ge(exp_done, r * WAYS + w + 1)
                        nc.vector.tensor_reduce(inv_sum[w][:, :], expo[w][:, :, :], AX.X, ALU.add).then_inc(sum_done, 1)
                    for w in range(WAYS):
                        dve.wait_ge(sum_done, r * WAYS + w + 1)
                        nc.vector.reciprocal(inv_sum[w][:, :], inv_sum[w][:, :]).then_inc(inv_done, 1)

                def coarse_half(r, ways_now=range(WAYS)):
                    for w in ways_now:
                        n = r * WAYS + w + 1
                        dve.wait_ge(inv_done, n)
                        dve.wait_ge(coarse_done, n)
                        dve.wait_ge(h_stored[w], (r + 1) * 16)
                        nc.vector.tensor_tensor(h[w][:, :, HALF:DIM],
                                                psV[w][:, 0:TILES * HALF].rearrange("p (t n) -> p t n", t=TILES),
                                                inv_sum[w][:, :].unsqueeze(2).to_broadcast([P, TILES, HALF]),
                                                ALU.mult).then_inc(coarse_scaled, 1)

                def stats_front(r):
                    for w in range(WAYS):
                        dve.wait_ge(coarse_scaled, r * WAYS + w + 1)
                        dve.wait_ge(fine_copied, r * WAYS + w + 1)
                        for t in range(TILES):
                            last = nc.vector.bn_stats(stat[w][:, t, :], h[w][:, t, :])
                        last.then_inc(stats_done, 1)
                    for w in range(WAYS):
                        n = r * WAYS + w + 1
                        wait_apart(dve, stats_done, n)
                        for t in range(TILES):
                            last = nc.vector.bn_aggr(mv[w][:, t, :], stat[w][:, t, :])
                        last.then_inc(aggr_done, 1)
                        dve.wait_ge(aggr_done, n)
                        nc.vector.tensor_scalar(rs[w][:, :], mv[w][:, :, 1], 1.0 + EPS, EPS * EPS, ALU.mult,
                                                ALU.add).then_inc(both_var_done, 1)

                def norm_front(r):
                    for w in range(WAYS):
                        dve.wait_ge(rstd_done, r * WAYS + w + 1)
                        for t in range(TILES):
                            last = nc.vector.tensor_scalar(xn[w][:, t, :], h[w][:, t, :], mv[w][:, t, 0:1],
                                                           rs[w][:, t:t + 1], ALU.subtract, ALU.mult)
                        last.then_inc(xn_done, 1)

                def silu(r):
                    for w in range(WAYS):
                        dve.wait_ge(tanh_done, r * WAYS + w + 1)
                        nc.vector.scalar_tensor_tensor(out=sx[w][:, :, :], in0=sx[w][:, :, :], scalar=1.0,
                                                       in1=xn[w][:, :, :], op0=ALU.add, op1=ALU.mult).then_inc(silu_done, 1)

                def stats_back(r, ways_now=range(WAYS)):
                    for w in ways_now:
                        dve.wait_ge(qk_copied, r * WAYS + w + 1)
                        for t in range(TILES):
                            for a in range(2):
                                last = nc.vector.bn_stats(stat2[w][:, 2 * t + a, :], qk[w][:, t, a, :])
                        last.then_inc(stats2_done, 1)

                def aggregate_back(r, ways_now=range(WAYS)):
                    for w in ways_now:
                        n = r * WAYS + w + 1
                        wait_apart(dve, stats2_done, n)
                        for j in range(2 * TILES):
                            last = nc.vector.bn_aggr(mv2[w][:, j, :], stat2[w][:, j, :])
                        last.then_inc(means2_done, 1)
                        dve.wait_ge(means2_done, n)
                        nc.vector.tensor_scalar(rs3[w][:, :], mv2[w][:, :, 1], EPS, None, ALU.add).then_inc(aggr2_done, 1)

                def norm_back(r, ways_now=range(WAYS)):
                    for w in ways_now:
                        dve.wait_ge(rstd2_done, r * WAYS + w + 1)
                        nc.vector.scalar_tensor_tensor(
                            out=k_offset[w][:, :], in0=mv2[w][:, :, 0].rearrange("p (t a) -> p t a", a=2)[:, :, 1], scalar=-1.0,
                            in1=rs3[w][:, :].rearrange("p (t a) -> p t a", a=2)[:, :, 1],
                            op0=ALU.mult, op1=ALU.mult).then_inc(k_offset_done, 1)
                        for t in range(TILES):
                            last = nc.vector.tensor_scalar(qk[w][:, t, 0, :], qk[w][:, t, 0, :], mv2[w][:, 2 * t, 0:1],
                                                           rs3[w][:, 2 * t:2 * t + 1], ALU.subtract, ALU.mult)
                        last.then_inc(q_normed, 1)

                def subtract_part1(r, ways_now=range(WAYS), skipped=0):
                    for w in ways_now:
                        dve.wait_ge(part1_done, r * WAYS + w + 1 - skipped)
                        nc.vector.tensor_tensor(part[2][w][:, :, :], rest[w][:, :, :], part[1][w][:, :, :],
                                                ALU.subtract).then_inc(part2_done, 1)

                nc.vector.memset(stacks["ks"][DATA_ROWS:ROWS, :, :], 1.0).then_inc(stacks["cleared"], 1)
                dve.wait_ge(c["weights_loaded"], 16 * len(loads))
                nc.vector.tensor_scalar(c["gain"][:, 0:1], c["gain"][:, 0:1], QSCALE, None, ALU.mult).then_inc(gain_scaled, 1)
                nc.vector.tensor_scalar(c["shift"][:, 0:1], c["shift"][:, 0:1], QSCALE, None, ALU.mult).then_inc(gain_scaled, 1)
                nc.vector.memset(c["bias_parts"][:, :], 0.0).then_inc(bias_split, 1)
                nc.vector.tensor_copy(bias_part[0][:, :], c["bias"][:, :]).then_inc(bias_split, 1)
                dve.wait_ge(bias_split, 2)
                nc.vector.tensor_tensor(bias_rest[:, :], c["bias"][:, :], bias_part[0][:, :], ALU.subtract).then_inc(bias_split, 1)
                dve.wait_ge(bias_split, 3)
                nc.vector.tensor_copy(bias_part[1][:, :], bias_rest[:, :]).then_inc(bias_split, 1)
                dve.wait_ge(bias_split, 4)
                nc.vector.tensor_tensor(bias_part[2][:, :], bias_rest[:, :], bias_part[1][:, :], ALU.subtract).then_inc(bias_split, 1)
                dve.wait_ge(bias_split, 5)
                for n in range(PARTS):
                    row = slice(n * HP, n * HP + 1)
                    nc.vector.tensor_copy(c["bias_parts"][row, :], bias_part[n][row, :]).then_inc(bias_ready, 1)

                logits(0)
                exp_sums(0)
                coarse_half(0)
                stats_front(0)
                norm_front(0)
                silu(0)
                logits(1)
                with dve.Fori(0, ITERS - 1) as it:
                    stats_back(it, (0,))
                    exp_sums(it + 1)
                    stats_back(it, (1,))
                    aggregate_back(it, (0, 1))
                    stats_back(it, (2,))
                    aggregate_back(it, (2,))
                    stats_back(it, (3,))
                    aggregate_back(it, (3,))
                    for w in range(WAYS):
                        coarse_half(it + 1, (w,))
                        norm_back(it, (w,))
                    stats_front(it + 1)
                    norm_front(it + 1)
                    silu(it + 1)
                    logits(it + 2)
                    subtract_part1(it)
                for w in range(WAYS):
                    stats_back(ITERS - 1, (w,))
                    aggregate_back(ITERS - 1, (w,))
                    if w:
                        norm_back(ITERS - 1, (w - 1,))
                norm_back(ITERS - 1, (WAYS - 1,))
                for w in range(SLOTS):
                    dve.wait_ge(part0_done, (ITERS - 1) * WAYS + w + 1)
                    nc.vector.tensor_tensor(rest[w][:, :, :], full[w][:, :, :], part[0][w][:, :, :], ALU.subtract).then_inc(rest_by_dve, 1)
                    dve.wait_ge(rest_by_dve, 2 * w + 1)
                    nc.vector.tensor_copy(part[1][w][:, :, :], rest[w][:, :, :]).then_inc(rest_by_dve, 1)
                    dve.wait_ge(rest_by_dve, 2 * w + 2)
                    nc.vector.tensor_tensor(part[2][w][:, :, :], rest[w][:, :, :], part[1][w][:, :, :],
                                            ALU.subtract).then_inc(part2_done, 1)
                subtract_part1(ITERS - 1, range(SLOTS, WAYS), skipped=SLOTS)

            @block.scalar
            def _(act):
                def copy_fine(r):
                    for w in range(WAYS):
                        act.wait_ge(gathered[w], (r + 1) * 16 * TILES)
                        act.wait_ge(h_stored[w], (r + 1) * 16)
                        nc.scalar.activation(h[w][:, :, 0:HALF], emb[w][:, :, 0:HALF], ACT.Copy).then_inc(fine_copied, 1)

                def exponentials(r):
                    for w in range(WAYS):
                        act.wait_ge(logit_shifted, r * WAYS + w + 1)
                        nc.scalar.activation(expo[w][:, :, :], logit[w][:, :, :], ACT.Exp).then_inc(exp_done, 1)

                def copy_exp_t(r):
                    for w in range(WAYS):
                        act.wait_ge(exp_t_done, r * WAYS + w + 1)
                        nc.scalar.activation(expo_t[w][:, :], psA[w][0:CLUSTERS, :], ACT.Copy).then_inc(exp_t_copied, 1)

                def tanh(r, ways_now=range(WAYS)):
                    for w in ways_now:
                        act.wait_ge(xn_done, r * WAYS + w + 1)
                        nc.scalar.activation(sx[w][:, :, :], xn[w][:, :, :], ACT.Tanh, scale=0.5).then_inc(tanh_done, 1)

                def copy_silu_t(r, ways_now):
                    for w in ways_now:
                        act.wait_ge(silu_t_done, r * WAYS + w + 1)
                        nc.scalar.activation(sx_t[w][:, :], psA[w][:, :], ACT.Copy, scale=0.5).then_inc(silu_t_copied, 1)

                def copy_projected(r, ways_now):
                    for w in ways_now:
                        n = r * WAYS + w + 1
                        act.wait_ge(qk_projected, n)
                        nc.scalar.activation(qk[w][:, :, :, :].rearrange("p t a n -> p (t a n)"),
                                             psQK[w][:, :, :].rearrange("p b n -> p (b n)"), ACT.Copy).then_inc(qk_copied, 1)
                        act.wait_ge(v_stored[w], (r + 1) * 16)
                        act.wait_ge(v_projected, n)
                        nc.scalar.activation(vrow[w][:, :, :, 0:HD],
                                             psV[w][:, :].rearrange("p (t h d) -> p t h d", t=TILES, h=HEADS),
                                             ACT.Copy).then_inc(v_copied, 1)

                def norm_k(r, ways_now=range(WAYS)):
                    for w in ways_now:
                        act.wait_ge(k_offset_done, r * WAYS + w + 1)
                        for t in range(TILES):
                            last = nc.scalar.activation(qk[w][:, t, 1, :], qk[w][:, t, 1, :], ACT.Identity,
                                                        bias=k_offset[w][:, t:t + 1], scale=rs3[w][:, 2 * t + 1:2 * t + 2])
                        last.then_inc(k_normed, 1)

                def scale_qk(r, ways_now=range(WAYS)):
                    for w in ways_now:
                        act.wait_ge(qk_t_done, r * WAYS + w + 1)
                        for a in range(2):
                            last = nc.scalar.activation(full[w][:, a, :], psQK[w][:, a, :], ACT.Identity,
                                                        bias=c["shift"][:, a:a + 1], scale=c["gain"][:, a:a + 1])
                        last.then_inc(qk_scaled, 1)
                        act.wait_ge(parts_stored[w], (r + 1) * 16 * PARTS)
                        act.wait_ge(qk_scaled, r * WAYS + w + 1 + SLOTS)
                        nc.scalar.activation(part[0][w][:, :, :], full[w][:, :, :], ACT.Copy).then_inc(part0_done, 1)

                def round_rest(r, ways_now=range(WAYS), skipped=0):
                    for w in ways_now:
                        act.wait_ge(rest1_done, r * WAYS + w + 1 - skipped)
                        nc.scalar.activation(part[1][w][:, :, :], rest[w][:, :, :], ACT.Copy).then_inc(part1_done, 1)

                copy_fine(0)
                exponentials(0)
                copy_exp_t(0)
                tanh(0)
                copy_silu_t(0, range(SLOTS))
                act.wait_ge(gain_scaled, 2)
                with act.Fori(0, ITERS - 1) as it:
                    copy_silu_t(it, range(SLOTS, WAYS))
                    copy_fine(it + 1)
                    exponentials(it + 1)
                    copy_projected(it, range(SLOTS))
                    copy_exp_t(it + 1)
                    copy_projected(it, range(SLOTS, WAYS))
                    norm_k(it)
                    scale_qk(it, (0, 1, 2))
                    tanh(it + 1)
                    scale_qk(it, (3,))
                    copy_silu_t(it + 1, range(SLOTS))
                    round_rest(it)
                copy_silu_t(ITERS - 1, range(SLOTS, WAYS))
                copy_projected(ITERS - 1, (0, 1, 2))
                norm_k(ITERS - 1, (0,))
                copy_projected(ITERS - 1, (3,))
                norm_k(ITERS - 1, (1, 2))
                scale_qk(ITERS - 1, (0,))
                norm_k(ITERS - 1, (3,))
                scale_qk(ITERS - 1, (1, 2, 3))
                round_rest(ITERS - 1, range(SLOTS, WAYS), skipped=SLOTS)

            @block.tensor
            def _(pe):
                def transpose_exp(r, alone=False):
                    for w in range(WAYS):
                        if w >= SLOTS:
                            pe.wait_ge(exp_t_copied, r * WAYS + w + 1 - SLOTS)
                        elif not alone:
                            pe.wait_ge(silu_t_copied, (r - 1) * WAYS + w + 1 + SLOTS)
                        wait_apart(pe, exp_done, r * WAYS + w + 1)
                        for t in range(TILES):
                            last = nc.tensor.transpose(psA[w][0:CLUSTERS, t * P:(t + 1) * P], expo[w][:, t, :], c["ident"][:, :])
                        last.then_inc(exp_t_done, 1)

                def coarse(r, alone=False):
                    for w in range(WAYS):
                        pe.wait_ge(exp_t_copied, r * WAYS + w + 1)
                        if w >= SLOTS:
                            pe.wait_ge(coarse_scaled, r * WAYS + w + 1 - SLOTS)
                        elif not alone:
                            pe.wait_ge(v_copied, (r - 1) * WAYS + w + 1 + SLOTS)
                        for t in range(TILES):
                            last = nc.tensor.matmul(psV[w][:, t * HALF:(t + 1) * HALF], expo_t[w][:, t * P:(t + 1) * P],
                                                    c["coarse_w"][:, :], start=True, stop=True)
                        last.then_inc(coarse_done, 1)

                def transpose_silu(r):
                    for w in range(WAYS):
                        pe.wait_ge(silu_done, r * WAYS + w + 1)
                        if w >= SLOTS:
                            pe.wait_ge(silu_t_copied, r * WAYS + w + 1 - SLOTS)
                        for t in range(TILES):
                            last = nc.tensor.transpose(psA[w][:, t * P:(t + 1) * P], sx[w][:, t, :], c["ident"][:, :])
                        last.then_inc(silu_t_done, 1)

                def project(r, ways_now):
                    for w in ways_now:
                        if w >= SLOTS:
                            pe.wait_ge(qk_copied, r * WAYS + w + 1 - SLOTS)
                            pe.wait_ge(v_copied, r * WAYS + w + 1 - SLOTS)
                        else:
                            pe.wait_ge(qk_scaled, r * WAYS + w + 1)
                        for half in range(2):
                            add_bias(nc, c, psQK[w][:, half, :], 0, 2 * DIM)
                        add_bias(nc, c, psV[w][:, :], 2 * DIM, DIM)
                        pe.wait_ge(silu_t_copied, r * WAYS + w + 1)
                        for t in range(TILES):
                            last = nc.tensor.matmul(psQK[w][:, t // 2, (t % 2) * 2 * DIM:(t % 2 + 1) * 2 * DIM],
                                                    sx_t[w][:, t * P:(t + 1) * P], c["w_qkv"][:, 0:2 * DIM],
                                                    start=False, stop=t % 2 == 1)
                        last.then_inc(qk_projected, 1)
                        for t in range(TILES):
                            last = nc.tensor.matmul(psV[w][:, t * DIM:(t + 1) * DIM], sx_t[w][:, t * P:(t + 1) * P],
                                                    c["w_qkv"][:, 2 * DIM:], start=False, stop=t == TILES - 1)
                        last.then_inc(v_projected, 1)

                def transpose_qk(r):
                    for w in range(WAYS):
                        pe.wait_ge(q_normed, r * WAYS + w + 1)
                        pe.wait_ge(k_normed, r * WAYS + w + 1)
                        if w >= SLOTS:
                            pe.wait_ge(qk_scaled, r * WAYS + w + 1)
                        else:
                            pe.wait_ge(qk_copied, r * WAYS + w + 1 + SLOTS)
                        for a in range(2):
                            for t in range(TILES):
                                last = nc.tensor.transpose(psQK[w][:, a, t * P:(t + 1) * P], qk[w][:, t, a, :], c["ident"][:, :])
                        last.then_inc(qk_t_done, 1)

                pe.wait_ge(c["weights_loaded"], 16 * len(loads))
                transpose_exp(0, alone=True)
                coarse(0, alone=True)
                pe.wait_ge(bias_ready, PARTS)
                with pe.Fori(0, ITERS - 1) as it:
                    transpose_silu(it)
                    project(it, range(SLOTS))
                    transpose_exp(it + 1)
                    project(it, range(SLOTS, WAYS))
                    coarse(it + 1)
                    transpose_qk(it)
                transpose_silu(ITERS - 1)
                project(ITERS - 1, range(WAYS))
                transpose_qk(ITERS - 1)

            @block.sync
            def _(sp):
                def store_h(r):
                    for w in range(WAYS):
                        sp.wait_ge(coarse_scaled, r * WAYS + w + 1)
                        sp.wait_ge(fine_copied, r * WAYS + w + 1)
                        sp.dma_start(h_rows[r, w], h[w][:, :, :].rearrange("p t n -> p (t n)")).then_inc(h_stored[w], 16)

                def store_v(r):
                    for w in range(WAYS):
                        sp.wait_ge(v_copied, r * WAYS + w + 1)
                        at = w % PER_BATCH
                        sp.dma_start(v_rows[r * (WAYS // PER_BATCH) + w // PER_BATCH, :, at * TILES:(at + 1) * TILES, :],
                                     vrow[w][:, :, :, :].rearrange("p t h d -> p t (h d)")).then_inc(v_stored[w], 16)

                def store_parts(r):
                    for w in range(WAYS):
                        sp.wait_ge(part2_done, r * WAYS + w + 1)
                        for n in range(PARTS):
                            at = w % PER_BATCH
                            sp.dma_start(qk_parts[r * (WAYS // PER_BATCH) + w // PER_BATCH, :, n, :,
                                                  at * CHUNK:(at + 1) * CHUNK].rearrange("a p n -> p a n"),
                                         part[n][w][:, :, :]).then_inc(parts_stored[w], 16)

                for dst, src in loads:
                    sp.dma_start(dst, src).then_inc(c["weights_loaded"], 16)
                store_h(0)
                with sp.Fori(0, ITERS - 1) as it:
                    store_v(it)
                    store_h(it + 1)
                    store_parts(it)
                for w in range(PER_BATCH):
                    sp.wait_ge(parts_stored[w], ITERS * 16 * PARTS)
                    sp.wait_ge(v_stored[w], ITERS * 16)
                load_stacks(sp, 0, qk_parts, v_rows, stacks["qs"], stacks["ks"], stacks["vs"], stacks["loaded"])
                store_v(ITERS - 1)
                store_parts(ITERS - 1)
                for w in range(WAYS):
                    sp.wait_ge(h_stored[w], (ITERS + 1) * 16)
                    sp.wait_ge(v_stored[w], (ITERS + 1) * 16)
                    sp.wait_ge(parts_stored[w], (ITERS + 1) * 16 * PARTS)


def load_stacks(sp, batch, qk_parts, v_rows, qs, ks, vs, loaded):
    for i, (qp, kp) in enumerate(zip(Q_TERMS, K_TERMS)):
        r = slice(i * HD, (i + 1) * HD)
        for half in range(HALVES):
            sp.dma_start(qs[r, half, :, :], qk_parts[batch, 0, qp].rearrange("(h d) (s n) -> d s h n", d=HD, s=HALVES)[:, half]).then_inc(
                loaded, 16)
        sp.dma_start(ks[r, :, :], qk_parts[batch, 1, kp].rearrange("(h d) n -> d h n", d=HD)).then_inc(loaded, 16)
    sp.dma_start(vs[:, :, :, :].rearrange("p t h d -> p t (h d)"), v_rows[batch]).then_inc(loaded, 16)


def attend(nc, qk_parts, v_rows, o_cols, inv_l, h_rows, stacks, inputs):
    STEPS = HALVES * TOKT
    PAIR = 2 * GROUPS * STEPS
    PAIRS = BATCH // 2
    LEAD = TOKT + 5
    SRING, MRING, PRING = 3, 2, 4
    HTILES = TOKT // HALVES
    MAXES = GH * HTILES
    M_STEP = MAXES // TOKT
    SETS = 2 * GROUPS * HALVES
    PLACES = PARTS * (P // HP)
    LOADS = (HALVES + 1) * len(Q_TERMS) + 1

    ctx = ExitStack()
    with ctx:
        def sb(name, shape, dt=F32):
            return ctx.enter_context(nc.sbuf_tensor(name, shape, dt))

        def ps(name, shape):
            return ctx.enter_context(nc.psum_tensor(name, shape, F32))

        def sem(name):
            return ctx.enter_context(nc.semaphore("b_" + name))

        qs = [stacks["qs"], sb("qs1", [ROWS, HALVES, HEADS, BANK], BF16)]
        ks = [stacks["ks"], sb("ks1", [ROWS, HEADS, SEQ], BF16)]
        vs = [stacks["vs"], sb("vs1", [P, TOKT, HEADS, VW])]
        prob = [sb(f"prob{i}", [P, GH, BANK]) for i in range(PRING)]
        neg_max = [sb(f"b_neg_max{i}", [P, MAXES]) for i in range(2)]
        mrest = [sb(f"mrest{i}", [P, MAXES]) for i in range(2)]
        mpart = [sb(f"mpart{i}", [P, PARTS + 1, MAXES], BF16) for i in range(2)]
        mpart_t = [sb(f"mpart_t{i}", [P, (PARTS + 1) * MAXES // HP, HP], BF16) for i in range(2)]
        ot = [sb(f"ot{i}", [P, BANK]) for i in range(2)]
        early_rows = (BATCH - 2) * HEADS
        sums = sb("early_sums", [early_rows * HALVES, BANK])
        psS = [ps(f"psS{i}", [P, BANK]) for i in range(SRING)]
        psM = [ps(f"psM{i}", [P, HALVES, BANK]) for i in range(MRING)]
        psO = ps("psO", [P, BANK])

        loaded = [stacks["loaded"], sem("loaded1")]
        cleared = [stacks["cleared"], sem("cleared1")]
        out_cleared = sem("out_cleared")
        scored = sem("scored")
        score_free = sem("score_free")
        prob_free = sem("prob_free")
        max_scored = sem("max_scored")
        max_free = sem("max_free")
        split = sem("split")
        max_t_done = sem("max_t_done")
        max_loaded = [sem(f"max_loaded{i}") for i in range(2)]
        out_free = sem("out_free")
        o_stored = [sem(f"o_stored{i}") for i in range(2)]
        SPLITS = 4
        sums_loaded = sem("sums_loaded")
        sums_inverted = sem("sums_inverted")
        inv_stored = sem("inv_stored")

        with nc.Block() as block:
            @block.sync
            def _(sp):
                preset(sp, score_free, 1)
                preset(sp, prob_free, PRING)
                preset(sp, max_free, MRING)
                preset(sp, out_free, 1)
                for i in range(2):
                    preset(sp, o_stored[i], 16)

            @block.vector
            def _(dve):
                nc.vector.memset(psO[:, :], 0.0).then_inc(out_cleared, 1)
                for i in range(2):
                    nc.vector.memset(mpart[i][:, PARTS, :], 0.0)

        def load(sp, batch, buf):
            load_stacks(sp, batch, qk_parts, v_rows, qs[buf], ks[buf], vs[buf], loaded[buf])

        def place(step):
            g = step // STEPS
            return g, (g // GROUPS) % 2, g % GROUPS, step % STEPS // TOKT, step % TOKT

        with nc.Block() as block:
            @block.gpsimd
            def _(pool):
                nc.gpsimd.memset(ks[1][DATA_ROWS:ROWS, :, :], 1.0).then_inc(cleared[1], 1)

            @block.sync
            def _(sp):
                def place_maxima(p, e):
                    buf, gb, half = e // (GROUPS * HALVES) % 2, e // HALVES % GROUPS, e % HALVES
                    sp.wait_ge(max_t_done, p * SETS + e + 1)
                    for a in range(P // HP):
                        for n in range(PARTS):
                            dst = qs[buf][DATA_ROWS + n:DATA_ROWS + n + 1, half, GH * gb:GH * (gb + 1), :]
                            dst = dst.rearrange("o h (t a r) -> o a (h t) r", a=P // HP, r=HP)[:, a, :, :]
                            row = a * HP + n * MAXES % HP
                            sp.dma_start(dst, mpart_t[e % 2][row:row + MAXES, n * MAXES // HP, :]).then_inc(max_loaded[e % 2], 16)

                def store(p, half):
                    sp.wait_ge(out_free, p * (PAIR // TOKT) + half + 2)
                    sp.dma_start(o_cols[2 * p + half // 4, half // 2 % 2, :, half % 2 * BANK:(half % 2 + 1) * BANK],
                                 ot[half % 2][:, :]).then_inc(o_stored[half % 2], 16)

                def load_next(p, buf, last):
                    if buf == 1 or not last:
                        sp.wait_ge(prob_free, p * PAIR + (PAIR // 2 if buf == 0 else 0) + PRING)
                        load(sp, 2 * p + 2 - buf, buf)
                    if buf == 1 and last:
                        for i in range(2):
                            sp.wait_ge(o_stored[i], 16 + 16 * (BATCH - 2) * GROUPS)
                        sp.dma_start(sums[:, :], in_pieces(by_head(o_cols)[0:early_rows, HD, :], BANK)).then_inc(sums_loaded, 16)
                    if buf == 0 and last:
                        sp.wait_ge(sums_inverted, 1)
                        sp.dma_start(in_pieces(inv_l[0:early_rows, :], BANK), sums[:, :]).then_inc(inv_stored, 16)

                def pair(p, last):
                    for e in range(SETS):
                        if not (last and e == SETS - 1):
                            place_maxima(p, e + 1)
                        if e % (SETS // 2) == 0:
                            load_next(p, 0 if e else 1, last)
                        if last and e == SETS - 2:
                            sp.wait_ge(inv_stored, 16)
                            for w in range(WAYS):
                                load_outputs(sp, 0, w, o_cols, inv_l, inputs)
                                load_h(sp, 0, w, h_rows, inputs)
                        store(p, e)

                place_maxima(0, 0)
                with sp.Fori(0, PAIRS - 1) as p:
                    pair(p, False)
                pair(PAIRS - 1, True)
                for i in range(2):
                    sp.wait_ge(o_stored[i], 16 + 16 * BATCH * GROUPS)
                sp.wait_ge(inv_stored, 16)

            @block.tensor
            def _(pe):
                def find_max(p, step):
                    g, buf, gb, half, _ = place(step)
                    if step % (GROUPS * STEPS) == 0:
                        pe.wait_ge(loaded[buf], (p + 1 + step // PAIR) * 16 * LOADS)
                    for m in range(M_STEP):
                        unit = step % TOKT * M_STEP + m
                        hh = GH * gb + unit // HTILES
                        count = step * M_STEP + m
                        pe.wait_ge(max_free, p * PAIR * M_STEP + count + 1)
                        for kh in range(HALVES):
                            last_mm = nc.tensor.matmul(psM[count % MRING][:, kh, :],
                                                       qs[buf][0:DATA_ROWS, half, hh, unit % HTILES * P:(unit % HTILES + 1) * P],
                                                       ks[buf][0:DATA_ROWS, hh, kh * BANK:(kh + 1) * BANK],
                                                       start=True, stop=True)
                        last_mm.then_inc(max_scored, 1)
                        yield

                def score(p, step, heads):
                    g, buf, gb, half, tile = place(step)
                    if step % TOKT == 0 and heads[0] == 0:
                        e = step // TOKT
                        if e % (SETS // 2) == 0:
                            pe.wait_ge(cleared[buf], 1)
                        pe.wait_ge(max_loaded[e % 2], (p * (SETS // 2) + e // 2 + 1) * 16 * PLACES)
                    for hh in heads:
                        unit = step * GH + hh
                        pe.wait_ge(score_free, p * PAIR * GH + 1 + max(unit - SRING + 1, 0))
                        nc.tensor.matmul(psS[unit % SRING][:, :],
                                         ks[buf][0:ROWS, GH * gb + hh, tile * P:(tile + 1) * P],
                                         qs[buf][0:ROWS, half, GH * gb + hh, :],
                                         start=True, stop=True).then_inc(scored, 1)

                def add_values(p, step):
                    g, buf, gb, _, tile = place(step)
                    pe.wait_ge(score_free, p * PAIR * GH + (step + 1) * GH + 1)
                    if tile == 0:
                        pe.wait_ge(out_free, p * (PAIR // TOKT) + step // TOKT + 1)
                    for hh in range(GH):
                        last_mm = nc.tensor.matmul(psO[HP * hh:HP * hh + VW, :], vs[buf][:, tile, GH * gb + hh, :],
                                                   prob[step % PRING][:, hh, :], start=tile == 0, stop=tile == TOKT - 1)
                    last_mm.then_inc(prob_free, 1)

                def pair(p, last):
                    for step in range(PAIR):
                        ahead = step + LEAD
                        units = find_max(p, ahead) if not (last and ahead >= PAIR) else iter(())
                        score(p, step, (0, 1))
                        next(units, None)
                        score(p, step, (2, 3))
                        next(units, None)
                        if step:
                            add_values(p, step - 1)
                    add_values(p, PAIR - 1)

                pe.wait_ge(out_cleared, 1)
                for step in range(LEAD):
                    for _ in find_max(0, step):
                        pass
                with pe.Fori(0, PAIRS - 1) as p:
                    pair(p, False)
                pair(PAIRS - 1, True)

            @block.scalar
            def _(act):
                def pair(p):
                    for step in range(PAIR):
                        act.wait_ge(prob_free, p * PAIR + step + 1)
                        for hh in range(GH):
                            unit = step * GH + hh
                            act.wait_ge(scored, p * PAIR * GH + unit + 1)
                            nc.scalar.activation(prob[step % PRING][:, hh, :], psS[unit % SRING][:, :],
                                                 ACT.Exp).then_inc(score_free, 1)

                with act.Fori(0, PAIRS) as p:
                    pair(p)

            @block.vector
            def _(dve):
                def find_max(p, step):
                    e = step // TOKT
                    for m in range(M_STEP):
                        unit = step % TOKT * M_STEP + m
                        count = step * M_STEP + m
                        dve.wait_ge(max_scored, p * PAIR * M_STEP + count + 1)
                        nc.vector.tensor_reduce(neg_max[e % 2][:, unit:unit + 1], psM[count % MRING][:, :, :],
                                                AX.XY, ALU.max, negate=True).then_inc(max_free, 1)
                    if step % TOKT == TOKT - 1:
                        i, k = e % 2, (p * SETS + e) * SPLITS
                        dve.wait_ge(max_free, p * PAIR * M_STEP + (step + 1) * M_STEP + MRING)
                        nc.vector.tensor_copy(mpart[i][:, 0, :], neg_max[i][:, :]).then_inc(split, 1)
                        dve.wait_ge(split, k + 1)
                        nc.vector.tensor_tensor(mrest[i][:, :], neg_max[i][:, :], mpart[i][:, 0, :], ALU.subtract).then_inc(split, 1)
                        dve.wait_ge(split, k + 2)
                        nc.vector.tensor_copy(mpart[i][:, 1, :], mrest[i][:, :]).then_inc(split, 1)
                        dve.wait_ge(split, k + 3)
                        nc.vector.tensor_tensor(mpart[i][:, 2, :], mrest[i][:, :], mpart[i][:, 1, :], ALU.subtract).then_inc(split, 1)
                        dve.wait_ge(split, k + 4)
                        nc.vector.transpose(mpart_t[i][:, :, :].rearrange("p b r -> p (b r)"),
                                            mpart[i][:, :, :].rearrange("p n m -> p (n m)")).then_inc(max_t_done, 1)

                def copy_out(p, half):
                    dve.wait_ge(prob_free, p * PAIR + (half + 1) * TOKT + PRING)
                    dve.wait_ge(o_stored[half % 2], (p * (PAIR // TOKT // 2) + half // 2 + 1) * 16)
                    nc.vector.tensor_copy(ot[half % 2][:, :], psO[:, :]).then_inc(out_free, 1)

                def pair(p, last):
                    for step in range(PAIR):
                        ahead = step + LEAD
                        if not (last and ahead >= PAIR):
                            find_max(p, ahead)
                        if last and step == 2 * TOKT:
                            dve.wait_ge(sums_loaded, 16)
                            nc.vector.reciprocal(sums[:, :], sums[:, :]).then_inc(sums_inverted, 1)
                        if step and step % TOKT == 0:
                            copy_out(p, step // TOKT - 1)
                    copy_out(p, PAIR // TOKT - 1)

                for step in range(LEAD):
                    find_max(0, step)
                with dve.Fori(0, PAIRS - 1) as p:
                    pair(p, False)
                pair(PAIRS - 1, True)


def load_outputs(sp, r, w, o_cols, inv_l, inputs):
    heads = bass.ds((r * (WAYS // PER_BATCH) + w // PER_BATCH) * HEADS, HEADS)
    tokens = slice(w % PER_BATCH * CHUNK, (w % PER_BATCH + 1) * CHUNK)
    sp.dma_start(inputs["o_in"][w][:, :], by_head(o_cols)[heads, 0:HD, tokens]).then_inc(inputs["o_loaded"][w], 16)
    sp.dma_start(inputs["inv_in"][w][:, :], inv_l[heads, tokens].unsqueeze(1).to_broadcast([HEADS, HD, CHUNK])).then_inc(
        inputs["o_loaded"][w], 16)


def load_h(sp, r, w, h_rows, inputs):
    sp.dma_start(inputs["h_in"][w][:, :], h_rows[r, w]).then_inc(inputs["h_loaded"][w], 16)


def finish(nc, c, h_rows, o_cols, inv_l, inputs, out):
    ctx = ExitStack()
    with ctx:
        def ways(name, shape, dt=F32):
            return [ctx.enter_context(nc.sbuf_tensor(f"{name}{w}", shape, dt)) for w in range(WAYS)]

        def sem(name):
            return ctx.enter_context(nc.semaphore("c_" + name))

        def way_sems(name):
            return [sem(f"{name}{w}") for w in range(WAYS)]

        late_rows = 2 * HEADS
        piece = late_rows * SEQ // P
        sums = ctx.enter_context(nc.sbuf_tensor("late_sums", [P, piece], F32))
        o_in, inv_in, h_in = inputs["o_in"], inputs["inv_in"], inputs["h_in"]
        half_o = ways("half_o", [P, CHUNK])
        so = ways("so", [P, CHUNK])
        h2 = ways("h2_", [P, TILES, DIM])
        h2_kept = ways("h2_kept", [P, TILES, DIM])
        stat = ways("c_stat", [P, TILES, 6])
        mv = ways("c_mv", [P, TILES, 2])
        var_eps = ways("c_var_eps", [P, TILES])
        rstd = ways("c_rstd", [P, TILES])
        y = ways("y", [P, TILES, DIM])
        y_t = ways("y_t", [P, CHUNK])
        neg_max = ways("c_neg_max", [P, TILES])
        logit = ways("c_logit", [P, TILES, EXPERTS])
        prob = ways("c_prob", [P, TILES, EXPERTS])
        inv_sum = ways("c_inv_sum", [P, TILES])
        top = ways("top", [P, TILES, 8])
        top_i = ways("top_i", [P, TILES, 8], U32)
        top_f = ways("top_f", [P, TILES, 2])
        first = ways("first", [P, TILES, EXPERTS])
        second = ways("second", [P, TILES, EXPERTS])
        chosen = ways("chosen", [P, TILES, EXPERTS], BF16)
        before = ways("before", [P, TILES, EXPERTS])
        gate = ways("gate", [P, TILES])
        hid = ways("hid", [P, FK, CHUNK])
        res = ways("res", [P, TILES, DIM])
        psT = [ctx.enter_context(nc.psum_tensor(f"c_psT{i}", [P, 2, BANK], F32)) for i in range(SLOTS)] * (WAYS // SLOTS)
        psR = [ctx.enter_context(nc.psum_tensor(f"c_psR{i}", [P, 2, TILES * EXPERTS], F32)) for i in range(SLOTS)] * (WAYS // SLOTS)
        psF = [ctx.enter_context(nc.psum_tensor(f"c_psF{i}", [P, BANK], F32)) for i in range(SLOTS)] * (WAYS // SLOTS)

        o_loaded, h_loaded = inputs["o_loaded"], inputs["h_loaded"]
        sums_loaded = sem("sums_loaded")
        sums_inverted = sem("sums_inverted")
        inv_stored = sem("inv_stored")
        o_done = sem("o_done")
        tanh_done = sem("tanh_done")
        silu_done = sem("silu_done")
        projected = sem("projected")
        h2_done = sem("h2_done")
        h2_copied = sem("h2_copied")
        stats_done = sem("stats_done")
        aggr_done = sem("aggr_done")
        eps_done = sem("eps_done")
        rstd_done = sem("rstd_done")
        y_done = sem("y_done")
        y_t_done = sem("y_t_done")
        y_t_copied = sem("y_t_copied")
        routed = sem("routed")
        max_found = sem("max_found")
        logit_shifted = sem("logit_shifted")
        exp_done = sem("exp_done")
        sum_done = sem("sum_done")
        inv_sum_done = sem("inv_sum_done")
        prob_done = sem("prob_done")
        top_done = sem("top_done")
        index_done = sem("index_done")
        index_cast = sem("index_cast")
        hot_done = sem("hot_done")
        chosen_done = sem("chosen_done")
        counted = sem("counted")
        before_done = sem("before_done")
        carried = sem("carried")
        kept_done = sem("kept_done")
        kept_prob_done = sem("kept_prob_done")
        gate_done = sem("gate_done")
        up_done = sem("up_done")
        gelu_done = sem("gelu_done")
        down_done = sem("down_done")
        res_done = sem("res_done")
        res_stored = way_sems("res_stored")
        RES_PRESET = 2 * WAYS

        with nc.Block() as block:
            @block.sync
            def _(sp):
                preset(sp, o_done, WAYS)
                preset(sp, h2_done, WAYS)
                preset(sp, h2_copied, WAYS)
                preset(sp, res_done, RES_PRESET)
                preset(sp, carried, 1)
                for w in range(WAYS):
                    preset(sp, res_stored[w], 16)

        def count_chosen(pe, it, w):
            pe.wait_ge(chosen_done, it * WAYS + w + 1)
            if w >= SLOTS:
                pe.wait_ge(carried, it * WAYS + w + 2 - SLOTS)
            for t in range(TILES):
                dst = psR[w][:, 1, t * EXPERTS:(t + 1) * EXPERTS]
                for u in range(t):
                    nc.tensor.matmul(dst, c["ones"][:, :], chosen[w][:, u, :], start=u == 0, stop=False)
                nc.tensor.matmul(dst, c["later"][:, :], chosen[w][:, t, :], start=t == 0, stop=True)
            for u in range(TILES):
                last = nc.tensor.matmul(psR[w][:, 0, 0:EXPERTS], c["ones"][:, :], chosen[w][:, u, :],
                                        start=u == 0, stop=u == TILES - 1)
            last.then_inc(counted, 1)

        with nc.Block() as block:
            @block.sync
            def _(sp):
                sp.dma_start(sums[:, :], in_pieces(by_head(o_cols)[BATCH * HEADS - late_rows:, HD, :], piece)).then_inc(sums_loaded, 16)
                sp.wait_ge(sums_inverted, 1)
                sp.dma_start(in_pieces(inv_l[BATCH * HEADS - late_rows:, :], piece), sums[:, :]).then_inc(inv_stored, 16)
                sp.wait_ge(inv_stored, 16)
                with sp.Fori(0, ITERS - 1) as it:
                    for w in range(WAYS):
                        sp.wait_ge(o_done, it * WAYS + w + 1 + WAYS)
                        load_outputs(sp, it + 1, w, o_cols, inv_l, inputs)
                        sp.wait_ge(h2_done, it * WAYS + w + 1 + WAYS)
                        load_h(sp, it + 1, w, h_rows, inputs)

            @block.gpsimd
            def _(pool):
                def root(r):
                    for w in range(WAYS):
                        pool.wait_ge(eps_done, r * WAYS + w + 1)
                        nc.gpsimd.tensor_tensor(rstd[w][:, :], var_eps[w][:, :], c["neg_half"][:, 0:TILES], ALU.pow).then_inc(rstd_done, 1)

                def keep_h2(r):
                    for w in range(WAYS):
                        pool.wait_ge(res_done, (r - 1) * WAYS + w + 1 + RES_PRESET)
                        wait_apart(pool, h2_done, r * WAYS + w + 1 + WAYS)
                        nc.gpsimd.tensor_copy(h2_kept[w][:, :, :], h2[w][:, :, :]).then_inc(h2_copied, 1)

                root(0)
                keep_h2(0)
                with pool.Fori(0, ITERS - 1) as it:
                    root(it + 1)
                    keep_h2(it + 1)

            @block.scalar
            def _(act):
                def tanh(r):
                    for w in range(WAYS):
                        act.wait_ge(o_done, r * WAYS + w + 1 + WAYS)
                        nc.scalar.activation(so[w][:, :], half_o[w][:, :], ACT.Tanh).then_inc(tanh_done, 1)

                def copy_y_t(r):
                    for w in range(WAYS):
                        act.wait_ge(y_t_done, r * WAYS + w + 1)
                        nc.scalar.activation(y_t[w][:, :], psT[w][:, 0, :], ACT.Copy).then_inc(y_t_copied, 1)

                def exponentials(r):
                    for w in range(WAYS):
                        act.wait_ge(logit_shifted, r * WAYS + w + 1)
                        nc.scalar.activation(prob[w][:, :, :], logit[w][:, :, :], ACT.Exp).then_inc(exp_done, 1)

                def gelu(r):
                    for w in range(WAYS):
                        for k in range(FK):
                            act.wait_ge(up_done, (r * WAYS + w) * FK + k + 1)
                            src = psF[w][:, :] if k % 2 == 0 else psT[w][:, 0, :]
                            nc.scalar.activation(hid[w][:, k, :], src, ACT.Gelu, bias=c["b1"][:, k:k + 1]).then_inc(gelu_done, 1)

                def store(r):
                    for w in range(WAYS):
                        act.wait_ge(res_done, r * WAYS + w + 1 + RES_PRESET)
                        at = w % PER_BATCH
                        act.dma_start(out[r * (WAYS // PER_BATCH) + w // PER_BATCH, :, at * TILES:(at + 1) * TILES, :],
                                      res[w][:, :, :]).then_inc(res_stored[w], 16)

                tanh(0)
                copy_y_t(0)
                exponentials(0)
                gelu(0)
                with act.Fori(0, ITERS - 1) as it:
                    tanh(it + 1)
                    copy_y_t(it + 1)
                    exponentials(it + 1)
                    store(it)
                    gelu(it + 1)
                store(ITERS - 1)
                for w in range(WAYS):
                    act.wait_ge(res_stored[w], (ITERS + 1) * 16)

            @block.tensor
            def _(pe):
                def project(r, alone=False):
                    for w in range(WAYS):
                        if w >= SLOTS:
                            pe.wait_ge(h2_done, r * WAYS + w + 1 + WAYS - SLOTS)
                        elif not alone:
                            pe.wait_ge(gelu_done, ((r - 1) * WAYS + w + 1 + SLOTS) * FK)
                        add_bias(nc, c, psF[w][:, :], 3 * DIM, DIM)
                        pe.wait_ge(silu_done, r * WAYS + w + 1)
                        for t in range(TILES):
                            last = nc.tensor.matmul(psF[w][:, t * DIM:(t + 1) * DIM], so[w][:, t * P:(t + 1) * P],
                                                    c["w_o"][:, :], start=False, stop=t == TILES - 1)
                        last.then_inc(projected, 1)

                def transpose_y(r, alone=False):
                    for w in range(WAYS):
                        if w >= SLOTS:
                            pe.wait_ge(y_t_copied, r * WAYS + w + 1 - SLOTS)
                        elif not alone:
                            pe.wait_ge(gelu_done, ((r - 1) * WAYS + w + 1 + SLOTS) * FK)
                        pe.wait_ge(y_done, r * WAYS + w + 1)
                        for t in range(TILES):
                            last = nc.tensor.transpose(psT[w][:, 0, t * P:(t + 1) * P], y[w][:, t, :], c["ident"][:, :])
                        last.then_inc(y_t_done, 1)

                def route(r):
                    for w in range(WAYS):
                        pe.wait_ge(y_t_copied, r * WAYS + w + 1)
                        if w >= SLOTS:
                            pe.wait_ge(logit_shifted, r * WAYS + w + 1 - SLOTS)
                        for t in range(TILES):
                            last = nc.tensor.matmul(psR[w][:, 0, t * EXPERTS:(t + 1) * EXPERTS], y_t[w][:, t * P:(t + 1) * P],
                                                    c["router"][:, :], start=True, stop=True)
                        last.then_inc(routed, 1)

                def up(r):
                    for w in range(WAYS):
                        for k in range(FK):
                            if k >= 2:
                                pe.wait_ge(gelu_done, (r * WAYS + w) * FK + k - 1)
                            elif w >= SLOTS:
                                pe.wait_ge(gelu_done, (r * WAYS + w - SLOTS) * FK + k + 3)
                            dst = psF[w][:, :] if k % 2 == 0 else psT[w][:, 0, :]
                            nc.tensor.matmul(dst, c["w1"][:, k * P:(k + 1) * P], y_t[w][:, :], start=True, stop=True).then_inc(up_done, 1)

                def down(r, ways_now):
                    for w in ways_now:
                        pe.wait_ge(res_done, r * WAYS + w + 1 - SLOTS + RES_PRESET)
                        add_bias(nc, c, psT[w][:, 1, :], 4 * DIM, DIM)
                        pe.wait_ge(gelu_done, (r * WAYS + w + 1) * FK)
                        for t in range(TILES):
                            for k in range(FK):
                                last = nc.tensor.matmul(psT[w][:, 1, t * DIM:(t + 1) * DIM], hid[w][:, k, t * P:(t + 1) * P],
                                                        c["w2"][:, k, :], start=False,
                                                        stop=t == TILES - 1 and k == FK - 1)
                        last.then_inc(down_done, 1)

                def count(r, ways_now):
                    for w in ways_now:
                        count_chosen(pe, r, w)

                project(0, alone=True)
                transpose_y(0, alone=True)
                route(0)
                up(0)
                with pe.Fori(0, ITERS - 1) as it:
                    count(it, range(SLOTS))
                    down(it, (0,))
                    project(it + 1)
                    count(it, range(SLOTS, WAYS))
                    down(it, (1, 2, 3))
                    transpose_y(it + 1)
                    route(it + 1)
                    up(it + 1)
                count(ITERS - 1, range(SLOTS))
                down(ITERS - 1, (0,))
                count(ITERS - 1, range(SLOTS, WAYS))
                down(ITERS - 1, (1, 2, 3))

            @block.vector
            def _(dve):
                def divide(r):
                    for w in range(WAYS):
                        dve.wait_ge(o_loaded[w], (r + 1) * 32)
                        nc.vector.scalar_tensor_tensor(out=half_o[w][:, :], in0=o_in[w][:, :], scalar=0.5, in1=inv_in[w][:, :],
                                                       op0=ALU.mult, op1=ALU.mult).then_inc(o_done, 1)

                def silu(r):
                    for w in range(WAYS):
                        dve.wait_ge(tanh_done, r * WAYS + w + 1)
                        nc.vector.scalar_tensor_tensor(out=so[w][:, :], in0=so[w][:, :], scalar=1.0, in1=half_o[w][:, :],
                                                       op0=ALU.add, op1=ALU.mult).then_inc(silu_done, 1)

                def residual(r):
                    for w in range(WAYS):
                        n = r * WAYS + w + 1
                        dve.wait_ge(projected, n)
                        dve.wait_ge(h_loaded[w], (r + 1) * 16)
                        dve.wait_ge(h2_copied, n)
                        nc.vector.tensor_tensor(h2[w][:, :, :], psF[w][:, :].rearrange("p (t n) -> p t n", t=TILES),
                                                h_in[w][:, :].rearrange("p (t n) -> p t n", t=TILES), ALU.add).then_inc(h2_done, 1)

                def statistics(r):
                    for w in range(WAYS):
                        dve.wait_ge(h2_done, r * WAYS + w + 1 + WAYS)
                        for t in range(TILES):
                            last = nc.vector.bn_stats(stat[w][:, t, :], h2[w][:, t, :])
                        last.then_inc(stats_done, 1)
                    for w in range(WAYS):
                        n = r * WAYS + w + 1
                        wait_apart(dve, stats_done, n)
                        for t in range(TILES):
                            last = nc.vector.bn_aggr(mv[w][:, t, :], stat[w][:, t, :])
                        last.then_inc(aggr_done, 1)
                        dve.wait_ge(aggr_done, n)
                        nc.vector.tensor_scalar(var_eps[w][:, :], mv[w][:, :, 1], EPS, None, ALU.add).then_inc(eps_done, 1)

                def norm(r):
                    for w in range(WAYS):
                        dve.wait_ge(rstd_done, r * WAYS + w + 1)
                        for t in range(TILES):
                            last = nc.vector.tensor_scalar(y[w][:, t, :], h2[w][:, t, :], mv[w][:, t, 0:1],
                                                           rstd[w][:, t:t + 1], ALU.subtract, ALU.mult)
                        last.then_inc(y_done, 1)

                def softmax(r):
                    for w in range(WAYS):
                        n = r * WAYS + w + 1
                        scores = psR[w][:, 0, :].rearrange("p (t e) -> p t e", t=TILES)
                        dve.wait_ge(routed, n)
                        nc.vector.tensor_reduce(neg_max[w][:, :], scores, AX.X, ALU.max, negate=True).then_inc(max_found, 1)
                        dve.wait_ge(max_found, n)
                        nc.vector.tensor_tensor(logit[w][:, :, :], scores,
                                                neg_max[w][:, :].unsqueeze(2).to_broadcast([P, TILES, EXPERTS]),
                                                ALU.add).then_inc(logit_shifted, 1)
                    for w in range(WAYS):
                        n = r * WAYS + w + 1
                        dve.wait_ge(exp_done, n)
                        nc.vector.tensor_reduce(inv_sum[w][:, :], prob[w][:, :, :], AX.X, ALU.add).then_inc(sum_done, 1)
                        dve.wait_ge(sum_done, n)
                        nc.vector.reciprocal(inv_sum[w][:, :], inv_sum[w][:, :]).then_inc(inv_sum_done, 1)
                        dve.wait_ge(inv_sum_done, n)
                        nc.vector.tensor_tensor(prob[w][:, :, :], prob[w][:, :, :],
                                                inv_sum[w][:, :].unsqueeze(2).to_broadcast([P, TILES, EXPERTS]),
                                                ALU.mult).then_inc(prob_done, 1)

                def choose(r):
                    for w in range(WAYS):
                        n = r * WAYS + w + 1
                        wait_apart(dve, prob_done, n)
                        for t in range(TILES):
                            last = nc.vector.max(top[w][:, t, :], prob[w][:, t, :])
                        last.then_inc(top_done, 1)
                    for w in range(WAYS):
                        n = r * WAYS + w + 1
                        wait_apart(dve, top_done, n)
                        for t in range(TILES):
                            last = nc.vector.max_index(top_i[w][:, t, :], top[w][:, t, :], prob[w][:, t, :])
                        last.then_inc(index_done, 1)
                    for w in range(WAYS):
                        n = r * WAYS + w + 1
                        dve.wait_ge(index_done, n)
                        nc.vector.tensor_copy(top_f[w][:, :, :], top_i[w][:, :, 0:2]).then_inc(index_cast, 1)
                    for w in range(WAYS):
                        n = r * WAYS + w + 1
                        dve.wait_ge(index_cast, n)
                        ids = c["expert_ids"][:, :].unsqueeze(1).to_broadcast([P, TILES, EXPERTS])
                        for j, hot in enumerate((first, second)):
                            last = nc.vector.tensor_tensor(hot[w][:, :, :], ids,
                                                           top_f[w][:, :, j:j + 1].to_broadcast([P, TILES, EXPERTS]),
                                                           ALU.is_equal)
                        last.then_inc(hot_done, 1)
                    for w in range(WAYS):
                        dve.wait_ge(hot_done, r * WAYS + w + 1)
                        nc.vector.tensor_tensor(chosen[w][:, :, :], first[w][:, :, :], second[w][:, :, :],
                                                ALU.add).then_inc(chosen_done, 1)

                def weigh(r, ways_now):
                    for w in ways_now:
                        n = r * WAYS + w + 1
                        dve.wait_ge(counted, n)
                        dve.wait_ge(carried, n)
                        nc.vector.tensor_tensor(before[w][:, :, :],
                                                psR[w][:, 1, :].rearrange("p (t e) -> p t e", t=TILES),
                                                c["carry"][:, :].unsqueeze(1).to_broadcast([P, TILES, EXPERTS]),
                                                ALU.add).then_inc(before_done, 1)
                        dve.wait_ge(before_done, n)
                        nc.vector.tensor_tensor(c["carry"][:, :], psR[w][:, 0, 0:EXPERTS], c["carry"][:, :],
                                                ALU.add).then_inc(carried, 1)
                        nc.vector.scalar_tensor_tensor(out=before[w][:, :, :], in0=before[w][:, :, :], scalar=float(CAP),
                                                       in1=chosen[w][:, :, :], op0=ALU.is_lt, op1=ALU.mult).then_inc(kept_done, 1)
                        dve.wait_ge(kept_done, n)
                        nc.vector.tensor_tensor(before[w][:, :, :], before[w][:, :, :], prob[w][:, :, :],
                                                ALU.mult).then_inc(kept_prob_done, 1)
                        dve.wait_ge(kept_prob_done, n)
                        nc.vector.tensor_reduce(gate[w][:, :], before[w][:, :, :], AX.X, ALU.add).then_inc(gate_done, 1)

                def result(r, ways_now):
                    for w in ways_now:
                        n = r * WAYS + w + 1
                        dve.wait_ge(gate_done, n)
                        dve.wait_ge(down_done, n)
                        dve.wait_ge(h2_copied, n + WAYS)
                        dve.wait_ge(res_stored[w], (r + 1) * 16)
                        for t in range(TILES):
                            last = nc.vector.scalar_tensor_tensor(out=res[w][:, t, :], in0=psT[w][:, 1, t * DIM:(t + 1) * DIM],
                                                                  scalar=gate[w][:, t:t + 1], in1=h2_kept[w][:, t, :],
                                                                  op0=ALU.mult, op1=ALU.add)
                        last.then_inc(res_done, 1)

                divide(0)
                dve.wait_ge(sums_loaded, 16)
                nc.vector.reciprocal(sums[:, :], sums[:, :]).then_inc(sums_inverted, 1)
                silu(0)
                residual(0)
                statistics(0)
                norm(0)
                softmax(0)
                choose(0)
                with dve.Fori(0, ITERS - 1) as it:
                    divide(it + 1)
                    silu(it + 1)
                    weigh(it, range(SLOTS))
                    residual(it + 1)
                    result(it, (0,))
                    weigh(it, range(SLOTS, WAYS))
                    result(it, (1,))
                    statistics(it + 1)
                    norm(it + 1)
                    result(it, (2, 3))
                    softmax(it + 1)
                    choose(it + 1)
                weigh(ITERS - 1, range(SLOTS))
                result(ITERS - 1, (0,))
                weigh(ITERS - 1, range(SLOTS, WAYS))
                result(ITERS - 1, (1, 2, 3))


def kernel(**inputs):
    import numpy as _np
    import concourse.bacc as _bacc
    from concourse.bass_utils import run_bass_kernel_spmd as _run

    a = {k: _np.asarray(v) for k, v in inputs.items()}
    t, at, f = "L0_tok_", "L0_attn_", "L0_ffn_"
    chunks = BATCH * SEQ // CHUNK
    arrays = {
        "x_idx": a["x"].reshape(chunks, TILES, P).transpose(0, 2, 1),
        "table": _np.concatenate([a[t + "fine_embed_w"], a[t + "loc_to_cluster_w"].T], axis=1),
        "cluster_b": a[t + "loc_to_cluster_b"], "coarse_w": a[t + "coarse_embed_w"],
        "w_q": a[at + "w_q"], "b_q": a[at + "b_q"], "w_k": a[at + "w_k"], "b_k": a[at + "b_k"],
        "w_v": a[at + "w_v"], "b_v": a[at + "b_v"], "g_q": a[at + "g_q"], "be_q": a[at + "be_q"],
        "g_k": a[at + "g_k"], "be_k": a[at + "be_k"], "w_o": a[at + "w_o"], "b_o": a[at + "b_o"],
        "router_t": a[f + "router_w"].T, "w1_t": a[f + "w1"].T, "b1_c": a[f + "b1"].reshape(FK, P).T,
        "w2_t": a[f + "w2"].T, "b2": a[f + "b2"],
    }
    arrays = {k: _np.ascontiguousarray(v) for k, v in arrays.items()}
    nc = _bacc.Bacc("TRN2", target_bir_lowering=False, num_devices=1)
    args = {k: nc.dram_tensor("in_" + k, v.shape, mybir.dt.from_np(v.dtype), kind="ExternalInput").ap()
            for k, v in arrays.items()}
    out = nc.dram_tensor("out", (BATCH, SEQ, DIM), F32, kind="ExternalOutput").ap()
    build(nc, out=out.rearrange("b (t p) n -> b p t n", p=P), **args)
    r = _run(nc, [{"in_" + k: v for k, v in arrays.items()}], core_ids=[0])
    return r.results[0]["out"]
```
